# Optimizing a Trainium2 kernel written in Bass

```python
import numpy as np
import jax
import jax.numpy as jnp

def _softmax(x, axis=-1):
    return jax.nn.softmax(x, axis=axis)

def _gelu(x):
    return jax.nn.gelu(x, approximate=True)

def _silu(x):
    return jax.nn.silu(x)

def _sigmoid(x):
    return jax.nn.sigmoid(x)

def _layernorm(x, axis=-1, eps=1e-05):
    m = jnp.mean(x, axis=axis, keepdims=True)
    v = jnp.var(x, axis=axis, keepdims=True)
    return (x - m) / jnp.sqrt(v + eps)

def _scatter_add(tgt, idx, src, axis=0):
    return tgt.at[idx].add(src)

def _segment_sum(src, seg, n):
    return jax.ops.segment_sum(src, seg, n)
kernel_name = 'mk_gnn_resnorm_d4_gnn_r8_8fa63c'

def setup_inputs(seed: int=0):
    np.random.seed(seed)
    _w = jnp.asarray

    def _rec_inputs():
        import jax
        import jax.numpy as jnp
        _gk = jax.random.key(seed)
        x = -0.000202 + 1 * jax.random.normal(jax.random.fold_in(_gk, 1), (6250, 128), jnp.float32)
        _s = jax.random.randint(jax.random.fold_in(_gk, 2), (50000,), 0, 6250, jnp.int32)
        _d = jax.random.randint(jax.random.fold_in(_gk, 3), (50000,), 0, 6250, jnp.int32)
        _loop = jnp.arange(6250, dtype=jnp.int32)
        src = jnp.concatenate([_s, _d, _loop])
        dst = jnp.concatenate([_d, _s, _loop])
        _o = jnp.argsort(dst, stable=True)
        src = src[_o]
        dst = dst[_o]
        edge_attr_128 = -4.21973e-05 + 0.999841 * jax.random.normal(jax.random.fold_in(_gk, 11), (106250, 128), jnp.float32)
        edge_attr_16 = -1.02531e-05 + 0.999808 * jax.random.normal(jax.random.fold_in(_gk, 12), (106250, 16), jnp.float32)
        edge_attr_64 = 7.68618e-05 + 1.00005 * jax.random.normal(jax.random.fold_in(_gk, 13), (106250, 64), jnp.float32)
        return (x, src, dst, edge_attr_128, edge_attr_16, edge_attr_64)
    x, src, dst, edge_attr_128, edge_attr_16, edge_attr_64 = _rec_inputs()

    def _L0_gnn_setup():
        import jax, jax.numpy as jnp
        import numpy as np
        N, E, D, L = (6250, 75000, 128, 4)
        BN_EPS = 1e-05
        LN_EPS = 1e-05

        def _bn(h, g, b):
            m = h.mean(axis=0)
            v = h.var(axis=0)
            return (h - m) * jax.lax.rsqrt(v + BN_EPS) * g + b

        def _ln(h, g, b):
            m = h.mean(axis=-1, keepdims=True)
            v = h.var(axis=-1, keepdims=True)
            return (h - m) * jax.lax.rsqrt(v + LN_EPS) * g + b
        key = jax.random.key(seed)
        ks = jax.random.split(key, 8)
        s = 0.08
        return {'x': jax.random.normal(ks[0], (N, D), dtype=jnp.float32), 'edge_index': jax.random.randint(ks[1], (2, E), 0, N, dtype=jnp.int64), 'eps': jnp.zeros((L,), jnp.float32), 'W1': jax.random.normal(ks[2], (L, D, D), dtype=jnp.float32) * s, 'b1': jnp.zeros((L, D), jnp.float32), 'bn1_g': jnp.ones((L, D), jnp.float32), 'bn1_b': jnp.zeros((L, D), jnp.float32), 'W2': jax.random.normal(ks[3], (L, D, D), dtype=jnp.float32) * s, 'b2': jnp.zeros((L, D), jnp.float32), 'bn2_g': jnp.ones((L, D), jnp.float32), 'bn2_b': jnp.zeros((L, D), jnp.float32), 'obn_g': jnp.ones((L, D), jnp.float32), 'obn_b': jnp.zeros((L, D), jnp.float32), 'ln_g': jnp.ones((D,), jnp.float32), 'ln_b': jnp.zeros((D,), jnp.float32), 'fp_W1': jax.random.normal(ks[4], (D, 2 * D), dtype=jnp.float32) * s, 'fp_b1': jnp.zeros((2 * D,), jnp.float32), 'fp_ln1_g': jnp.ones((2 * D,), jnp.float32), 'fp_ln1_b': jnp.zeros((2 * D,), jnp.float32), 'fp_W2': jax.random.normal(ks[5], (2 * D, D), dtype=jnp.float32) * s, 'fp_b2': jnp.zeros((D,), jnp.float32), 'fp_ln2_g': jnp.ones((D,), jnp.float32), 'fp_ln2_b': jnp.zeros((D,), jnp.float32)}
    _L0_gnn_all = _L0_gnn_setup()
    _L0_gnn_in = {k: v for k, v in _L0_gnn_all.items() if k in ('eps', 'W1', 'b1', 'bn1_g', 'bn1_b', 'W2', 'b2', 'bn2_g', 'bn2_b', 'obn_g', 'obn_b', 'ln_g', 'ln_b', 'fp_W1', 'fp_b1', 'fp_ln1_g', 'fp_ln1_b', 'fp_W2', 'fp_b2', 'fp_ln2_g', 'fp_ln2_b')}
    del _L0_gnn_all

    def _L1_gnn_setup():
        import jax, jax.numpy as jnp
        import numpy as np
        N_NODES = 12500
        N_EDGES = 125000
        IN_CH = 128
        OUT_CH = 128
        T_DIM = 64
        key = jax.random.key(seed)
        ks = jax.random.split(key, 9)
        x = jax.random.normal(ks[0], (N_NODES, IN_CH), dtype=jnp.float32)
        edge_index = jax.random.randint(ks[1], (2, N_EDGES), 0, N_NODES, dtype=jnp.int64)
        temporal_features = jax.random.normal(ks[2], (N_EDGES, T_DIM), dtype=jnp.float32)
        s = 1.0 / np.sqrt(IN_CH)
        st = 1.0 / np.sqrt(T_DIM)
        W_S_w = jax.random.uniform(ks[3], (OUT_CH, IN_CH), minval=-s, maxval=s, dtype=jnp.float32)
        W_S_b = jax.random.uniform(ks[4], (OUT_CH,), minval=-s, maxval=s, dtype=jnp.float32)
        W_T_w = jax.random.uniform(ks[5], (OUT_CH, IN_CH), minval=-s, maxval=s, dtype=jnp.float32)
        W_T_b = jax.random.uniform(ks[6], (OUT_CH,), minval=-s, maxval=s, dtype=jnp.float32)
        T_w = jax.random.uniform(ks[7], (OUT_CH, T_DIM), minval=-st, maxval=st, dtype=jnp.float32)
        T_b = jax.random.uniform(ks[8], (OUT_CH,), minval=-st, maxval=st, dtype=jnp.float32)
        return {'x': x, 'edge_index': edge_index, 'temporal_features': temporal_features, 'W_S_w': W_S_w, 'W_S_b': W_S_b, 'W_T_w': W_T_w, 'W_T_b': W_T_b, 'T_w': T_w, 'T_b': T_b}
    _L1_gnn_all = _L1_gnn_setup()
    _L1_gnn_in = {k: v for k, v in _L1_gnn_all.items() if k in ('W_S_w', 'W_S_b', 'W_T_w', 'W_T_b', 'T_w', 'T_b')}
    del _L1_gnn_all

    def _L2_gnn_setup():
        import jax, jax.numpy as jnp
        import numpy as np
        N, E, C, EC, L = (6250, 75000, 128, 16, 4)
        LN_EPS = 1e-05
        key = jax.random.key(seed)
        ks = jax.random.split(key, 10)
        return {'x': jax.random.normal(ks[0], (N, C), jnp.float32), 'edge_attr': jax.random.normal(ks[1], (E, EC), jnp.float32), 'We': jax.random.normal(ks[2], (EC, C), jnp.float32) / np.sqrt(EC).astype(np.float32), 'be': jnp.zeros((C,), jnp.float32), 'W1': jax.random.normal(ks[3], (L, C, C), jnp.float32) / np.sqrt(C).astype(np.float32), 'b1': jnp.zeros((L, C), jnp.float32), 'W2': jax.random.normal(ks[4], (L, C, C), jnp.float32) / np.sqrt(C).astype(np.float32), 'b2': jnp.zeros((L, C), jnp.float32), 'gamma': jnp.ones((L, C), jnp.float32), 'beta': jnp.zeros((L, C), jnp.float32), 'edge_index': jax.random.randint(ks[5], (2, E), 0, N, dtype=jnp.int32)}
    _L2_gnn_all = _L2_gnn_setup()
    _L2_gnn_in = {k: v for k, v in _L2_gnn_all.items() if k in ('We', 'be', 'W1', 'b1', 'W2', 'b2', 'gamma', 'beta')}
    del _L2_gnn_all

    def _L3_gnn_setup():
        import jax, jax.numpy as jnp
        import numpy as np
        NUM_HEADS = 8
        BN_EPS = 1e-05
        ATTN_EPS = 1e-06
        key = jax.random.key(seed)
        N, E, D = (6250, 75000, 128)
        ks = jax.random.split(key, 7)
        s = 1.0 / np.sqrt(D).astype(np.float32)
        return {'x': jax.random.normal(ks[0], (N, D), jnp.float32), 'edge_attr': jax.random.normal(ks[1], (E, D), jnp.float32), 'WQ': jax.random.normal(ks[2], (D, D), jnp.float32) * s, 'WK': jax.random.normal(ks[3], (D, D), jnp.float32) * s, 'WV': jax.random.normal(ks[4], (D, D), jnp.float32) * s, 'WE': jax.random.normal(ks[5], (D, D), jnp.float32) * s, 'bn_gamma': jnp.ones((D,), jnp.float32), 'bn_beta': jnp.zeros((D,), jnp.float32), 'edge_index': jax.random.randint(ks[6], (2, E), 0, N, dtype=jnp.int32)}
    _L3_gnn_all = _L3_gnn_setup()
    _L3_gnn_in = {k: v for k, v in _L3_gnn_all.items() if k in ('WQ', 'WK', 'WV', 'WE', 'bn_gamma', 'bn_beta')}
    del _L3_gnn_all
    return {'x': x, 'src': src, 'dst': dst, 'edge_attr_128': edge_attr_128, 'edge_attr_16': edge_attr_16, 'edge_attr_64': edge_attr_64, 'L0_gnn_eps': _L0_gnn_in['eps'], 'L0_gnn_W1': _L0_gnn_in['W1'], 'L0_gnn_b1': _L0_gnn_in['b1'], 'L0_gnn_bn1_g': _L0_gnn_in['bn1_g'], 'L0_gnn_bn1_b': _L0_gnn_in['bn1_b'], 'L0_gnn_W2': _L0_gnn_in['W2'], 'L0_gnn_b2': _L0_gnn_in['b2'], 'L0_gnn_bn2_g': _L0_gnn_in['bn2_g'], 'L0_gnn_bn2_b': _L0_gnn_in['bn2_b'], 'L0_gnn_obn_g': _L0_gnn_in['obn_g'], 'L0_gnn_obn_b': _L0_gnn_in['obn_b'], 'L0_gnn_ln_g': _L0_gnn_in['ln_g'], 'L0_gnn_ln_b': _L0_gnn_in['ln_b'], 'L0_gnn_fp_W1': _L0_gnn_in['fp_W1'], 'L0_gnn_fp_b1': _L0_gnn_in['fp_b1'], 'L0_gnn_fp_ln1_g': _L0_gnn_in['fp_ln1_g'], 'L0_gnn_fp_ln1_b': _L0_gnn_in['fp_ln1_b'], 'L0_gnn_fp_W2': _L0_gnn_in['fp_W2'], 'L0_gnn_fp_b2': _L0_gnn_in['fp_b2'], 'L0_gnn_fp_ln2_g': _L0_gnn_in['fp_ln2_g'], 'L0_gnn_fp_ln2_b': _L0_gnn_in['fp_ln2_b'], 'L1_gnn_W_S_w': _L1_gnn_in['W_S_w'], 'L1_gnn_W_S_b': _L1_gnn_in['W_S_b'], 'L1_gnn_W_T_w': _L1_gnn_in['W_T_w'], 'L1_gnn_W_T_b': _L1_gnn_in['W_T_b'], 'L1_gnn_T_w': _L1_gnn_in['T_w'], 'L1_gnn_T_b': _L1_gnn_in['T_b'], 'L2_gnn_We': _L2_gnn_in['We'], 'L2_gnn_be': _L2_gnn_in['be'], 'L2_gnn_W1': _L2_gnn_in['W1'], 'L2_gnn_b1': _L2_gnn_in['b1'], 'L2_gnn_W2': _L2_gnn_in['W2'], 'L2_gnn_b2': _L2_gnn_in['b2'], 'L2_gnn_gamma': _L2_gnn_in['gamma'], 'L2_gnn_beta': _L2_gnn_in['beta'], 'L3_gnn_WQ': _L3_gnn_in['WQ'], 'L3_gnn_WK': _L3_gnn_in['WK'], 'L3_gnn_WV': _L3_gnn_in['WV'], 'L3_gnn_WE': _L3_gnn_in['WE'], 'L3_gnn_bn_gamma': _L3_gnn_in['bn_gamma'], 'L3_gnn_bn_beta': _L3_gnn_in['bn_beta']}

def reference(x, src, dst, edge_attr_128, edge_attr_16, edge_attr_64, L0_gnn_eps, L0_gnn_W1, L0_gnn_b1, L0_gnn_bn1_g, L0_gnn_bn1_b, L0_gnn_W2, L0_gnn_b2, L0_gnn_bn2_g, L0_gnn_bn2_b, L0_gnn_obn_g, L0_gnn_obn_b, L0_gnn_ln_g, L0_gnn_ln_b, L0_gnn_fp_W1, L0_gnn_fp_b1, L0_gnn_fp_ln1_g, L0_gnn_fp_ln1_b, L0_gnn_fp_W2, L0_gnn_fp_b2, L0_gnn_fp_ln2_g, L0_gnn_fp_ln2_b, L1_gnn_W_S_w, L1_gnn_W_S_b, L1_gnn_W_T_w, L1_gnn_W_T_b, L1_gnn_T_w, L1_gnn_T_b, L2_gnn_We, L2_gnn_be, L2_gnn_W1, L2_gnn_b1, L2_gnn_W2, L2_gnn_b2, L2_gnn_gamma, L2_gnn_beta, L3_gnn_WQ, L3_gnn_WK, L3_gnn_WV, L3_gnn_WE, L3_gnn_bn_gamma, L3_gnn_bn_beta):
    import jax
    import jax.numpy as jnp

    def _L0_gnn_ref(x, edge_index, eps, W1, b1, bn1_g, bn1_b, W2, b2, bn2_g, bn2_b, obn_g, obn_b, ln_g, ln_b, fp_W1, fp_b1, fp_ln1_g, fp_ln1_b, fp_W2, fp_b2, fp_ln2_g, fp_ln2_b):
        import jax, jax.numpy as jnp
        import numpy as np
        N, E, D, L = (6250, 75000, 128, 4)
        BN_EPS = 1e-05
        LN_EPS = 1e-05

        def _bn(h, g, b):
            m = h.mean(axis=0)
            v = h.var(axis=0)
            return (h - m) * jax.lax.rsqrt(v + BN_EPS) * g + b

        def _ln(h, g, b):
            m = h.mean(axis=-1, keepdims=True)
            v = h.var(axis=-1, keepdims=True)
            return (h - m) * jax.lax.rsqrt(v + LN_EPS) * g + b
        src, dst = (edge_index[0], edge_index[1])
        for i in range(L):
            x_in = x
            agg = jax.ops.segment_sum(x[src], dst, num_segments=N)
            h = (1.0 + eps[i]) * x + agg
            h = jax.nn.relu(_bn(h @ W1[i] + b1[i], bn1_g[i], bn1_b[i]))
            h = _bn(h @ W2[i] + b2[i], bn2_g[i], bn2_b[i])
            if i < L - 1:
                h = jax.nn.relu(h)
            h = _bn(h, obn_g[i], obn_b[i])
            if i < L - 1:
                h = jax.nn.relu(h)
            x = h + x_in
        x = _ln(x, ln_g, ln_b)
        h = jax.nn.relu(_ln(x @ fp_W1 + fp_b1, fp_ln1_g, fp_ln1_b))
        h = jax.nn.relu(_ln(h @ fp_W2 + fp_b2, fp_ln2_g, fp_ln2_b))
        return h

    def _L1_gnn_ref(x, edge_index, temporal_features, W_S_w, W_S_b, W_T_w, W_T_b, T_w, T_b):
        import jax, jax.numpy as jnp
        import numpy as np
        N_NODES = 12500
        N_EDGES = 125000
        IN_CH = 128
        OUT_CH = 128
        T_DIM = 64
        num_nodes = x.shape[0]
        row, col = (edge_index[0], edge_index[1])
        self_features = x @ W_S_w.T + W_S_b
        neighbor_features = x[col] @ W_T_w.T + W_T_b
        temporal_encodings = temporal_features @ T_w.T + T_b
        messages = neighbor_features + temporal_encodings
        aggregated = jax.ops.segment_sum(messages, row, num_segments=num_nodes)
        return jax.nn.relu(self_features + aggregated)

    def _L2_gnn_ref(x, edge_attr, We, be, W1, b1, W2, b2, gamma, beta, edge_index):
        import jax, jax.numpy as jnp
        import numpy as np
        N, E, C, EC, L = (6250, 75000, 128, 16, 4)
        LN_EPS = 1e-05
        src = edge_index[0]
        dst = edge_index[1]
        ea = jax.nn.silu(edge_attr @ We + be)
        n = x.shape[0]
        for l in range(L):
            msg = jax.nn.relu(x[src] + ea)
            agg = jax.ops.segment_sum(msg, dst, num_segments=n)
            h = x + agg
            h = jax.nn.silu(h @ W1[l] + b1[l]) @ W2[l] + b2[l]
            y = x + h
            mu = y.mean(-1, keepdims=True)
            var = y.var(-1, keepdims=True)
            x = (y - mu) * jax.lax.rsqrt(var + LN_EPS) * gamma[l] + beta[l]
        return x

    def _L3_gnn_ref(x, edge_attr, WQ, WK, WV, WE, bn_gamma, bn_beta, edge_index):
        import jax, jax.numpy as jnp
        import numpy as np
        NUM_HEADS = 8
        BN_EPS = 1e-05
        ATTN_EPS = 1e-06
        N, D = x.shape
        H = NUM_HEADS
        dh = D // H
        Q = (x @ WQ).reshape(N, H, dh)
        K = (x @ WK).reshape(N, H, dh)
        V = (x @ WV).reshape(N, H, dh)
        Eh = (edge_attr @ WE).reshape(-1, H, dh)
        src, dst = (edge_index[0], edge_index[1])
        score = K[src] * Q[dst] / jnp.sqrt(jnp.float32(dh)) * Eh
        score = jnp.exp(jnp.clip(score.sum(-1, keepdims=True), -5.0, 5.0))
        msg = V[src] * score
        wV = jax.ops.segment_sum(msg, dst, num_segments=N)
        Z = jax.ops.segment_sum(score, dst, num_segments=N)
        h_attn = (wV / (Z + ATTN_EPS)).reshape(N, D)
        h = x + h_attn
        mean = h.mean(axis=0)
        var = jnp.mean((h - mean) ** 2, axis=0)
        return (h - mean) * jax.lax.rsqrt(var + BN_EPS) * bn_gamma + bn_beta
    edge_index = jnp.stack([src, dst])
    x = _layernorm(x + _L0_gnn_ref(x, edge_index, L0_gnn_eps, L0_gnn_W1, L0_gnn_b1, L0_gnn_bn1_g, L0_gnn_bn1_b, L0_gnn_W2, L0_gnn_b2, L0_gnn_bn2_g, L0_gnn_bn2_b, L0_gnn_obn_g, L0_gnn_obn_b, L0_gnn_ln_g, L0_gnn_ln_b, L0_gnn_fp_W1, L0_gnn_fp_b1, L0_gnn_fp_ln1_g, L0_gnn_fp_ln1_b, L0_gnn_fp_W2, L0_gnn_fp_b2, L0_gnn_fp_ln2_g, L0_gnn_fp_ln2_b), axis=-1)
    x = _layernorm(x + _L1_gnn_ref(x, edge_index, edge_attr_64, L1_gnn_W_S_w, L1_gnn_W_S_b, L1_gnn_W_T_w, L1_gnn_W_T_b, L1_gnn_T_w, L1_gnn_T_b), axis=-1)
    x = _layernorm(x + _L2_gnn_ref(x, edge_attr_16, L2_gnn_We, L2_gnn_be, L2_gnn_W1, L2_gnn_b1, L2_gnn_W2, L2_gnn_b2, L2_gnn_gamma, L2_gnn_beta, edge_index), axis=-1)
    x = _layernorm(x + _L3_gnn_ref(x, edge_attr_128, L3_gnn_WQ, L3_gnn_WK, L3_gnn_WV, L3_gnn_WE, L3_gnn_bn_gamma, L3_gnn_bn_beta, edge_index), axis=-1)
    return x

_drawn_inputs = setup_inputs


def setup_inputs(seed=0):
    import zlib

    import numpy as np

    out = dict(_drawn_inputs(seed))
    spreads = {'L0_gnn_eps': (0.0, 0.676),
     'L0_gnn_b1': (0.0, 0.8),
     'L0_gnn_bn1_g': (1.0, 0.2),
     'L0_gnn_bn1_b': (0.0, 0.1),
     'L0_gnn_b2': (0.0, 0.8),
     'L0_gnn_bn2_g': (1.0, 0.6),
     'L0_gnn_bn2_b': (0.0, 0.328),
     'L0_gnn_obn_g': (1.0, 0.2),
     'L0_gnn_obn_b': (0.0, 0.1),
     'L0_gnn_ln_g': (1.0, 0.2),
     'L0_gnn_ln_b': (0.0, 0.1),
     'L0_gnn_fp_b1': (0.0, 0.1),
     'L0_gnn_fp_ln1_g': (1.0, 0.2),
     'L0_gnn_fp_ln1_b': (0.0, 0.1),
     'L0_gnn_fp_b2': (0.0, 0.1),
     'L0_gnn_fp_ln2_g': (1.0, 0.2),
     'L0_gnn_fp_ln2_b': (0.0, 0.1),
     'L2_gnn_be': (0.0, 0.1),
     'L2_gnn_b1': (0.0, 0.8),
     'L2_gnn_b2': (0.0, 0.8),
     'L2_gnn_gamma': (1.0, 0.2),
     'L2_gnn_beta': (0.0, 0.1),
     'L3_gnn_bn_gamma': (1.0, 0.2),
     'L3_gnn_bn_beta': (0.0, 0.1)}
    factors = {'L1_gnn_W_S_b': 6.334}
    for name, (base, spread) in spreads.items():
        noise = np.random.default_rng([zlib.crc32(name.encode()), seed]).standard_normal(out[name].shape)
        drawn = base * np.exp(spread * noise) if base else spread * noise
        out[name] = jnp.asarray(drawn.astype(out[name].dtype))
    for name, factor in factors.items():
        out[name] = (out[name] * factor).astype(out[name].dtype)
    return out
```

```python
from contextlib import ExitStack

import numpy as np
import concourse.bass as bass
from concourse import mybir

F32, I32 = mybir.dt.float32, mybir.dt.int32
ALU, ACT = mybir.AluOpType, mybir.ActivationFunctionType
ds = bass.ds

N, E, D = 6250, 106250, 128
P = 128
LAYERS = 4
HEADS = 8
DH = D // HEADS
A16, A64 = 16, 64
EPS = 1e-5
ATTN_EPS = 1e-6

TILES = -(-N // P)
BUCKETS = TILES + 1
NODES_PAD = BUCKETS * P
PER = 4
RING = 4
COLS = -(-E // (P * PER * RING)) * PER * RING
E_PAD = COLS * P
CHUNKS = (E + TILES * (P - 1)) // P + -(-(E_PAD - E) // P)
CHUNKS = -(-CHUNKS // (PER * RING)) * PER * RING
SLOTS = CHUNKS * P
LOOK = PER * RING
TCOLS = -(-CHUNKS // P)
GROUPS = CHUNKS // PER
TRIPS = GROUPS // RING
LOADS = COLS // PER // RING
TAIL = CHUNKS - COLS + PER

NT = 125
NTILES = N // NT
BLK = 2 * NT
NBLK = N // BLK
SLOTS_PS = 5
SWEEPS = NBLK // SLOTS_PS

REC_D = D + D + 3
REC_S = A64 + 2 + 2
XT, HT, AC, NA, RE = range(5)


def weight_columns():
    at, where = 0, {}
    for name, width in (("w1", LAYERS * D), ("w2", LAYERS * D), ("v1", LAYERS * D), ("v2", LAYERS * D),
                        ("f1", 2 * D), ("f2", 2 * D), ("ws", D), ("wt", D), ("we", D), ("kv", 2 * D), ("q", D)):
        where[name] = at
        at += width
    return where, at


def row_columns():
    at, where = 0, {}
    for name, width in (("ln_g", D), ("ln_b", D), ("f_b1", 2 * D), ("f_g1", 2 * D), ("f_h1", 2 * D),
                        ("f_b2", D), ("f_g2", D), ("f_h2", D), ("v_b2", LAYERS * D), ("gamma", LAYERS * D),
                        ("beta", LAYERS * D), ("eps", LAYERS)):
        where[name] = at
        at += width
    return where, at


def feature_columns():
    names = [f"{n}{l}" for n in ("b1", "bn1_g", "bn1_b", "b2", "bn2_g", "bn2_b", "obn_g", "obn_b", "v_b1")
             for l in range(LAYERS)] + ["s_b", "bn_g", "bn_b"]
    return {n: i for i, n in enumerate(names)}, len(names)


W_AT, W_N = weight_columns()
R_AT, R_N = row_columns()
C_AT, C_N = feature_columns()


def network(do):
    do("setup")
    do("rank", "d")
    do("rank", "s")
    do("scatter_d")
    do("scatter_s")
    do("load_meta")
    do("load_xt")
    for l in range(LAYERS):
        last = l == LAYERS - 1
        act = ACT.Identity if last else ACT.Relu
        do("edges", "sum", "x" if l == 0 else "xg", l)
        do("linear", [(("w1", l), AC)], ACT.Identity, f"b1{l}", HT, f"bn1_g{l}", f"bn1_b{l}")
        do("norm_apply", HT, AC, ACT.Relu, None)
        do("linear", [(("w2", l), AC)], ACT.Identity, f"b2{l}", HT, f"bn2_g{l}", f"bn2_b{l}")
        do("norm_apply", HT, AC, act, (f"obn_g{l}", f"obn_b{l}"))
        do("norm_apply", AC, HT, act, "residual")
        do("to_nat", XT, NA)
        if not last:
            do("store", NA, "xg", D)
    do("layer_norm", NA, D, "ln_g", "ln_b", False)
    do("to_t", NA, D, 0, AC)
    do("linear_nat", [(AC, "f1", 0)], 2 * D, "f_b1", XT, False)
    do("layer_norm", XT, 2 * D, "f_g1", "f_h1", True)
    do("to_t", XT, 2 * D, 0, AC)
    do("to_t", XT, 2 * D, D, RE)
    do("linear_nat", [(AC, "f2", 0), (RE, "f2", D)], D, "f_b2", NA, False)
    do("layer_norm", NA, D, "f_g2", "f_h2", True)
    do("load_x", RE)
    do("add", NA, RE)
    do("layer_norm", NA, D, None, None, False)
    do("store", NA, "xg", D)
    do("to_t", NA, D, 0, XT)
    do("edges", "attr", "xg", 0)
    do("linear", [(("ws", 0), XT), (("wt", 0), AC), ("attr", HT)], ACT.Relu, "s_b", AC, None, None)
    do("to_nat", AC, RE)
    do("add", NA, RE)
    do("layer_norm", NA, D, None, None, False)
    do("store", NA, "xg", D)
    do("to_t", NA, D, 0, XT)
    do("copy", RE, NA)
    for l in range(LAYERS):
        do("edges", "msg", "xg", l)
        do("linear", [(("v1", l), AC)], ACT.Silu, f"v_b1{l}", HT, None, None)
        do("linear_nat", [(HT, "v2", l * D)], D, ("v_b2", l), NA, True)
        do("layer_norm", NA, D, ("gamma", l), ("beta", l), False)
        if l < LAYERS - 1:
            do("store", NA, "xg", D)
            do("to_t", NA, D, 0, XT)
    do("add", NA, RE)
    do("layer_norm", NA, D, None, None, False)
    do("to_t", NA, D, 0, XT)
    do("linear_nat", [(XT, "kv", 0)], 2 * D, None, AC, False)
    do("store", AC, "kv", 2 * D)
    do("linear_nat", [(XT, "q", 0)], D, None, RE, False)
    do("store", RE, "q", D)
    do("edges", "attn", "kv", 0)
    do("attend")
    do("norm_apply", AC, HT, ACT.Identity, "residual")
    do("to_nat", XT, NA)
    do("layer_norm", NA, D, None, None, False)
    do("store", NA, "out", D)


def rolled(eng, count, body):
    body(0, True)
    if count > 1:
        with eng.Fori(1, count) as i:
            body(i, False)


class Chain:

    def __init__(self, eng, sem):
        self.eng, self.sem, self.n, self.base, self.k = eng, sem, 0, None, 0

    def mark(self, ins):
        ins.then_inc(self.sem, 1)
        if self.base is None:
            self.n += 1
        else:
            self.k += 1

    def wait(self):
        self.eng.wait_ge(self.sem, self.n if self.base is None else self.base + self.k)

    def link(self, ins):
        self.mark(ins)
        self.wait()

    def trip(self, i, per):
        self.base, self.k = self.n + i * per, 0

    def leave(self, trips, per):
        assert self.k == per, (self.k, per)
        self.n, self.base = self.n + trips * per, None


def program(nc, A):
    ctx = ExitStack()
    with ctx:
        def sb(name, shape, dt=F32):
            return ctx.enter_context(nc.sbuf_tensor(name, shape, dt))

        def sem(name):
            return ctx.enter_context(nc.semaphore(name))

        rec_d = nc.dram_tensor("rec_d", [SLOTS, REC_D], F32).ap()
        rec_s = nc.dram_tensor("rec_s", [SLOTS, REC_S], F32).ap()
        tile_row = {w: nc.dram_tensor(f"tile_row_{w}", [TCOLS, P], I32).ap() for w in "ds"}
        table = {"x": A["x"], "out": A["out"],
                 "xg": nc.dram_tensor("x_table", [N, D], F32).ap(),
                 "kv": nc.dram_tensor("kv_table", [N, 2 * D], F32).ap(),
                 "q": nc.dram_tensor("q_table", [N, D], F32).ap()}

        big = sb("big", [P, 5 * NODES_PAD])
        weights = sb("weights", [P, W_N])
        rows = sb("rows", [P, R_N])
        feats = sb("feats", [P, C_N])
        attr_w = sb("attr_w", [A64 + 2, D])
        ea_w = sb("ea_w", [A16 + 1, D])
        idx = {w: sb(f"idx_{w}", [P, CHUNKS + LOOK], I32) for w in "ds"}
        node = {w: sb(f"node_{w}", [P, CHUNKS + LOOK]) for w in "ds"}
        q_idx = sb("q_idx", [P, CHUNKS + LOOK], I32)
        tile_at = {w: sb(f"tile_at_{w}", [1, TCOLS * P], I32) for w in "ds"}
        last_chunk = {w: sb(f"last_chunk_{w}", [1, BUCKETS], I32) for w in "ds"}
        gath = sb("gath", [P, RING, PER, D])
        onehot = sb("onehot", [P, RING, PER, P])
        idx_ring = sb("idx_ring", [P, RING, PER], I32)
        q_ring = sb("q_ring", [P, RING, PER], I32)
        heads = sb("heads", [P, RING, PER * HEADS])
        iota = sb("iota", [P, P])
        part = sb("part", [P, 1])
        ident = sb("ident", [P, P])
        before = sb("before", [P, P])
        ones = sb("ones", [P, P])
        stats = sb("stats", [P, NTILES * 6])
        st3 = stats[0:NT, :].rearrange("p (t s) -> p t s", s=6)
        mv = sb("mv", [P, NTILES * 3])
        mv3 = mv[:, :].rearrange("p (t s) -> p t s", s=3)
        scale = sb("scale", [P, NTILES])
        shift = sb("shift", [P, NTILES])
        eps1 = sb("eps1", [P, LAYERS])
        small = sb("small", [P, 8, BUCKETS])
        small_i = sb("small_i", [P, 2, BUCKETS], I32)
        ps = ctx.enter_context(nc.psum_tensor("ps", [P, 8, 512], F32))

        small_i_tiles = small_i[:, 0, 0:TCOLS]

        def T(b, n=N, rows_=P):
            return big[0:rows_, b * NODES_PAD:b * NODES_PAD + n]

        def nat(b, w=D):
            return big[0:NT, b * NODES_PAD:b * NODES_PAD + NTILES * w].rearrange("p (t w) -> p t w", w=w)

        def weight(name, off=0, width=D):
            return weights[:, W_AT[name] + off:W_AT[name] + off + width]

        def row(name, width=D):
            name, l = name if isinstance(name, tuple) else (name, 0)
            at = R_AT[name] + l * D
            return rows[0:NT, at:at + width]

        def feat(name):
            return feats[:, C_AT[name]:C_AT[name] + 1]

        at = [0]

        def part_of_big(shape, start=None):
            if start is not None:
                at[0] = start
            n = int(np.prod(shape[1:]))
            v = big[0:shape[0], at[0]:at[0] + n]
            at[0] += n
            assert at[0] <= 5 * NODES_PAD
            if len(shape) == 4:
                v = v.rearrange("p (a b c) -> p a b c", a=shape[1], b=shape[2])
            elif len(shape) == 3:
                v = v.rearrange("p (a b) -> p a b", a=shape[1])
            return v

        meta_d = part_of_big([P, COLS, 3]).bitcast(I32)
        meta_s = part_of_big([P, COLS, 2]).bitcast(I32)
        pos = {w: part_of_big([P, COLS]).bitcast(I32) for w in "ds"}
        key = {w: part_of_big([P, COLS]).bitcast(I32) for w in "ds"}
        val = {w: part_of_big([P, COLS]).bitcast(I32) for w in "ds"}
        tile_i = part_of_big([P, COLS]).bitcast(I32)
        tile_f = part_of_big([P, COLS])
        equal = part_of_big([P, COLS])
        count = part_of_big([P, COLS])
        match = part_of_big([P, COLS])
        pos_f = part_of_big([P, COLS])
        ones_c = part_of_big([P, COLS])
        blank = part_of_big([P, REC_D])
        blank_s = part_of_big([P, REC_S])
        rec = part_of_big([P, RING, PER, REC_D])
        attr_t = part_of_big([P, RING, PER * P])
        a16_t = part_of_big([A16 + 1, RING, PER * P])
        rec2 = part_of_big([P, RING, PER, REC_S])
        meta_in = {"d": part_of_big([P, CHUNKS, 3], 0).bitcast(I32), "s": part_of_big([P, CHUNKS, 2]).bitcast(I32)}
        attr_r = part_of_big([P, RING, PER, A64 + 2], RE * NODES_PAD)
        ea_r = part_of_big([P, RING, PER, D], HT * NODES_PAD)
        msg_r = part_of_big([P, RING, PER, D])
        kv_r = part_of_big([P, RING, PER, 2 * D], NA * NODES_PAD)
        q_r = part_of_big([P, RING, PER, D])
        eh_r = part_of_big([P, RING, PER, D], RE * NODES_PAD)
        sc_r = part_of_big([P, RING, PER * HEADS, DH])
        at_r = msg_a = gath

        stage_done = sem("stage_done")
        loaded = sem("loaded")
        consts = sem("consts")
        pool_step = sem("pool_step")
        dve_chain, act_chain = sem("dve_chain"), sem("act_chain")
        totals_ready = sem("totals_ready")
        sums_ready = sem("sums_ready")
        tiles_ready = sem("tiles_ready")
        ranked = sem("ranked")
        moved = sem("moved")
        blanked = sem("blanked")
        att_in = [sem(f"att_in{q}") for q in range(RING)]
        att2_in = [sem(f"att2_in{q}") for q in range(RING)]
        rec_mm, silu_done, rec_ready = sem("rec_mm"), sem("silu_done"), sem("rec_ready")
        rec2_ready = sem("rec2_ready")
        rec_out = [sem(f"rec_out{q}") for q in range(RING)]
        rec2_out = [sem(f"rec2_out{q}") for q in range(RING)]
        meta_loaded = sem("meta_loaded")
        idx_ready = sem("idx_ready")
        onehot_ready = sem("onehot_ready")
        msg_sum, msg_ready = sem("msg_sum"), sem("msg_ready")
        attn_ready, score_ready, exp_done = sem("attn_ready"), sem("score_ready"), sem("exp_done")
        seg_done = sem("seg_done")
        gathered = {k: [sem(f"gathered_{k}{q}") for q in range(RING)] for k in ("sum", "attr", "msg", "attn")}
        q_gathered = [sem(f"q_gathered{q}") for q in range(RING)]
        edge_in = {k: [sem(f"edge_in_{k}{q}") for q in range(RING)] for k in ("attr", "msg", "attn")}
        mm_full, mm_free = sem("mm_full"), sem("mm_free")
        act_blk = sem("act_blk")
        var_ready, std_ready = sem("var_ready"), sem("std_ready")
        stat_ready = sem("stat_ready")
        ln_part = sem("ln_part")
        io_done = sem("io_done")

        block = ctx.enter_context(nc.Block())

        def walk(eng, **mine):
            seen = {}
            stage = [0]

            def do(kind, *args):
                names = [kind, (kind, args[0])] if kind == "edges" else [kind]
                if kind in ("linear", "to_nat", "to_t", "linear_nat"):
                    names.append("blocks")
                if kind in ("store", "load_x", "load_xt"):
                    names.append("io")
                if kind in ("layer_norm", "attend") or (kind == "linear" and args[4] is not None) \
                        or (kind == "norm_apply" and isinstance(args[3], tuple)):
                    names.append("norms")
                n = {x: seen.get(x, 0) for x in names}
                if kind in mine:
                    if stage[0]:
                        eng.wait_ge(stage_done, stage[0])
                    mine[kind](n, *args)
                stage[0] += 1
                for x in names:
                    seen[x] = seen.get(x, 0) + 1

            network(do)
            return stage[0]

        src_of = {"sum": "d", "attr": "s", "msg": "d", "attn": "d"}

        @block.sync
        def _(sp):
            rd = rec_d.rearrange("(c p) w -> p c w", p=P)
            rs = rec_s.rearrange("(c p) w -> p c w", p=P)

            def setup(n):
                for dst, src in ((weights[:, :], A["weights"]), (feats[:, :], A["feats"]),
                                 (rows[:, :], A["rows"].partition_broadcast(P)),
                                 (attr_w[:, :], A["attr_w"]), (ea_w[:, :], A["ea_w"]),
                                 (key["d"], A["dst_key"]), (key["s"], A["src_key"]),
                                 (val["d"], A["src_val"]), (val["s"], A["dst_val"])):
                    sp.dma_start(dst, src).then_inc(loaded, 16)

            def rank(n, w):
                k = n["rank"]
                sp.wait_ge(tiles_ready, k + 1)
                with nc.allow_non_contiguous_dma(reason="a few hundred values"):
                    sp.dma_start(tile_row[w].rearrange("k p -> p k"), small_i_tiles).then_inc(moved, 16)
                sp.wait_ge(moved, 32 * k + 16)
                sp.dma_start(tile_at[w][:, :], tile_row[w].rearrange("k p -> (k p)").unsqueeze(0)).then_inc(moved, 16)
                sp.wait_ge(moved, 32 * k + 32)
                r, b = (rec_d, blank) if w == "d" else (rec_s, blank_s)
                tail = (rd if w == "d" else rs)[:, CHUNKS - TAIL:CHUNKS, :]
                sp.dma_start(tail, b.unsqueeze(1).to_broadcast([P, TAIL, b.shape[1]])).then_inc(blanked, 16)
                with sp.Fori(0, BUCKETS) as i:
                    c = sp.value_load(last_chunk[w][0:1, ds(i, 1)], min_val=0, max_val=SLOTS - P)
                    sp.wait_ge(blanked, 16 * (BUCKETS + 1) * k + 16 * i + 16)
                    sp.dma_start(r[ds(c, P), :], b).then_inc(blanked, 16)
                sp.wait_ge(blanked, 16 * (BUCKETS + 1) * (k + 1))
                sp.wait_ge(ranked, k + 1)
                sp.nop(nofuse=True).then_inc(stage_done, 1)

            def scatter_d(n):
                def trip(i, first):
                    for q in range(RING):
                        if not first:
                            sp.wait_ge(rec_ready, RING * i + q - RING + 1)
                        cols = ds((i * RING + q) * PER * P, PER * P)
                        sp.dma_start(attr_t[:, q, :], A["attr128_t"][:, cols]).then_inc(att_in[q], 16)
                        sp.dma_start(a16_t[:, q, :], A["attr16_t"][:, cols]).then_inc(att_in[q], 16)
                rolled(sp, LOADS, trip)
                for q in range(RING):
                    sp.wait_ge(rec_out[q], 16 * PER * LOADS)
                sp.nop(nofuse=True).then_inc(stage_done, 1)

            def scatter_s(n):
                a64 = A["attr64"].rearrange("(c p) w -> p c w", p=P)

                def trip(i, first):
                    for q in range(RING):
                        if not first:
                            sp.wait_ge(rec2_out[q], 16 * PER * i)
                        sp.dma_start(rec2[:, q, :, 0:A64], a64[:, ds((i * RING + q) * PER, PER), :])\
                          .then_inc(att2_in[q], 16)
                rolled(sp, LOADS, trip)
                for q in range(RING):
                    sp.wait_ge(rec2_out[q], 16 * PER * LOADS)
                sp.nop(nofuse=True).then_inc(stage_done, 1)

            def load_meta(n):
                sp.dma_start(meta_in["d"], rd[:, :, 2 * D:REC_D].bitcast(I32)).then_inc(meta_loaded, 16)
                sp.dma_start(meta_in["s"], rs[:, :, A64 + 2:REC_S].bitcast(I32)).then_inc(meta_loaded, 16)

            def edges(n, way, tab, l):
                if way == "sum":
                    return
                ring, src = {"attr": (attr_r, rs[:, :, 0:A64 + 2]), "msg": (ea_r, rd[:, :, D:2 * D]),
                             "attn": (eh_r, rd[:, :, 0:D])}[way]
                base, done = n["edges"] * (GROUPS + RING), n["edges", way]
                with sp.Fori(0, TRIPS) as i:
                    for q in range(RING):
                        sp.wait_ge(idx_ready, base + RING * i + q + 1)
                        sp.dma_start(ring[:, q, :, :], src[:, ds((i * RING + q) * PER, PER), :])\
                          .then_inc(edge_in[way][q], 16)

            def store(n, b, tab, w):
                sp.dma_start(table[tab].rearrange("(t p) w -> p t w", p=NT), nat(b, w)).then_inc(io_done, 16)
                sp.wait_ge(io_done, 16 * (n["io"] + 1))
                sp.nop(nofuse=True).then_inc(stage_done, 1)

            def load_xt(n):
                sp.dma_start(T(XT), A["x_t"]).then_inc(io_done, 16)
                sp.wait_ge(io_done, 16 * (n["io"] + 1))
                sp.nop(nofuse=True).then_inc(stage_done, 1)

            def load_x(n, b):
                sp.dma_start(nat(b), A["x"].rearrange("(t p) w -> p t w", p=NT)).then_inc(io_done, 16)
                sp.wait_ge(io_done, 16 * (n["io"] + 1))
                sp.nop(nofuse=True).then_inc(stage_done, 1)

            total = walk(sp, setup=setup, rank=rank, scatter_d=scatter_d, scatter_s=scatter_s,
                         load_meta=load_meta, edges=edges, store=store, load_x=load_x, load_xt=load_xt)
            sp.wait_ge(stage_done, total)

        @block.gpsimd
        def _(pool):
            def setup(n):
                pool.iota(iota[:, :], [[1, P]], base=0, channel_multiplier=0,
                          allow_small_or_imprecise_dtypes=True).then_inc(consts, 1)
                pool.iota(part[:, :], [[0, 1]], base=0, channel_multiplier=1,
                          allow_small_or_imprecise_dtypes=True).then_inc(consts, 1)
                pool.memset(ident[:, :], 0.0).then_inc(pool_step, 1)
                pool.memset(before[:, :], 1.0).then_inc(pool_step, 1)
                pool.memset(ones[:, :], 1.0).then_inc(consts, 1)
                pool.wait_ge(pool_step, 2)
                pool.affine_select(out=ident[:, :], in_=ident[:, :], compare_op=ALU.not_equal, fill=1.0, base=0,
                                   pattern=[[-1, P]], channel_multiplier=1).then_inc(consts, 1)
                pool.affine_select(out=before[:, :], in_=before[:, :], compare_op=ALU.is_gt, fill=0.0, base=0,
                                   pattern=[[1, P]], channel_multiplier=-1).then_inc(consts, 1)

            def scatter(ready, rec_ring, out, done, idx_):
                def trip(i, first):
                    for q in range(RING):
                        for r, per in ready:
                            s = r if not isinstance(r, list) else r[q]
                            pool.wait_ge(s, (RING * i + q + 1) if per is None else per * (i + 1))
                        pool.nop(nofuse=True)
                        for k in range(PER):
                            pool.indirect_dma_start(
                                out, bass.IndirectOffsetOnAxis(ap=idx_[:, q, k:k + 1], axis=0),
                                rec_ring[:, q, k, :], None).then_inc(done[q], 16)
                rolled(pool, LOADS, trip)

            def scatter_d(n):
                scatter([(rec_ready, None)], rec, rec_d, rec_out, idx_ring)

            def scatter_s(n):
                scatter([(rec2_ready, None), (att2_in, 16)], rec2, rec_s, rec2_out, q_ring)

            def edges(n, way, tab, l):
                base = n["edges"] * (GROUPS + RING)
                ring = kv_r if way == "attn" else gath
                with pool.Fori(0, TRIPS) as i:
                    for q in range(RING):
                        pool.wait_ge(idx_ready, base + RING * i + q + 1)
                        pool.nop(nofuse=True)
                        for k in range(PER):
                            pool.indirect_dma_start(
                                ring[:, q, k, :], None, table[tab],
                                bass.IndirectOffsetOnAxis(ap=idx_ring[:, q, k:k + 1], axis=0))\
                                .then_inc(gathered[way][q], 16)
                            if way == "attn":
                                pool.indirect_dma_start(
                                    q_r[:, q, k, :], None, table["q"],
                                    bass.IndirectOffsetOnAxis(ap=q_ring[:, q, k:k + 1], axis=0))\
                                    .then_inc(q_gathered[q], 16)

            walk(pool, setup=setup, scatter_d=scatter_d, scatter_s=scatter_s, edges=edges)

        @block.tensor
        def _(pe):
            def rank(n, w):
                k = n["rank"]
                pe.wait_ge(totals_ready, k + 1)
                pe.matmul(ps[:, 0, 0:BUCKETS], ones[:, :], small[:, 0, :], start=True, stop=True)
                pe.matmul(ps[:, 1, 0:BUCKETS], before[:, :], small[:, 0, :], start=True, stop=True)\
                  .then_inc(sums_ready, 1)

            def scatter_d(n):
                def trip(i, first):
                    for q in range(RING):
                        pe.wait_ge(att_in[q], 32 * i + 32)
                        for k in range(PER):
                            c = slice(k * P, (k + 1) * P)
                            pe.matmul(ps[:, q, c], attr_t[:, q, c], weight("we"), start=True, stop=True)
                            last = pe.matmul(ps[:, RING + q, c], a16_t[:, q, c], ea_w[:, :], start=True, stop=True)
                        last.then_inc(rec_mm, 1)
                rolled(pe, LOADS, trip)

            def edges(n, way, tab, l):
                base, done = n["edges"] * GROUPS, n["edges", way]
                with pe.Fori(0, TRIPS) as i:
                    for q in range(RING):
                        pe.wait_ge(onehot_ready, base + RING * i + q + 1)
                        if way in ("sum", "attr"):
                            pe.wait_ge(gathered[way][q], 16 * PER * (done * TRIPS + i + 1))
                        if way == "attr":
                            pe.wait_ge(edge_in[way][q], 16 * (done * TRIPS + i + 1))
                        if way == "msg":
                            pe.wait_ge(msg_ready, done * GROUPS + RING * i + q + 1)
                        if way == "attn":
                            pe.wait_ge(attn_ready, done * GROUPS + RING * i + q + 1)
                        src = msg_r if way == "msg" else gath
                        for k in range(PER):
                            c = slice(k * P, (k + 1) * P)
                            last = pe.matmul(ps[:, q, c], src[:, q, k, :], onehot[:, q, k, :], start=True, stop=True)
                            if way == "attr":
                                last = pe.matmul(ps[0:A64 + 2, RING + q, c], attr_r[:, q, k, :], onehot[:, q, k, :],
                                                 start=True, stop=True)
                            if way == "attn":
                                sc = sc_r[:, q, k * HEADS:(k + 1) * HEADS, :].rearrange("p h d -> p (h d)")
                                last = pe.matmul(ps[:, RING + q, c], sc, onehot[:, q, k, :], start=True, stop=True)
                        last.then_inc(seg_done, 1)

            def blocks(n, one, fixed=False):
                base = n["blocks"] * NBLK

                def sweep(i, first):
                    for s in range(SLOTS_PS):
                        if not first:
                            pe.wait_ge(mm_free, base + SLOTS_PS * i + s - SLOTS_PS + 1)
                        one(i * SLOTS_PS + s, s).then_inc(mm_full, 1)
                if fixed:
                    for i in range(SWEEPS):
                        sweep(i, i == 0)
                else:
                    rolled(pe, SWEEPS, sweep)

            def linear(n, terms, func, bias, dst, g, b):
                def one(j, s):
                    for t, (w, src) in enumerate(terms):
                        k = P if w != "attr" else A64 + 2
                        lhs = attr_w[:, :] if w == "attr" else weight(w[0], w[1] * D)
                        last = pe.matmul(ps[:, s, 0:BLK], lhs, T(src, rows_=k)[:, ds(j * BLK, BLK)],
                                         start=t == 0, stop=t == len(terms) - 1)
                    return last
                blocks(n, one)

            def to_nat(n, src, dst):
                def one(j, s):
                    for k in range(2):
                        last = pe.transpose(ps[0:NT, s, k * D:(k + 1) * D], T(src)[:, j * BLK + k * NT:j * BLK + (k + 1) * NT],
                                            ident[:, :])
                    return last
                blocks(n, one, fixed=True)

            def to_t(n, src, w, off, dst):
                def one(j, s):
                    for k in range(2):
                        last = pe.transpose(ps[:, s, k * NT:(k + 1) * NT],
                                            big[0:NT, src * NODES_PAD + off + (2 * j + k) * w:src * NODES_PAD + off + (2 * j + k) * w + D],
                                            ident[0:NT, 0:NT])
                    return last
                blocks(n, one, fixed=True)

            def linear_nat(n, terms, w, bias, dst, plus):
                def one(j, s):
                    for k in range(2):
                        for t, (src, name, off) in enumerate(terms):
                            last = pe.matmul(ps[0:NT, s, k * w:(k + 1) * w], T(src)[:, j * BLK + k * NT:j * BLK + (k + 1) * NT],
                                             weight(name, off, w), start=t == 0, stop=t == len(terms) - 1)
                    return last
                blocks(n, one, fixed=True)

            walk(pe, rank=rank, scatter_d=scatter_d, edges=edges, linear=linear, to_nat=to_nat, to_t=to_t,
                 linear_nat=linear_nat)

        @block.scalar
        def _(act):
            def scatter_d(n):
                def trip(i, first):
                    for q in range(RING):
                        act.wait_ge(rec_mm, RING * i + q + 1)
                        if not first:
                            act.wait_ge(rec_out[q], 16 * PER * i)
                        act.activation(rec[:, q, :, D:2 * D], ps[:, RING + q, :].rearrange("p (k f) -> p k f", f=D),
                                       ACT.Silu).then_inc(silu_done, 1)
                rolled(act, LOADS, trip)

            def edges(n, way, tab, l):
                done = n["edges", way]
                if way == "msg":
                    with act.Fori(0, TRIPS) as i:
                        for q in range(RING):
                            act.wait_ge(msg_sum, done * GROUPS + RING * i + q + 1)
                            act.activation(msg_r[:, q, :, :], msg_r[:, q, :, :], ACT.Relu).then_inc(msg_ready, 1)
                if way == "attn":
                    with act.Fori(0, TRIPS) as i:
                        for q in range(RING):
                            act.wait_ge(score_ready, RING * i + q + 1)
                            act.activation(sc_r[:, q, :, :], heads[:, q, :].unsqueeze(2)
                                           .to_broadcast([P, PER * HEADS, DH]), ACT.Exp).then_inc(exp_done, 1)

            def root(n, v):
                act.wait_ge(var_ready, n["norms"] + 1)
                act.activation(v, v, ACT.Sqrt).then_inc(std_ready, 1)

            def attend(n):
                root(n, mv[:, 1:2])

            def evacuate(n, one, end):
                base = n["blocks"] * NBLK
                with act.Fori(0, SWEEPS) as i:
                    for s in range(SLOTS_PS):
                        act.wait_ge(mm_full, base + SLOTS_PS * i + s + 1)
                        one(i * SLOTS_PS + s, s).then_inc(mm_free, 1)
                if end:
                    act.wait_ge(mm_free, base + NBLK)
                    act.nop(nofuse=True).then_inc(stage_done, 1)

            def linear(n, terms, func, bias, dst, g, b):
                base = n["blocks"] * NBLK
                evacuate(n, lambda j, s: act.activation(T(dst)[:, ds(j * BLK, BLK)], ps[:, s, 0:BLK], func,
                                                        bias=feat(bias)), g is None)
                if g is not None:
                    root(n, mv[:, 1:2])

            def to_nat(n, src, dst):
                evacuate(n, lambda j, s: act.activation(
                    big[0:NT, ds(dst * NODES_PAD + j * 2 * D, 2 * D)], ps[0:NT, s, 0:2 * D], ACT.Copy), True)

            def to_t(n, src, w, off, dst):
                evacuate(n, lambda j, s: act.activation(T(dst)[:, ds(j * BLK, BLK)], ps[:, s, 0:BLK], ACT.Copy), True)

            def norm_apply(n, src, dst, func, then):
                with act.Fori(0, NBLK) as j:
                    act.activation(T(dst)[:, ds(j * BLK, BLK)], T(src)[:, ds(j * BLK, BLK)], func,
                                   bias=shift[:, 0:1], scale=scale[:, 0:1]).then_inc(act_blk, 1)
                if then is None:
                    act.wait_ge(act_blk, NBLK * (n["norm_apply"] + 1))
                    act.nop(nofuse=True).then_inc(stage_done, 1)
                elif then != "residual":
                    root(n, mv[:, 1:2])

            def layer_norm(n, b, w, g, h, relu):
                root(n, mv3[0:NT, :, 2])
                act.wait_ge(stat_ready, n["layer_norm"] + 1)
                with act.Fori(0, 5) as i:
                    for k in range(NTILES // 5):
                        t = big[0:NT, ds(b * NODES_PAD + k * w + i * (NTILES // 5 * w), w)]
                        last = act.activation(t, t, ACT.Identity,
                                              bias=shift[0:NT, ds(i * (NTILES // 5) + k, 1)],
                                              scale=scale[0:NT, ds(i * (NTILES // 5) + k, 1)])
                    last.then_inc(ln_part, 1)

            walk(act, scatter_d=scatter_d, edges=edges, linear=linear, to_nat=to_nat, to_t=to_t,
                 norm_apply=norm_apply, layer_norm=layer_norm, attend=attend)

        @block.vector
        def _(dve):
            ch = Chain(dve, dve_chain)

            def setup(n):
                dve.wait_ge(loaded, 16 * 9)
                dve.wait_ge(consts, 5)
                ch.mark(dve.memset(blank, 0.0))
                ch.link(dve.memset(blank_s, 0.0))
                dve.memset(blank[:, REC_D - 1:REC_D].bitcast(I32), P)
                dve.memset(blank_s[:, REC_S - 1:REC_S].bitcast(I32), P)
                dve.memset(ones_c, 1.0)
                dve.memset(rec2[:, :, :, A64:A64 + 2], 1.0)
                eps = rows[:, R_AT["eps"]:R_AT["eps"] + LAYERS]
                dve.tensor_scalar(eps1[:, :], eps, 1.0, None, ALU.add)
                for w in "ds":
                    dve.memset(idx[w][:, CHUNKS:], 0)
                    dve.memset(node[w][:, CHUNKS:], -1.0)
                dve.memset(q_idx[:, CHUNKS:], 0).then_inc(stage_done, 1)

            def rank(n, w):
                k = n["rank"]
                meta = meta_d if w == "d" else meta_s
                ch.link(dve.tensor_single_scalar(tile_i, key[w], 7, ALU.arith_shift_right))
                ch.link(dve.tensor_copy(tile_f, tile_i))
                dve.tensor_single_scalar(meta[:, :, meta.shape[2] - 1], key[w], P - 1, ALU.bitwise_and)
                dve.tensor_copy(meta[:, :, 0], val[w])
                if w == "d":
                    dve.tensor_copy(meta[:, :, 1], val["s"])
                with dve.Fori(0, BUCKETS) as b:
                    ch.trip(b, 1)
                    ch.link(dve.tensor_scalar(equal, tile_f, iota[:, ds(b, 1)], 0.0, ALU.is_equal, ALU.add,
                                              accum_out=small[:, 0, ds(b, 1)]))
                ch.leave(BUCKETS, 1)
                dve.memset(pos_f, 0.0).then_inc(totals_ready, 1)
                dve.wait_ge(sums_ready, k + 1)
                ch.link(dve.tensor_scalar(small[:, 1, :], ps[:, 0, 0:BUCKETS], float(P - 1), None, ALU.add))
                ch.link(dve.tensor_copy(small_i[:, 0, :], small[:, 1, :]))
                ch.link(dve.tensor_single_scalar(small_i[:, 1, :], small_i[:, 0, :], 7, ALU.arith_shift_right))
                ch.link(dve.tensor_copy(small[:, 2, :], small_i[:, 1, :]))
                ch.link(dve.tensor_tensor_scan(small[:, 3, :], ones[:, 0:BUCKETS], small[:, 2, :], 0.0,
                                               ALU.mult, ALU.add))
                ch.link(dve.tensor_tensor(small[:, 4, :], small[:, 3, :], small[:, 2, :], ALU.subtract))
                ch.link(dve.scalar_tensor_tensor(small[:, 5, :], small[:, 4, :], float(P), ps[:, 1, 0:BUCKETS],
                                                 ALU.mult, ALU.add))
                ch.link(dve.tensor_scalar(small[:, 5, :], small[:, 5, :], -1.0, None, ALU.add))
                ch.link(dve.tensor_scalar(small[:, 6, :], small[:, 3, :], -1.0, 0.0, ALU.add, ALU.max))
                dve.tensor_scalar(last_chunk[w][:, :], small[0:1, 6, :], float(P), None, ALU.mult)
                for c in range(TCOLS):
                    ch.link(dve.tensor_scalar(small[:, 7, c:c + 1], part[:, :], float(c * P), None, ALU.add))
                    ch.link(dve.tensor_scalar(small[:, 1, :], small[:, 4, :], small[:, 7, c:c + 1], 0.0, ALU.is_le,
                                              ALU.add, accum_out=small[:, 2, c:c + 1]))
                ch.link(dve.tensor_scalar(small[:, 7, 0:TCOLS], small[:, 2, 0:TCOLS], -1.0, float(P), ALU.add, ALU.mult))
                dve.tensor_copy(small_i_tiles, small[:, 7, 0:TCOLS]).then_inc(tiles_ready, 1)
                for_b = 4
                with dve.Fori(0, BUCKETS) as b:
                    ch.trip(b, for_b)
                    ch.link(dve.tensor_scalar(equal, tile_f, iota[:, ds(b, 1)], None, ALU.is_equal))
                    ch.link(dve.tensor_tensor_scan(count, ones_c, equal, small[:, 5, ds(b, 1)], ALU.mult, ALU.add))
                    ch.link(dve.tensor_tensor(match, equal, count, ALU.mult))
                    ch.link(dve.tensor_tensor(pos_f, pos_f, match, ALU.add))
                ch.leave(BUCKETS, for_b)
                dve.tensor_copy(pos[w], pos_f).then_inc(ranked, 1)

            def scatter_d(n):
                def trip(i, first):
                    for q in range(RING):
                        g = i * RING + q
                        dve.wait_ge(rec_mm, g + 1)
                        if not first:
                            dve.wait_ge(rec_out[q], 16 * PER * i)
                        dve.tensor_copy(rec[:, q, :, 0:D], ps[:, q, :].rearrange("p (k f) -> p k f", f=D))
                        dve.tensor_copy(rec[:, q, :, 2 * D:REC_D].bitcast(I32), meta_d[:, ds(g * PER, PER), :])
                        dve.wait_ge(silu_done, g + 1)
                        dve.tensor_copy(idx_ring[:, q, :], pos["d"][:, ds(g * PER, PER)]).then_inc(rec_ready, 1)
                rolled(dve, LOADS, trip)

            def scatter_s(n):
                def trip(i, first):
                    for q in range(RING):
                        g = i * RING + q
                        if not first:
                            dve.wait_ge(rec2_out[q], 16 * PER * i)
                        dve.tensor_copy(rec2[:, q, :, A64 + 2:REC_S].bitcast(I32), meta_s[:, ds(g * PER, PER), :])
                        dve.tensor_copy(q_ring[:, q, :], pos["s"][:, ds(g * PER, PER)]).then_inc(rec2_ready, 1)
                rolled(dve, LOADS, trip)

            def load_meta(n):
                dve.wait_ge(meta_loaded, 32)
                dve.tensor_copy(idx["d"][:, 0:CHUNKS], meta_in["d"][:, :, 0])
                dve.tensor_copy(q_idx[:, 0:CHUNKS], meta_in["d"][:, :, 1])
                dve.tensor_copy(node["d"][:, 0:CHUNKS], meta_in["d"][:, :, 2])
                dve.tensor_copy(idx["s"][:, 0:CHUNKS], meta_in["s"][:, :, 0])
                ch.link(dve.tensor_copy(node["s"][:, 0:CHUNKS], meta_in["s"][:, :, 1]))
                dve.nop(nofuse=True).then_inc(stage_done, 1)

            def edges(n, way, tab, l):
                w, done = src_of[way], n["edges", way]
                for q in range(RING):
                    if way == "attn":
                        dve.tensor_copy(q_ring[:, q, :], q_idx[:, q * PER:(q + 1) * PER])
                    dve.tensor_copy(idx_ring[:, q, :], idx[w][:, q * PER:(q + 1) * PER]).then_inc(idx_ready, 1)
                if way == "sum":
                    dve.tensor_scalar(T(AC), T(XT), eps1[:, l:l + 1], None, ALU.mult)
                elif way == "msg":
                    dve.tensor_copy(T(AC), T(XT))
                else:
                    dve.memset(T(AC), 0.0)
                    dve.memset(T(HT, NODES_PAD, A64 + 2 if way == "attr" else P), 0.0)
                ch.link(dve.memset(T(AC, NODES_PAD)[:, N:], 0.0))
                per = {"sum": PER, "attr": 2 * PER, "msg": PER, "attn": 2 * PER + 4}[way]
                adds = PER if way in ("sum", "msg") else 2 * PER

                def add(g, q):
                    at_ = [dve.value_load(tile_at[w][0:1, ds(g * PER + k, 1)], min_val=0, max_val=NODES_PAD - P)
                           for k in range(PER)]
                    dve.wait_ge(seg_done, n["edges"] * GROUPS + g + 1)
                    if way == "attn":
                        dve.tensor_copy(q_ring[:, q, :], q_idx[:, ds((g + RING) * PER, PER)])
                    dve.tensor_copy(idx_ring[:, q, :], idx[w][:, ds((g + RING) * PER, PER)]).then_inc(idx_ready, 1)
                    for k in range(PER):
                        c = slice(k * P, (k + 1) * P)
                        a = big[:, ds(at_[k] + AC * NODES_PAD, P)]
                        ch.mark(dve.tensor_tensor(a, a, ps[:, q, c], ALU.add))
                        if way in ("attr", "attn"):
                            r = A64 + 2 if way == "attr" else P
                            z = big[0:r, ds(at_[k] + HT * NODES_PAD, P)]
                            ch.mark(dve.tensor_tensor(z, z, ps[0:r, RING + q, c], ALU.add))
                        ch.wait()

                def trip(i, first):
                    ch.trip(i, RING * per)
                    if not first:
                        ch.k -= adds
                    for q in range(RING):
                        g = i * RING + q
                        dve.tensor_tensor(onehot[:, q, :, :], iota[:, :].unsqueeze(1).to_broadcast([P, PER, P]),
                                          node[w][:, ds(g * PER, PER)].unsqueeze(2).to_broadcast([P, PER, P]),
                                          ALU.is_equal).then_inc(onehot_ready, 1)
                        if way == "msg":
                            dve.wait_ge(gathered[way][q], 16 * PER * (done * TRIPS + i + 1))
                            dve.wait_ge(edge_in[way][q], 16 * (done * TRIPS + i + 1))
                            dve.tensor_tensor(msg_r[:, q, :, :], gath[:, q, :, :], ea_r[:, q, :, :], ALU.add)\
                               .then_inc(msg_sum, 1)
                        if way == "attn":
                            dve.wait_ge(gathered[way][q], 16 * PER * (i + 1))
                            dve.wait_ge(q_gathered[q], 16 * PER * (i + 1))
                            m = gath[:, q, :, :]
                            ch.link(dve.tensor_tensor(m, kv_r[:, q, :, 0:D], q_r[:, q, :, :], ALU.mult))
                            dve.wait_ge(edge_in[way][q], 16 * (i + 1))
                            ch.link(dve.tensor_tensor(m, m, eh_r[:, q, :, :], ALU.mult))
                            ch.link(dve.tensor_reduce(heads[:, q, :], m.rearrange("p k (h d) -> p (k h) d", d=DH),
                                                      mybir.AxisListType.X, ALU.add))
                            ch.link(dve.tensor_scalar(heads[:, q, :], heads[:, q, :], 1.0 / DH ** 0.5, -5.0,
                                                      ALU.mult, ALU.max))
                            dve.tensor_scalar(heads[:, q, :], heads[:, q, :], 5.0, None, ALU.min)\
                               .then_inc(score_ready, 1)
                            dve.wait_ge(exp_done, g + 1)
                            sc = sc_r[:, q, :, :].rearrange("p (k h) d -> p k (h d)", k=PER)
                            dve.tensor_tensor(m, kv_r[:, q, :, D:2 * D], sc, ALU.mult).then_inc(attn_ready, 1)
                        if not (first and q == 0):
                            add(g - 1, (q - 1) % RING)
                rolled(dve, TRIPS, trip)
                ch.k += adds
                ch.leave(TRIPS, RING * per)
                ch.n -= adds
                add(GROUPS - 1, RING - 1)
                dve.nop(nofuse=True).then_inc(stage_done, 1)

            def bn_finish(n, g, b):
                ch.link(dve.bn_aggr(mv[:, 0:2], stats[:, 0:NBLK * 6]))
                dve.tensor_scalar(mv[:, 1:2], mv[:, 1:2], EPS, None, ALU.add).then_inc(var_ready, 1)
                dve.wait_ge(std_ready, n["norms"] + 1)
                ch.link(dve.reciprocal(mv[:, 1:2], mv[:, 1:2]))
                ch.link(dve.tensor_tensor(scale[:, 0:1], mv[:, 1:2], feat(g), ALU.mult))
                ch.link(dve.tensor_tensor(mv[:, 0:1], mv[:, 0:1], scale[:, 0:1], ALU.mult))
                dve.tensor_tensor(shift[:, 0:1], feat(b), mv[:, 0:1], ALU.subtract).then_inc(stage_done, 1)

            def linear(n, terms, func, bias, dst, g, b):
                if g is None:
                    return
                with dve.Fori(0, NBLK) as j:
                    dve.wait_ge(mm_free, n["blocks"] * NBLK + j + 1)
                    ch.trip(j, 1)
                    ch.mark(dve.bn_stats(stats[:, ds(j * 6, 6)],
                                         T(dst)[:, ds(j * BLK, BLK)]))
                ch.leave(NBLK, 1)
                ch.wait()
                bn_finish(n, g, b)

            def norm_apply(n, src, dst, func, then):
                if then is None:
                    return
                with dve.Fori(0, NBLK) as j:
                    dve.wait_ge(act_blk, n["norm_apply"] * NBLK + j + 1)
                    ch.trip(j, 1)
                    d = T(dst)[:, ds(j * BLK, BLK)]
                    if then == "residual":
                        x = T(XT)[:, ds(j * BLK, BLK)]
                        ch.mark(dve.tensor_tensor(x, x, d, ALU.add))
                    else:
                        ch.mark(dve.bn_stats(stats[:, ds(j * 6, 6)], d))
                ch.leave(NBLK, 1)
                ch.wait()
                if then == "residual":
                    dve.nop(nofuse=True).then_inc(stage_done, 1)
                else:
                    bn_finish(n, *then)

            def linear_nat(n, terms, w, bias, dst, plus):
                base = n["blocks"] * NBLK
                with dve.Fori(0, SWEEPS) as i:
                    ch.trip(i, SLOTS_PS if plus else 0)
                    for s in range(SLOTS_PS):
                        dve.wait_ge(mm_full, base + SLOTS_PS * i + s + 1)
                        d = big[0:NT, ds(dst * NODES_PAD + s * 2 * w + i * (SLOTS_PS * 2 * w), 2 * w)]
                        p_ = ps[0:NT, s, 0:2 * w]
                        if bias is None:
                            ins = dve.tensor_copy(d, p_)
                        elif plus:
                            ch.link(dve.tensor_tensor(d, d, p_, ALU.add))
                            d2 = d.rearrange("p (t w) -> p t w", w=w)
                            ins = dve.tensor_tensor(d2, d2, row(bias, w).unsqueeze(1).to_broadcast([NT, 2, w]), ALU.add)
                        else:
                            ins = dve.tensor_tensor(d.rearrange("p (t w) -> p t w", w=w),
                                                    p_.rearrange("p (t w) -> p t w", w=w),
                                                    row(bias, w).unsqueeze(1).to_broadcast([NT, 2, w]), ALU.add)
                        ins.then_inc(mm_free, 1)
                ch.leave(SWEEPS, SLOTS_PS if plus else 0)
                dve.wait_ge(mm_free, base + NBLK)
                dve.nop(nofuse=True).then_inc(stage_done, 1)

            def layer_norm(n, b, w, g, h, relu):
                with dve.Fori(0, NTILES) as t:
                    ch.trip(t, 1)
                    ch.mark(dve.bn_stats(stats[0:NT, ds(t * 6, 6)],
                                         big[0:NT, ds(b * NODES_PAD + t * w, w)]))
                ch.leave(NTILES, 1)
                ch.wait()
                me, mo, se, so = (st3[:, :, k] for k in (1, 4, 2, 5))
                tot, dif, sq = (mv3[0:NT, :, k] for k in range(3))
                ch.mark(dve.tensor_tensor(tot, me, mo, ALU.add))
                ch.mark(dve.tensor_tensor(dif, me, mo, ALU.subtract))
                ch.link(dve.tensor_tensor(sq, se, so, ALU.add))
                ch.mark(dve.tensor_scalar(sq, sq, 1.0 / w, None, ALU.mult))
                ch.link(dve.scalar_tensor_tensor(dif, dif, 0.25, dif, ALU.mult, ALU.mult))
                ch.link(dve.tensor_tensor(sq, sq, dif, ALU.add))
                dve.tensor_scalar(sq, sq, EPS, None, ALU.add).then_inc(var_ready, 1)
                dve.wait_ge(std_ready, n["norms"] + 1)
                ch.link(dve.reciprocal(scale[0:NT, :], sq))
                dve.scalar_tensor_tensor(shift[0:NT, :], tot, -0.5, scale[0:NT, :], ALU.mult, ALU.mult)\
                   .then_inc(stat_ready, 1)
                k = NTILES // 5
                for i in range(5):
                    dve.wait_ge(ln_part, 5 * n["layer_norm"] + i + 1)
                    if g is None:
                        continue
                    x = nat(b, w)[:, i * k:(i + 1) * k, :]
                    ch.link(dve.tensor_tensor(x, x, row(g, w).unsqueeze(1).to_broadcast([NT, k, w]), ALU.mult))
                    ch.link(dve.tensor_tensor(x, x, row(h, w).unsqueeze(1).to_broadcast([NT, k, w]), ALU.add))
                    if relu:
                        ch.link(dve.tensor_scalar(x, x, 0.0, None, ALU.max))
                dve.nop(nofuse=True).then_inc(stage_done, 1)

            def add_(n, a, b):
                dve.tensor_tensor(nat(a), nat(a), nat(b), ALU.add).then_inc(stage_done, 1)

            def copy(n, a, b):
                dve.tensor_copy(nat(a), nat(b)).then_inc(stage_done, 1)

            def attend(n):
                ch.link(dve.tensor_scalar(T(HT), T(HT), ATTN_EPS, None, ALU.add))
                ch.link(dve.reciprocal(T(HT), T(HT)))
                ch.link(dve.tensor_tensor(T(AC), T(AC), T(HT), ALU.mult))
                ch.link(dve.tensor_tensor(T(AC), T(AC), T(XT), ALU.add))
                with dve.Fori(0, NBLK) as j:
                    ch.trip(j, 1)
                    ch.mark(dve.bn_stats(stats[:, ds(j * 6, 6)],
                                         T(AC)[:, ds(j * BLK, BLK)]))
                ch.leave(NBLK, 1)
                ch.wait()
                bn_finish(n, "bn_g", "bn_b")

            walk(dve, setup=setup, rank=rank, scatter_d=scatter_d, scatter_s=scatter_s, load_meta=load_meta,
                 edges=edges, linear=linear, norm_apply=norm_apply, linear_nat=linear_nat,
                 layer_norm=layer_norm, add=add_, copy=copy, attend=attend)


def kernel(**inputs):
    import concourse.bacc as bacc
    from concourse.bass_utils import run_bass_kernel_spmd

    g = {k: np.asarray(v) for k, v in inputs.items()}

    def columns(w):
        return np.concatenate(list(w), axis=1)

    def padded(a, fill):
        full = np.full(E_PAD, fill, a.dtype)
        full[:E] = a
        return np.ascontiguousarray(full.reshape(COLS, P).T)

    def rows_padded(a):
        full = np.zeros((E_PAD, a.shape[1]), a.dtype)
        full[:E] = a
        return full

    l0, l1, l2, l3 = ({k[len(p):]: v for k, v in g.items() if k.startswith(p)}
                      for p in ("L0_gnn_", "L1_gnn_", "L2_gnn_", "L3_gnn_"))
    src, dst = g["src"], g["dst"]
    if src.dtype != np.int32:
        src, dst = src.astype(np.int32), dst.astype(np.int32)
    attr16 = np.zeros((A16 + 1, E_PAD), np.float32)
    attr16[:A16, :E] = g["edge_attr_16"].T
    attr16[A16] = 1.0
    arrays = {
        "x": np.ascontiguousarray(g["x"]),
        "x_t": np.ascontiguousarray(g["x"].T),
        "dst_key": padded(dst, TILES * P), "src_key": padded(src, TILES * P),
        "src_val": padded(src, 0), "dst_val": padded(dst, 0),
        "attr128_t": np.ascontiguousarray(rows_padded(g["edge_attr_128"]).T),
        "attr16_t": attr16,
        "attr64": rows_padded(g["edge_attr_64"]),
        "weights": np.concatenate([
            columns(l0["W1"]), columns(l0["W2"]), columns(l2["W1"]), columns(l2["W2"]), l0["fp_W1"],
            l0["fp_W2"][:D], l0["fp_W2"][D:], l1["W_S_w"].T, l1["W_T_w"].T, l3["WE"], l3["WK"], l3["WV"],
            l3["WQ"]], axis=1),
        "rows": np.concatenate([np.ravel(a) for a in (
            l0["ln_g"], l0["ln_b"], l0["fp_b1"], l0["fp_ln1_g"], l0["fp_ln1_b"], l0["fp_b2"], l0["fp_ln2_g"],
            l0["fp_ln2_b"], l2["b2"], l2["gamma"], l2["beta"], l0["eps"])]),
        "feats": np.ascontiguousarray(np.concatenate([
            l0["b1"], l0["bn1_g"], l0["bn1_b"], l0["b2"], l0["bn2_g"], l0["bn2_b"], l0["obn_g"], l0["obn_b"],
            l2["b1"], l1["W_S_b"][None], l3["bn_gamma"][None], l3["bn_beta"][None]]).T),
        "attr_w": np.concatenate([l1["T_w"].T, l1["T_b"][None], l1["W_T_b"][None]]),
        "ea_w": np.concatenate([l2["We"], l2["be"][None]]),
    }
    nc = bacc.Bacc("TRN2", target_bir_lowering=False, num_devices=1)
    A = {k: nc.dram_tensor(f"in_{k}", v.shape, mybir.dt.from_np(v.dtype), kind="ExternalInput").ap()
         for k, v in arrays.items()}
    A["out"] = nc.dram_tensor("out", (N, D), F32, kind="ExternalOutput").ap()
    program(nc, A)
    r = run_bass_kernel_spmd(nc, [{f"in_{k}": np.ascontiguousarray(v) for k, v in arrays.items()}], core_ids=[0])
    return r.results[0]["out"]
```

```python
from contextlib import ExitStack

import numpy as np
import concourse.bass as bass
from concourse import mybir

F32, I32 = mybir.dt.float32, mybir.dt.int32
ALU, ACT = mybir.AluOpType, mybir.ActivationFunctionType
ds = bass.ds

N, E, D = 6250, 106250, 128
P = 128
LAYERS = 4
HEADS = 8
DH = D // HEADS
A16, A64 = 16, 64
EPS = 1e-5
ATTN_EPS = 1e-6

TILES = -(-N // P)
BUCKETS = TILES + 1
NODES_PAD = BUCKETS * P
PER = 4
RING = 4
COLS = -(-E // (P * PER * RING)) * PER * RING
E_PAD = COLS * P
CHUNKS = (E + TILES * (P - 1)) // P + -(-(E_PAD - E) // P)
CHUNKS = -(-CHUNKS // (PER * RING)) * PER * RING
SLOTS = CHUNKS * P
LOOK = PER * RING
TCOLS = -(-CHUNKS // P)
GROUPS = CHUNKS // PER
TRIPS = GROUPS // RING
LOADS = COLS // PER // RING
TAIL = CHUNKS - COLS + PER

NT = 125
NTILES = N // NT
BLK = 2 * NT
NBLK = N // BLK
SLOTS_PS = 5
SWEEPS = NBLK // SLOTS_PS

REC_D = D + D + 2
REC_S = A64 + 2 + 2
PARTS = (8, 8, 8)
XT, HT, AC, NA, RE = range(5)


def weight_columns():
    at, where = 0, {}
    for name, width in (("w1", LAYERS * D), ("w2", LAYERS * D), ("v1", LAYERS * D), ("v2", LAYERS * D),
                        ("f1", 2 * D), ("f2", 2 * D), ("ws", D), ("wt", D), ("we", D), ("kv", 2 * D), ("q", D)):
        where[name] = at
        at += width
    return where, at


def row_columns():
    at, where = 0, {}
    for name, width in (("ln_g", D), ("ln_b", D), ("f_b1", 2 * D), ("f_g1", 2 * D), ("f_h1", 2 * D),
                        ("f_b2", D), ("f_g2", D), ("f_h2", D), ("v_b2", LAYERS * D), ("gamma", LAYERS * D),
                        ("beta", LAYERS * D), ("eps", LAYERS)):
        where[name] = at
        at += width
    return where, at


def feature_columns():
    names = [f"{n}{l}" for n in ("b1", "bn1_g", "bn1_b", "b2", "bn2_g", "bn2_b", "obn_g", "obn_b", "v_b1")
             for l in range(LAYERS)] + ["s_b", "bn_g", "bn_b"]
    return {n: i for i, n in enumerate(names)}, len(names)


W_AT, W_N = weight_columns()
R_AT, R_N = row_columns()
C_AT, C_N = feature_columns()


def network(do):
    do("setup")
    do("rank", "d")
    do("scatter_d")
    do("load_meta", "d")
    for l in range(LAYERS):
        act = ACT.Identity if l == LAYERS - 1 else ACT.Relu
        do("edges", "sum", "x" if l == 0 else "xg", l)
        do("linear", [(("w1", l), AC)], ACT.Identity, f"b1{l}", HT, f"bn1_g{l}", f"bn1_b{l}")
        do("norm_linear", HT, AC, ("w2", l), f"b2{l}", f"bn2_g{l}", f"bn2_b{l}")
        do("norm_apply", HT, AC, act, (f"obn_g{l}", f"obn_b{l}"))
        do("norm_out", AC, HT, act, "xg" if l < LAYERS - 1 else None)
    do("layer_norm", NA, D, ("ln_g", 0), ("ln_b", 0), False, AC, None, False)
    do("linear_nat", [(AC, "f1", 0)], 2 * D, "f_b1", XT)
    do("layer_norm", XT, 2 * D, ("f_g1", 0), ("f_h1", 0), True, None, None, False)
    do("to_t", XT, 2 * D, 0, AC)
    do("to_t", XT, 2 * D, D, RE)
    do("linear_nat", [(AC, "f2", 0), (RE, "f2", D)], D, "f_b2", NA)
    do("load_x", RE)
    do("layer_norm", NA, D, ("f_g2", 0), ("f_h2", 0), True, None, None, False)
    do("add", NA, RE)
    do("layer_norm", NA, D, None, None, False, XT, "xg", False)
    do("load_meta", "s")
    do("edges", "attr", "xg", 0)
    do("linear", [(("ws", 0), XT), (("wt", 0), AC), ("attr", HT)], ACT.Relu, "s_b", AC, None, None)
    do("to_nat", AC, RE)
    do("add", RE, NA)
    do("layer_norm", RE, D, None, None, False, XT, "xg", False)
    do("copy", NA, RE)
    for l in range(LAYERS):
        do("edges", "msg", "xg", l)
        do("conv", l)
        do("layer_norm", NA, D, ("gamma", l), ("beta", l), False, XT if l < LAYERS - 1 else None,
           "xg" if l < LAYERS - 1 else None, True)
    do("add", NA, RE)
    do("layer_norm", NA, D, None, None, False, XT, None, False)
    do("linear_nat", [(XT, "kv", 0)], 2 * D, None, AC)
    do("store", AC, "kv", 2 * D)
    do("q_tiles", XT, RE)
    do("edges", "attn", "kv", 0)
    do("attend")
    do("norm_out", AC, HT, ACT.Identity, None)
    do("layer_norm", NA, D, None, None, False, None, "out", False)


def rolled(eng, count, body):
    body(0, True)
    if count > 1:
        with eng.Fori(1, count) as i:
            body(i, False)


class Chain:

    def __init__(self, eng, sem):
        self.eng, self.sem, self.n, self.base, self.k = eng, sem, 0, None, 0

    def mark(self, ins):
        ins.then_inc(self.sem, 1)
        if self.base is None:
            self.n += 1
        else:
            self.k += 1

    def wait(self):
        self.eng.wait_ge(self.sem, self.n if self.base is None else self.base + self.k)

    def link(self, ins):
        self.mark(ins)
        self.wait()

    def trip(self, i, per):
        self.base, self.k = self.n + i * per, 0

    def leave(self, trips, per):
        assert self.k == per, (self.k, per)
        self.n, self.base = self.n + trips * per, None


def program(nc, A):
    ctx = ExitStack()
    with ctx:
        def sb(name, shape, dt=F32):
            return ctx.enter_context(nc.sbuf_tensor(name, shape, dt))

        def sem(name):
            return ctx.enter_context(nc.semaphore(name))

        rec_d = nc.dram_tensor("rec_d", [SLOTS, REC_D], F32).ap()
        rec_s = nc.dram_tensor("rec_s", [SLOTS, REC_S], F32).ap()
        tile_row = {w: nc.dram_tensor(f"tile_row_{w}", [TCOLS, P], I32).ap() for w in "ds"}
        table = {"x": A["x"], "out": A["out"],
                 "xg": nc.dram_tensor("x_table", [N, D], F32).ap(),
                 "kv": nc.dram_tensor("kv_table", [N, 2 * D], F32).ap()}

        big = sb("big", [P, 5 * NODES_PAD])
        weights = sb("weights", [P, W_N])
        rows = sb("rows", [P, R_N])
        feats = sb("feats", [P, C_N])
        attr_w = sb("attr_w", [A64 + 2, D])
        ea_w = sb("ea_w", [A16 + 1, D])
        idx = {w: sb(f"idx_{w}", [P, CHUNKS + LOOK], I32) for w in "ds"}
        node = {w: sb(f"node_{w}", [P, CHUNKS + LOOK]) for w in "ds"}
        tile_at = {w: sb(f"tile_at_{w}", [1, PER + TCOLS * P], I32) for w in "ds"}
        last_chunk = {w: sb(f"last_chunk_{w}", [1, BUCKETS], I32) for w in "ds"}
        gath = sb("gath", [P, RING, PER, D])
        onehot = sb("onehot", [P, RING, PER, P])
        idx_ring = sb("idx_ring", [P, RING, PER], I32)
        q_ring = sb("q_ring", [P, RING, PER], I32)
        heads = sb("heads", [P, RING, PER * HEADS])
        iota = sb("iota", [P, P])
        part = sb("part", [P, 1])
        ident = sb("ident", [P, P])
        stats = sb("stats", [P, NTILES * 6])
        st3 = stats[0:NT, :].rearrange("p (t s) -> p t s", s=6)
        mv = sb("mv", [P, NTILES * 3])
        mv3 = mv[:, :].rearrange("p (t s) -> p t s", s=3)
        scale = sb("scale", [P, NTILES])
        shift = sb("shift", [P, NTILES])
        eps1 = sb("eps1", [P, LAYERS])
        small_i = sb("small_i", [P, 2, BUCKETS], I32)
        ps = ctx.enter_context(nc.psum_tensor("ps", [P, 8, 512], F32))

        before = onehot[:, 0, 0, :]
        ones = onehot[:, 0, 1, :]
        small = onehot[:, 1, :, :].rearrange("p k e -> p (k e)")[:, 0:8 * BUCKETS]\
            .rearrange("p (a b) -> p a b", b=BUCKETS)
        small_i_tiles = small_i[:, 0, 0:TCOLS]

        def T(b, n=N, rows_=P):
            return big[0:rows_, b * NODES_PAD:b * NODES_PAD + n]

        def nat(b, w=D):
            return big[0:NT, b * NODES_PAD:b * NODES_PAD + NTILES * w].rearrange("p (t w) -> p t w", w=w)

        def weight(name, off=0, width=D):
            return weights[:, W_AT[name] + off:W_AT[name] + off + width]

        def row(name, width=D):
            name, l = name if isinstance(name, tuple) else (name, 0)
            at = R_AT[name] + l * D
            return rows[0:NT, at:at + width]

        def feat(name):
            return feats[:, C_AT[name]:C_AT[name] + 1]

        at = [0]

        def part_of_big(shape, start=None):
            if start is not None:
                at[0] = start
            n = int(np.prod(shape[1:]))
            v = big[0:shape[0], at[0]:at[0] + n]
            at[0] += n
            assert at[0] <= 5 * NODES_PAD
            if len(shape) == 4:
                v = v.rearrange("p (a b c) -> p a b c", a=shape[1], b=shape[2])
            elif len(shape) == 3:
                v = v.rearrange("p (a b) -> p a b", a=shape[1])
            return v

        meta_d = part_of_big([P, COLS, 2], HT * NODES_PAD).bitcast(I32)
        pos_d = part_of_big([P, COLS]).bitcast(I32)
        key = {w: part_of_big([P, COLS]).bitcast(I32) for w in "ds"}
        val = {w: part_of_big([P, COLS]).bitcast(I32) for w in "ds"}
        tile_i = part_of_big([P, COLS]).bitcast(I32)
        tile_f = part_of_big([P, COLS])
        equal = part_of_big([P, COLS])
        count = part_of_big([P, COLS])
        match = part_of_big([P, COLS])
        pos_f = part_of_big([P, COLS])
        ones_c = part_of_big([P, COLS])
        rec = part_of_big([P, RING, PER, REC_D])
        attr_t = part_of_big([P, RING, PER * P])
        a16_t = gath[0:A16 + 1, :, :, :].rearrange("p r k e -> p r (k e)")
        blank = part_of_big([P, REC_D], RE * NODES_PAD)
        blank_s = part_of_big([P, REC_S])
        meta_in = {"d": part_of_big([P, CHUNKS, 2], NA * NODES_PAD).bitcast(I32),
                   "s": part_of_big([P, CHUNKS, 2], HT * NODES_PAD).bitcast(I32)}
        attr_r = part_of_big([P, RING, PER, A64 + 2], RE * NODES_PAD)
        ea_r = part_of_big([P, RING, PER, D], HT * NODES_PAD)
        msg_r = part_of_big([P, RING, PER, D])
        kv_r = part_of_big([P, RING, PER, 2 * D], NA * NODES_PAD)
        eh_r = part_of_big([P, RING, PER, D])
        spare = sb("spare", [P, COLS * 3 + RING * PER * REC_S])
        meta_s = spare[:, 0:2 * COLS].rearrange("p (c m) -> p c m", m=2).bitcast(I32)
        pos_s = spare[:, 2 * COLS:3 * COLS].bitcast(I32)
        rec2 = spare[:, 3 * COLS:].rearrange("p (r k w) -> p r k w", r=RING, k=PER)
        sc_r = spare[:, 0:RING * PER * D].rearrange("p (r h d) -> p r h d", r=RING, d=DH)
        oht_r = spare[:, RING * PER * D:RING * PER * D + 2 * PER * P].rearrange("p (r k e) -> p r k e", r=2, k=PER)
        pos = {"d": pos_d, "s": pos_s}

        stage_done = sem("stage_done")
        loaded = sem("loaded")
        consts = sem("consts")
        pool_step = sem("pool_step")
        dve_chain, act_chain = sem("dve_chain"), sem("act_chain")
        totals_ready = sem("totals_ready")
        sums_ready = sem("sums_ready")
        tiles_ready = sem("tiles_ready")
        ranked = sem("ranked")
        moved = sem("moved")
        blank_s_done = sem("blank_s_done")
        blanked = sem("blanked")
        att_in = [sem(f"att_in{q}") for q in range(RING)]
        att2_in = [sem(f"att2_in{q}") for q in range(RING)]
        rec_mm, silu_done, rec_ready = sem("rec_mm"), sem("silu_done"), sem("rec_ready")
        rec2_ready = sem("rec2_ready")
        rec_out = [sem(f"rec_out{q}") for q in range(RING)]
        rec2_out = [sem(f"rec2_out{q}") for q in range(RING)]
        meta_loaded = sem("meta_loaded")
        idx_ready = sem("idx_ready")
        onehot_ready = sem("onehot_ready")
        msg_sum, msg_ready = sem("msg_sum"), sem("msg_ready")
        attn_ready, score_ready, exp_done = sem("attn_ready"), sem("score_ready"), sem("exp_done")
        seg_done = sem("seg_done")
        gathered = {k: [sem(f"gathered_{k}{q}") for q in range(RING)] for k in ("sum", "attr", "msg", "attn")}
        turned, turned_in, q_rows = sem("turned"), sem("turned_in"), sem("q_rows")
        pads_zero = sem("pads_zero")
        hidden_full, hidden_free = sem("hidden_full"), sem("hidden_free")
        added = sem("added")
        ln_fifth = sem("ln_fifth")
        edge_in = {k: [sem(f"edge_in_{k}{q}") for q in range(RING)] for k in ("attr", "msg", "attn")}
        mm_full, mm_free = sem("mm_full"), sem("mm_free")
        act_blk = sem("act_blk")
        var_ready, std_ready = sem("var_ready"), sem("std_ready")
        stat_ready = sem("stat_ready")
        ln_part = sem("ln_part")
        io_done = sem("io_done")
        fifth_stored = sem("fifth_stored")

        block = ctx.enter_context(nc.Block())

        def walk(eng, **mine):
            seen = {}
            stage = [0]

            def do(kind, *args):
                names = [kind, (kind, args[0])] if kind == "edges" else [kind]
                if kind in ("linear", "to_nat", "to_t", "linear_nat", "norm_linear", "norm_out", "conv", "q_tiles") \
                        or (kind == "layer_norm" and args[5] is not None):
                    names.append("blocks")
                if kind == "layer_norm" and args[2] is not None:
                    names.append("scaled")
                if kind in ("norm_linear", "norm_out", "norm_apply"):
                    names.append("applied")
                if kind in ("store", "load_x"):
                    names.append("io")
                if kind == "norm_out" and args[3] or kind == "layer_norm" and args[6]:
                    names.append("io_fifths")
                if kind in ("layer_norm", "attend", "norm_linear", "norm_apply") \
                        or (kind == "linear" and args[4] is not None):
                    names.append("norms")
                n = {x: seen.get(x, 0) for x in names}
                if kind in mine:
                    if stage[0]:
                        eng.wait_ge(stage_done, stage[0])
                    mine[kind](n, *args)
                stage[0] += 1
                for x in names:
                    seen[x] = seen.get(x, 0) + 1

            network(do)
            return stage[0]

        HIDDEN_PS = 8 - SLOTS_PS

        def hid(j):
            return ps[:, SLOTS_PS + j % HIDDEN_PS, 0:BLK]

        def onehots_before(n):
            return n["edges"] * GROUPS

        src_of = {"sum": "d", "attr": "s", "msg": "d", "attn": "d"}

        @block.sync
        def _(sp):
            rd = rec_d.rearrange("(c p) w -> p c w", p=P)
            rs = rec_s.rearrange("(c p) w -> p c w", p=P)

            def setup(n):
                for dst, src in ((T(XT), A["x_t"]), (weights[:, :], A["weights"]), (feats[:, :], A["feats"]),
                                 (rows[:, :], A["rows"].partition_broadcast(P)),
                                 (attr_w[:, :], A["attr_w"]), (ea_w[:, :], A["ea_w"]),
                                 (key["d"], A["dst_key"]), (key["s"], A["src_key"]),
                                 (val["d"], A["src_val"]), (val["s"], A["dst_val"])):
                    sp.dma_start(dst, src).then_inc(loaded, 16)

            def prepare(w):
                k = "ds".index(w)
                sp.wait_ge(tiles_ready, k + 1)
                with nc.allow_non_contiguous_dma(reason="a few hundred values"):
                    sp.dma_start(tile_row[w].rearrange("k p -> p k"), small_i_tiles).then_inc(moved, 16)
                sp.wait_ge(moved, 32 * k + 16)
                sp.dma_start(tile_at[w][:, PER:], tile_row[w].rearrange("k p -> (k p)").unsqueeze(0)).then_inc(moved, 16)
                sp.wait_ge(moved, 32 * k + 32)
                r, b = (rec_d, blank) if w == "d" else (rec_s, blank_s)
                tail = (rd if w == "d" else rs)[:, CHUNKS - TAIL:CHUNKS, :]
                sp.dma_start(tail, b.unsqueeze(1).to_broadcast([P, TAIL, b.shape[1]])).then_inc(blanked, 16)
                with sp.Fori(0, BUCKETS) as i:
                    c = sp.value_load(last_chunk[w][0:1, ds(i, 1)], min_val=0, max_val=SLOTS - P)
                    sp.wait_ge(blanked, 16 * (BUCKETS + 1) * k + 16 * i + 16)
                    sp.dma_start(r[ds(c, P), :], b).then_inc(blanked, 16)
                sp.wait_ge(blanked, 16 * (BUCKETS + 1) * (k + 1))

            def rank(n, w):
                prepare(w)
                sp.wait_ge(ranked, 1)
                sp.nop(nofuse=True).then_inc(stage_done, 1)

            def scatter_d(n):
                def trip(i, first):
                    for q in range(RING):
                        if not first:
                            sp.wait_ge(rec_ready, RING * i + q - RING + 1)
                        cols = ds((i * RING + q) * PER * P, PER * P)
                        sp.dma_start(attr_t[:, q, :], A["attr128_t"][:, cols]).then_inc(att_in[q], 16)
                        sp.dma_start(a16_t[:, q, :], A["attr16_t"][:, cols]).then_inc(att_in[q], 16)
                rolled(sp, LOADS, trip)
                for q in range(RING):
                    sp.wait_ge(rec_out[q], 16 * PER * LOADS)
                sp.wait_ge(ranked, 2)
                sp.nop(nofuse=True).then_inc(stage_done, 1)

            def load_attr64():
                a64 = A["attr64"].rearrange("(c p) w -> p c w", p=P)

                def trip(i, first):
                    for q in range(RING):
                        if not first:
                            sp.wait_ge(rec2_out[q], 16 * PER * i)
                        sp.dma_start(rec2[:, q, :, 0:A64], a64[:, ds((i * RING + q) * PER, PER), :])\
                          .then_inc(att2_in[q], 16)
                rolled(sp, LOADS, trip)

            def load_meta(n, w):
                if w == "d":
                    src = rd[:, :, 2 * D:REC_D]
                else:
                    for q in range(RING):
                        sp.wait_ge(rec2_out[q], 16 * PER * LOADS)
                    src = rs[:, :, A64 + 2:REC_S]
                sp.dma_start(meta_in[w], src.bitcast(I32)).then_inc(meta_loaded, 16)

            def edges(n, way, tab, l):
                if way == "sum":
                    if l == 0:
                        prepare("s")
                        sp.nop(nofuse=True).then_inc(blank_s_done, 1)
                        load_attr64()
                    return
                ring, src = {"attr": (attr_r, rs[:, :, 0:A64 + 2]), "msg": (ea_r, rd[:, :, D:2 * D]),
                             "attn": (eh_r, rd[:, :, 0:D])}[way]
                base, done = n["edges"] * (GROUPS + RING), n["edges", way]
                with sp.Fori(0, TRIPS) as i:
                    for q in range(RING):
                        sp.wait_ge(idx_ready, base + RING * i + q + 1)
                        sp.dma_start(ring[:, q, :, :], src[:, ds((i * RING + q) * PER, PER), :])\
                          .then_inc(edge_in[way][q], 16)

            total = walk(sp, setup=setup, rank=rank, scatter_d=scatter_d, load_meta=load_meta, edges=edges)
            sp.wait_ge(stage_done, total)

        @block.gpsimd
        def _(pool):
            def setup(n):
                pool.iota(iota[:, :], [[1, P]], base=0, channel_multiplier=0,
                          allow_small_or_imprecise_dtypes=True).then_inc(consts, 1)
                pool.iota(part[:, :], [[0, 1]], base=0, channel_multiplier=1,
                          allow_small_or_imprecise_dtypes=True).then_inc(consts, 1)
                pool.memset(ident[:, :], 0.0).then_inc(pool_step, 1)
                pool.memset(before, 1.0).then_inc(pool_step, 1)
                pool.memset(ones, 1.0).then_inc(consts, 1)
                pool.wait_ge(pool_step, 2)
                pool.affine_select(out=ident[:, :], in_=ident[:, :], compare_op=ALU.not_equal, fill=1.0, base=0,
                                   pattern=[[-1, P]], channel_multiplier=1).then_inc(consts, 1)
                pool.affine_select(out=before, in_=before, compare_op=ALU.is_gt, fill=0.0, base=0,
                                   pattern=[[1, P]], channel_multiplier=-1).then_inc(consts, 1)

            def scatter_d(n):
                def trip(i, first):
                    for q in range(RING):
                        pool.wait_ge(rec_ready, RING * i + q + 1)
                        pool.nop(nofuse=True)
                        for k in range(PER):
                            pool.indirect_dma_start(
                                rec_d, bass.IndirectOffsetOnAxis(ap=idx_ring[:, q, k:k + 1], axis=0),
                                rec[:, q, k, :], None).then_inc(rec_out[q], 16)
                rolled(pool, LOADS, trip)

            def scatter_s(start, trips):
                def trip(i, first):
                    for q in range(RING):
                        g = RING * i + q
                        if not first:
                            pool.wait_ge(rec2_out[q], 16 * PER * i)
                            pool.nop(nofuse=True)
                        pool.tensor_copy(rec2[:, q, :, A64 + 2:REC_S].bitcast(I32), meta_s[:, ds(g * PER, PER), :])
                        pool.tensor_copy(q_ring[:, q, :], pos_s[:, ds(g * PER, PER)]).then_inc(pool_step, 1)
                        pool.wait_ge(pool_step, 2 + g + 1)
                        pool.wait_ge(att2_in[q], 16 * (i + 1))
                        pool.nop(nofuse=True)
                        for k in range(PER):
                            pool.indirect_dma_start(
                                rec_s, bass.IndirectOffsetOnAxis(ap=q_ring[:, q, k:k + 1], axis=0),
                                rec2[:, q, k, :], None).then_inc(rec2_out[q], 16)
                if start == 0:
                    pool.wait_ge(blank_s_done, 1)
                    trip(0, True)
                with pool.Fori(max(start, 1), start + trips) as i:
                    trip(i, False)

            def edges(n, way, tab, l):
                base = n["edges"] * (GROUPS + RING)
                ring = kv_r if way == "attn" else gath
                with pool.Fori(0, TRIPS) as i:
                    for q in range(RING):
                        pool.wait_ge(idx_ready, base + RING * i + q + 1)
                        pool.nop(nofuse=True)
                        for k in range(PER):
                            pool.indirect_dma_start(
                                ring[:, q, k, :], None, table[tab],
                                bass.IndirectOffsetOnAxis(ap=idx_ring[:, q, k:k + 1], axis=0))\
                                .then_inc(gathered[way][q], 16)
                if way == "sum":
                    start = sum(PARTS[:l])
                    scatter_s(start, PARTS[l] if l < LAYERS - 1 else LOADS - start)

            walk(pool, setup=setup, scatter_d=scatter_d, edges=edges)

        @block.tensor
        def _(pe):
            def rank(n, w):
                pe.wait_ge(totals_ready, "ds".index(w) + 1)
                pe.matmul(ps[:, 6, 0:BUCKETS], ones, small[:, 0, :], start=True, stop=True)
                pe.matmul(ps[:, 7, 0:BUCKETS], before, small[:, 0, :], start=True, stop=True)\
                  .then_inc(sums_ready, 1)

            def scatter_d(n):
                def trip(i, first):
                    for q in range(RING):
                        pe.wait_ge(att_in[q], 32 * i + 32)
                        if not first or q >= 2:
                            pe.wait_ge(rec_ready, RING * i + q - 1)
                        for k in range(PER):
                            c = slice(k * P, (k + 1) * P)
                            pe.matmul(ps[:, q % 2, c], attr_t[:, q, c], weight("we"), start=True, stop=True)
                            last = pe.matmul(ps[:, 2 + q % 2, c], a16_t[:, q, c], ea_w[:, :], start=True, stop=True)
                        last.then_inc(rec_mm, 1)
                trip(0, True)
                with pe.Fori(1, 4) as i:
                    trip(i, False)
                rank(n, "s")
                with pe.Fori(4, LOADS) as i:
                    trip(i, False)

            def edges_attn():
                with_tiles = lambda start: nc.values_load_multi_w_load_instructions(
                    tile_at["d"][0:1, ds(start, RING * PER)], engines=[mybir.EngineType.PE],
                    min_val=0, max_val=NODES_PAD - P)[1]

                def q_of(g, q, at_, base):
                    pe.wait_ge(onehot_ready, base + g + 1)
                    for k in range(PER):
                        last = pe.transpose(ps[:, 4 + q % 2, k * P:(k + 1) * P], onehot[:, q, k, :], ident[:, :])
                    last.then_inc(turned, 1)
                    pe.wait_ge(turned_in, g + 1)
                    for k in range(PER):
                        last = pe.matmul(ps[:, 6 + q % 2, k * P:(k + 1) * P], oht_r[:, q % 2, k, :],
                                         big[:, ds(at_[k] + RE * NODES_PAD, P)], start=True, stop=True)
                    last.then_inc(q_rows, 1)
                return with_tiles, q_of

            def edges(n, way, tab, l):
                base, done = onehots_before(n), n["edges", way]
                if way == "attn":
                    with_tiles, q_of = edges_attn()
                    q_of(0, 0, with_tiles(PER), base)
                    with pe.Fori(0, TRIPS) as i:
                        at_ = with_tiles(i * RING * PER + 2 * PER)
                        for q in range(RING):
                            g = i * RING + q
                            q_of(g + 1, (q + 1) % RING, at_[q * PER:(q + 1) * PER], base)
                            pe.wait_ge(attn_ready, g + 1)
                            for k in range(PER):
                                at2 = 2 * (q % 2) + k // 2
                                c = (k % 2) * 2 * P
                                sc = sc_r[:, q, k * HEADS:(k + 1) * HEADS, :].rearrange("p h d -> p (h d)")
                                pe.matmul(ps[:, at2, c:c + P], sc, onehot[:, q, k, :], start=True, stop=True)
                                last = pe.matmul(ps[:, at2, c + P:c + 2 * P], gath[:, q, k, :], onehot[:, q, k, :],
                                                 start=True, stop=True)
                            last.then_inc(seg_done, 1)
                    return
                with pe.Fori(0, TRIPS) as i:
                    for q in range(RING):
                        pe.wait_ge(onehot_ready, base + RING * i + q + 1)
                        if way in ("sum", "attr"):
                            pe.wait_ge(gathered[way][q], 16 * PER * (done * TRIPS + i + 1))
                        if way == "attr":
                            pe.wait_ge(edge_in[way][q], 16 * (done * TRIPS + i + 1))
                        if way == "msg":
                            pe.wait_ge(msg_ready, done * GROUPS + RING * i + q + 1)
                        src = msg_r if way == "msg" else gath
                        for k in range(PER):
                            c = slice(k * P, (k + 1) * P)
                            last = pe.matmul(ps[:, q, c], src[:, q, k, :], onehot[:, q, k, :], start=True, stop=True)
                            if way == "attr":
                                last = pe.matmul(ps[0:A64 + 2, RING + q, c], attr_r[:, q, k, :], onehot[:, q, k, :],
                                                 start=True, stop=True)
                        last.then_inc(seg_done, 1)

            def blocks(n, one, fixed=False, ready=None):
                base = n["blocks"] * NBLK

                def sweep(i, first):
                    for s in range(SLOTS_PS):
                        if not first:
                            pe.wait_ge(mm_free, base + SLOTS_PS * i + s - SLOTS_PS + 1)
                        if ready is not None:
                            ready(i * SLOTS_PS + s)
                        one(i * SLOTS_PS + s, s).then_inc(mm_full, 1)
                if fixed:
                    for i in range(SWEEPS):
                        sweep(i, i == 0)
                else:
                    rolled(pe, SWEEPS, sweep)

            def linear(n, terms, func, bias, dst, g, b):
                def one(j, s):
                    for t, (w, src) in enumerate(terms):
                        k = P if w != "attr" else A64 + 2
                        lhs = attr_w[:, :] if w == "attr" else weight(w[0], w[1] * D)
                        last = pe.matmul(ps[:, s, 0:BLK], lhs, T(src, rows_=k)[:, ds(j * BLK, BLK)],
                                         start=t == 0, stop=t == len(terms) - 1)
                    return last
                blocks(n, one)

            def to_nat(n, src, dst):
                def one(j, s):
                    for k in range(2):
                        last = pe.transpose(ps[0:NT, s, k * D:(k + 1) * D], T(src)[:, j * BLK + k * NT:j * BLK + (k + 1) * NT],
                                            ident[:, :])
                    return last
                blocks(n, one, fixed=True)

            def to_t(n, src, w, off, dst):
                def one(j, s):
                    for k in range(2):
                        last = pe.transpose(ps[:, s, k * NT:(k + 1) * NT],
                                            big[0:NT, src * NODES_PAD + off + (2 * j + k) * w:src * NODES_PAD + off + (2 * j + k) * w + D],
                                            ident[0:NT, 0:NT])
                    return last
                blocks(n, one, fixed=True)

            def linear_nat(n, terms, w, bias, dst):
                def one(j, s):
                    for k in range(2):
                        for t, (src, name, off) in enumerate(terms):
                            last = pe.matmul(ps[0:NT, s, k * w:(k + 1) * w], T(src)[:, j * BLK + k * NT:j * BLK + (k + 1) * NT],
                                             weight(name, off, w), start=t == 0, stop=t == len(terms) - 1)
                    return last
                blocks(n, one, fixed=True)

            def norm_linear(n, src, mid, w, bias, g, b):
                def one(j, s):
                    return pe.matmul(ps[:, s, 0:BLK], weight(w[0], w[1] * D), T(mid)[:, ds(j * BLK, BLK)],
                                     start=True, stop=True)
                blocks(n, one, ready=lambda j: pe.wait_ge(act_blk, n["applied"] * NBLK + j + 1))

            def norm_out(n, src, dst, func, tab):
                def one(j, s):
                    for k in range(2):
                        last = pe.transpose(ps[0:NT, s, k * D:(k + 1) * D],
                                            T(XT)[:, j * BLK + k * NT:j * BLK + (k + 1) * NT], ident[:, :])
                    return last
                blocks(n, one, fixed=True, ready=lambda j: pe.wait_ge(added, n["norm_out"] * NBLK + j + 1))

            def layer_norm(n, b, w, g, h, relu, to, tab, have):
                if to is None:
                    return

                def ready(j):
                    if j % SLOTS_PS == 0:
                        if g is None:
                            pe.wait_ge(ln_part, 5 * n["layer_norm"] + j // SLOTS_PS + 1)
                        else:
                            pe.wait_ge(ln_fifth, 5 * n["scaled"] + j // SLOTS_PS + 1)

                def one(j, s):
                    for k in range(2):
                        at_ = b * NODES_PAD + (2 * j + k) * w
                        last = pe.transpose(ps[:, s, k * NT:(k + 1) * NT], big[0:NT, at_:at_ + D], ident[0:NT, 0:NT])
                    return last
                blocks(n, one, fixed=True, ready=ready)

            def conv(n, l):
                def hidden(j):
                    if j >= HIDDEN_PS:
                        pe.wait_ge(hidden_free, n["conv"] * NBLK + j - HIDDEN_PS + 1)
                    pe.matmul(hid(j), weight("v1", l * D), T(AC)[:, j * BLK:(j + 1) * BLK], start=True, stop=True)\
                      .then_inc(hidden_full, 1)

                def one(j, s):
                    if j + 1 < NBLK:
                        hidden(j + 1)
                    pe.wait_ge(hidden_free, n["conv"] * NBLK + j + 1)
                    for k in range(2):
                        last = pe.matmul(ps[0:NT, s, k * D:(k + 1) * D],
                                         T(HT)[:, j * BLK + k * NT:j * BLK + (k + 1) * NT], weight("v2", l * D),
                                         start=True, stop=True)
                    return last
                hidden(0)
                blocks(n, one, fixed=True)

            def q_tiles(n, src, dst):
                pe.wait_ge(pads_zero, 1)

                def one(j, s):
                    for k in range(2):
                        c = (2 * j + k) * P
                        last = pe.matmul(ps[:, s, k * P:(k + 1) * P], T(src, NODES_PAD)[:, c:c + P], weight("q"),
                                         start=True, stop=True)
                    return last
                blocks(n, one, fixed=True)

            walk(pe, rank=rank, scatter_d=scatter_d, edges=edges, linear=linear, to_nat=to_nat, to_t=to_t,
                 linear_nat=linear_nat, norm_linear=norm_linear, norm_out=norm_out, layer_norm=layer_norm,
                 conv=conv, q_tiles=q_tiles)

        @block.scalar
        def _(act):
            def scatter_d(n):
                def trip(i, first):
                    for q in range(RING):
                        g = RING * i + q
                        act.wait_ge(rec_mm, g + 1)
                        if not first:
                            act.wait_ge(rec_out[q], 16 * PER * i)
                        act.activation(rec[:, q, :, 0:D], ps[:, q % 2, :].rearrange("p (k f) -> p k f", f=D), ACT.Copy)
                        act.activation(rec[:, q, :, D:2 * D], ps[:, 2 + q % 2, :].rearrange("p (k f) -> p k f", f=D),
                                       ACT.Silu)
                        act.copy(rec[:, q, :, 2 * D:REC_D].bitcast(I32), meta_d[:, ds(g * PER, PER), :])
                        act.copy(idx_ring[:, q, :], pos_d[:, ds(g * PER, PER)]).then_inc(rec_ready, 1)
                rolled(act, LOADS, trip)

            def edges(n, way, tab, l):
                done = n["edges", way]
                if way == "msg":
                    with act.Fori(0, TRIPS) as i:
                        for q in range(RING):
                            act.wait_ge(msg_sum, done * GROUPS + RING * i + q + 1)
                            act.activation(msg_r[:, q, :, :], msg_r[:, q, :, :], ACT.Relu).then_inc(msg_ready, 1)
                if way == "attn":
                    def turn(g, q):
                        act.wait_ge(turned, g + 1)
                        act.activation(oht_r[:, q % 2, :, :], ps[:, 4 + q % 2, :].rearrange("p (k e) -> p k e", e=P),
                                       ACT.Copy).then_inc(turned_in, 1)
                    turn(0, 0)
                    with act.Fori(0, TRIPS) as i:
                        for q in range(RING):
                            turn(i * RING + q + 1, q + 1)
                            act.wait_ge(score_ready, RING * i + q + 1)
                            act.activation(sc_r[:, q, :, :], heads[:, q, :].unsqueeze(2)
                                           .to_broadcast([P, PER * HEADS, DH]), ACT.Exp).then_inc(exp_done, 1)

            def root(n, v):
                act.wait_ge(var_ready, n["norms"] + 1)
                act.activation(v, v, ACT.Sqrt).then_inc(std_ready, 1)

            def attend(n):
                root(n, mv[:, 1:2])

            def evacuate(n, one, end):
                base = n["blocks"] * NBLK
                with act.Fori(0, SWEEPS) as i:
                    for s in range(SLOTS_PS):
                        act.wait_ge(mm_full, base + SLOTS_PS * i + s + 1)
                        one(i * SLOTS_PS + s, s).then_inc(mm_free, 1)
                if end:
                    act.wait_ge(mm_free, base + NBLK)
                    act.nop(nofuse=True).then_inc(stage_done, 1)

            def linear(n, terms, func, bias, dst, g, b):
                base = n["blocks"] * NBLK
                evacuate(n, lambda j, s: act.activation(T(dst)[:, ds(j * BLK, BLK)], ps[:, s, 0:BLK], func,
                                                        bias=feat(bias)), g is None)
                if g is not None:
                    root(n, mv[:, 1:2])

            def to_nat(n, src, dst):
                evacuate(n, lambda j, s: act.activation(
                    big[0:NT, ds(dst * NODES_PAD + j * 2 * D, 2 * D)], ps[0:NT, s, 0:2 * D], ACT.Copy), True)

            def to_t(n, src, w, off, dst):
                evacuate(n, lambda j, s: act.activation(T(dst)[:, ds(j * BLK, BLK)], ps[:, s, 0:BLK], ACT.Copy), True)

            def apply(dst, src, func, j):
                act.activation(T(dst)[:, ds(j * BLK, BLK)], T(src)[:, ds(j * BLK, BLK)], func,
                               bias=shift[:, 0:1], scale=scale[:, 0:1]).then_inc(act_blk, 1)

            def norm_apply(n, src, dst, func, then):
                with act.Fori(0, NBLK) as j:
                    apply(dst, src, func, j)
                root(n, mv[:, 1:2])

            def norm_linear(n, src, mid, w, bias, g, b):
                with act.Fori(0, NBLK) as j:
                    apply(mid, src, ACT.Relu, j)
                root(n, mv[:, 1:2])

            FIFTH = NTILES // 5

            def store_fifth(tab, b, i):
                act.dma_start(table[tab][ds(i * (FIFTH * NT), FIFTH * NT), :].rearrange("(t p) w -> p t w", p=NT),
                              big[0:NT, ds(b * NODES_PAD + i * (FIFTH * D), FIFTH * D)]
                              .rearrange("p (t w) -> p t w", w=D)).then_inc(fifth_stored, 16)

            def end_of(n, tab):
                if tab is not None:
                    act.wait_ge(fifth_stored, 16 * 5 * (n["io_fifths"] + 1))
                act.nop(nofuse=True).then_inc(stage_done, 1)

            def norm_out(n, src, dst, func, tab):
                base = n["blocks"] * NBLK

                def out(i):
                    for s in range(SLOTS_PS):
                        act.wait_ge(mm_full, base + SLOTS_PS * i + s + 1)
                        act.activation(big[0:NT, ds(NA * NODES_PAD + s * 2 * D + i * (SLOTS_PS * 2 * D), 2 * D)],
                                       ps[0:NT, s, 0:2 * D], ACT.Copy).then_inc(mm_free, 1)
                    if tab is not None:
                        act.wait_ge(mm_free, base + SLOTS_PS * i + SLOTS_PS)
                        store_fifth(tab, NA, i)

                def sweep(i, first):
                    for s in range(SLOTS_PS):
                        apply(dst, src, func, i * SLOTS_PS + s)
                    if not first:
                        out(i - 1)
                rolled(act, SWEEPS, sweep)
                out(SWEEPS - 1)
                act.wait_ge(mm_free, base + NBLK)
                end_of(n, tab)

            def layer_norm(n, b, w, g, h, relu, to, tab, have):
                base = n["blocks"] * NBLK if to is not None else 0
                root(n, mv3[0:NT, :, 2])
                act.wait_ge(stat_ready, n["layer_norm"] + 1)

                def out(i):
                    if tab is not None:
                        if g is None:
                            act.wait_ge(ln_part, 5 * n["layer_norm"] + i + 1)
                        else:
                            act.wait_ge(ln_fifth, 5 * n["scaled"] + i + 1)
                        store_fifth(tab, b, i)
                    if to is not None:
                        for s in range(SLOTS_PS):
                            act.wait_ge(mm_full, base + SLOTS_PS * i + s + 1)
                            act.activation(T(to)[:, ds(s * BLK + i * (SLOTS_PS * BLK), BLK)], ps[:, s, 0:BLK],
                                           ACT.Copy).then_inc(mm_free, 1)

                def fifth(i, first):
                    for k in range(FIFTH):
                        t = big[0:NT, ds(b * NODES_PAD + k * w + i * (FIFTH * w), w)]
                        last = act.activation(t, t, ACT.Identity, bias=shift[0:NT, ds(i * FIFTH + k, 1)],
                                              scale=scale[0:NT, ds(i * FIFTH + k, 1)])
                    last.then_inc(ln_part, 1)
                    if not first:
                        out(i - 1)
                rolled(act, 5, fifth)
                out(4)
                if to is not None:
                    act.wait_ge(mm_free, base + NBLK)
                if to is not None or tab is not None:
                    end_of(n, tab)

            def conv(n, l):
                for j in range(NBLK):
                    act.wait_ge(hidden_full, n["conv"] * NBLK + j + 1)
                    act.activation(T(HT)[:, j * BLK:(j + 1) * BLK], hid(j), ACT.Silu,
                                   bias=feat(f"v_b1{l}")).then_inc(hidden_free, 1)

            def q_tiles(n, src, dst):
                evacuate(n, lambda j, s: act.activation(T(dst, NODES_PAD)[:, ds(j * 2 * P, 2 * P)],
                                                        ps[:, s, 0:2 * P], ACT.Copy), True)

            def store(n, b, tab, w):
                act.dma_start(table[tab].rearrange("(t p) w -> p t w", p=NT), nat(b, w)).then_inc(io_done, 16)
                act.wait_ge(io_done, 16 * (n["io"] + 1))
                act.nop(nofuse=True).then_inc(stage_done, 1)

            def load_x(n, b):
                act.dma_start(nat(b), A["x"].rearrange("(t p) w -> p t w", p=NT)).then_inc(io_done, 16)
                act.wait_ge(io_done, 16 * (n["io"] + 1))
                act.nop(nofuse=True).then_inc(stage_done, 1)

            walk(act, scatter_d=scatter_d, edges=edges, linear=linear, to_nat=to_nat, to_t=to_t,
                 norm_apply=norm_apply, norm_linear=norm_linear, norm_out=norm_out, layer_norm=layer_norm,
                 attend=attend, conv=conv, q_tiles=q_tiles, store=store, load_x=load_x)

        @block.vector
        def _(dve):
            ch = Chain(dve, dve_chain)

            def setup(n):
                dve.wait_ge(loaded, 16 * 10)
                dve.wait_ge(consts, 5)
                ch.mark(dve.memset(blank, 0.0))
                ch.link(dve.memset(blank_s, 0.0))
                dve.memset(blank[:, REC_D - 1:REC_D].bitcast(I32), P)
                dve.memset(blank_s[:, REC_S - 1:REC_S].bitcast(I32), P)
                dve.memset(ones_c, 1.0)
                dve.memset(rec2[:, :, :, A64:A64 + 2], 1.0)
                eps = rows[:, R_AT["eps"]:R_AT["eps"] + LAYERS]
                dve.tensor_scalar(eps1[:, :], eps, 1.0, None, ALU.add)
                for w in "ds":
                    dve.memset(idx[w][:, CHUNKS:], 0)
                    dve.memset(tile_at[w][:, 0:PER], 0)
                    last = dve.memset(node[w][:, CHUNKS:], -1.0)
                last.then_inc(stage_done, 1)

            def rank(n, w):
                k = "ds".index(w)
                meta = meta_d if w == "d" else meta_s
                ch.link(dve.tensor_single_scalar(tile_i, key[w], 7, ALU.arith_shift_right))
                ch.link(dve.tensor_copy(tile_f, tile_i))
                dve.tensor_single_scalar(meta[:, :, meta.shape[2] - 1], key[w], P - 1, ALU.bitwise_and)
                dve.tensor_copy(meta[:, :, 0], val[w])
                with dve.Fori(0, BUCKETS) as b:
                    ch.trip(b, 1)
                    ch.link(dve.tensor_scalar(equal, tile_f, iota[:, ds(b, 1)], 0.0, ALU.is_equal, ALU.add,
                                              accum_out=small[:, 0, ds(b, 1)]))
                ch.leave(BUCKETS, 1)
                dve.memset(pos_f, 0.0).then_inc(totals_ready, 1)
                dve.wait_ge(sums_ready, k + 1)
                ch.link(dve.tensor_scalar(small[:, 1, :], ps[:, 6, 0:BUCKETS], float(P - 1), None, ALU.add))
                ch.link(dve.tensor_copy(small_i[:, 0, :], small[:, 1, :]))
                ch.link(dve.tensor_single_scalar(small_i[:, 1, :], small_i[:, 0, :], 7, ALU.arith_shift_right))
                ch.link(dve.tensor_copy(small[:, 2, :], small_i[:, 1, :]))
                ch.link(dve.tensor_tensor_scan(small[:, 3, :], ones[:, 0:BUCKETS], small[:, 2, :], 0.0,
                                               ALU.mult, ALU.add))
                ch.link(dve.tensor_tensor(small[:, 4, :], small[:, 3, :], small[:, 2, :], ALU.subtract))
                ch.link(dve.scalar_tensor_tensor(small[:, 5, :], small[:, 4, :], float(P), ps[:, 7, 0:BUCKETS],
                                                 ALU.mult, ALU.add))
                ch.link(dve.tensor_scalar(small[:, 5, :], small[:, 5, :], -1.0, None, ALU.add))
                ch.link(dve.tensor_scalar(small[:, 6, :], small[:, 3, :], -1.0, 0.0, ALU.add, ALU.max))
                dve.tensor_scalar(last_chunk[w][:, :], small[0:1, 6, :], float(P), None, ALU.mult)
                for c in range(TCOLS):
                    ch.link(dve.tensor_scalar(small[:, 7, c:c + 1], part[:, :], float(c * P), None, ALU.add))
                    ch.link(dve.tensor_scalar(small[:, 1, :], small[:, 4, :], small[:, 7, c:c + 1], 0.0, ALU.is_le,
                                              ALU.add, accum_out=small[:, 2, c:c + 1]))
                ch.link(dve.tensor_scalar(small[:, 7, 0:TCOLS], small[:, 2, 0:TCOLS], -1.0, float(P), ALU.add, ALU.mult))
                dve.tensor_copy(small_i_tiles, small[:, 7, 0:TCOLS]).then_inc(tiles_ready, 1)
                for_b = 4
                with dve.Fori(0, BUCKETS) as b:
                    ch.trip(b, for_b)
                    ch.link(dve.tensor_scalar(equal, tile_f, iota[:, ds(b, 1)], None, ALU.is_equal))
                    ch.link(dve.tensor_tensor_scan(count, ones_c, equal, small[:, 5, ds(b, 1)], ALU.mult, ALU.add))
                    ch.link(dve.tensor_tensor(match, equal, count, ALU.mult))
                    ch.link(dve.tensor_tensor(pos_f, pos_f, match, ALU.add))
                ch.leave(BUCKETS, for_b)
                dve.tensor_copy(pos[w], pos_f).then_inc(ranked, 1)

            def scatter_d(n):
                rank(n, "s")

            def load_meta(n, w):
                dve.wait_ge(meta_loaded, 16 * ("ds".index(w) + 1))
                dve.tensor_copy(idx[w][:, 0:CHUNKS], meta_in[w][:, :, 0])
                dve.tensor_copy(node[w][:, 0:CHUNKS], meta_in[w][:, :, 1]).then_inc(stage_done, 1)

            def edges(n, way, tab, l):
                w, done = src_of[way], n["edges", way]
                for q in range(RING):
                    dve.tensor_copy(idx_ring[:, q, :], idx[w][:, q * PER:(q + 1) * PER]).then_inc(idx_ready, 1)
                if way == "sum":
                    dve.tensor_scalar(T(AC), T(XT), eps1[:, l:l + 1], None, ALU.mult)
                elif way == "msg":
                    dve.tensor_copy(T(AC), T(XT))
                else:
                    dve.memset(T(AC), 0.0)
                    dve.memset(T(HT, NODES_PAD, A64 + 2 if way == "attr" else P), 0.0)
                ch.link(dve.memset(T(AC, NODES_PAD)[:, N:], 0.0))
                adds = 2 * PER if way == "attr" else PER
                per = adds + (4 if way == "attn" else 0)
                two = big[:, :].rearrange("p (b n) -> p b n", b=5)

                def tiles_of(start, n_):
                    return nc.values_load_multi_w_load_instructions(
                        tile_at[w][0:1, ds(start, n_)], engines=[mybir.EngineType.DVE],
                        min_val=0, max_val=NODES_PAD - P)[1]

                def add(g, q, at_):
                    dve.wait_ge(seg_done, n["edges"] * GROUPS + g + 1)
                    dve.tensor_copy(idx_ring[:, q, :], idx[w][:, ds((g + RING) * PER, PER)]).then_inc(idx_ready, 1)
                    for k in range(PER):
                        c = slice(k * P, (k + 1) * P)
                        if way == "attn":
                            a = two[:, HT:AC + 1, ds(at_[k], P)]
                            p_ = ps[:, 2 * (q % 2) + k // 2, (k % 2) * 2 * P:(k % 2 + 1) * 2 * P]
                            ch.link(dve.tensor_tensor(a, a, p_.rearrange("p (b n) -> p b n", b=2), ALU.add))
                            continue
                        a = big[:, ds(at_[k] + AC * NODES_PAD, P)]
                        ch.mark(dve.tensor_tensor(a, a, ps[:, q, c], ALU.add))
                        if way == "attr":
                            r = A64 + 2
                            z = big[0:r, ds(at_[k] + HT * NODES_PAD, P)]
                            ch.mark(dve.tensor_tensor(z, z, ps[0:r, RING + q, c], ALU.add))
                        ch.wait()

                def one_hots(g, q):
                    dve.tensor_tensor(onehot[:, q, :, :], iota[:, :].unsqueeze(1).to_broadcast([P, PER, P]),
                                      node[w][:, ds(g * PER, PER)].unsqueeze(2).to_broadcast([P, PER, P]),
                                      ALU.is_equal).then_inc(onehot_ready, 1)

                if way == "attn":
                    one_hots(0, 0)

                def trip(i, first):
                    ch.trip(i, RING * per)
                    if not first:
                        ch.k -= adds
                    at_ = tiles_of(i * RING * PER, RING * PER)
                    for q in range(RING):
                        g = i * RING + q
                        if way == "attn":
                            one_hots(g + 1, (q + 1) % RING)
                        else:
                            one_hots(g, q)
                        if way == "msg":
                            dve.wait_ge(gathered[way][q], 16 * PER * (done * TRIPS + i + 1))
                            dve.wait_ge(edge_in[way][q], 16 * (done * TRIPS + i + 1))
                            dve.tensor_tensor(msg_r[:, q, :, :], gath[:, q, :, :], ea_r[:, q, :, :], ALU.add)\
                               .then_inc(msg_sum, 1)
                        if way == "attn":
                            dve.wait_ge(gathered[way][q], 16 * PER * (i + 1))
                            dve.wait_ge(q_rows, g + 1)
                            m = gath[:, q, :, :]
                            ch.link(dve.tensor_tensor(m, kv_r[:, q, :, 0:D],
                                                      ps[:, 6 + q % 2, :].rearrange("p (k f) -> p k f", f=D), ALU.mult))
                            dve.wait_ge(edge_in[way][q], 16 * (i + 1))
                            ch.link(dve.tensor_tensor(m, m, eh_r[:, q, :, :], ALU.mult))
                            ch.link(dve.tensor_reduce(heads[:, q, :], m.rearrange("p k (h d) -> p (k h) d", d=DH),
                                                      mybir.AxisListType.X, ALU.add))
                            ch.link(dve.tensor_scalar(heads[:, q, :], heads[:, q, :], 1.0 / DH ** 0.5, -5.0,
                                                      ALU.mult, ALU.max))
                            dve.tensor_scalar(heads[:, q, :], heads[:, q, :], 5.0, None, ALU.min)\
                               .then_inc(score_ready, 1)
                            if not (first and q == 0):
                                add(g - 1, (q - 1) % RING, at_[q * PER:(q + 1) * PER])
                            dve.wait_ge(exp_done, g + 1)
                            sc = sc_r[:, q, :, :].rearrange("p (k h) d -> p k (h d)", k=PER)
                            dve.tensor_tensor(m, kv_r[:, q, :, D:2 * D], sc, ALU.mult).then_inc(attn_ready, 1)
                        if way != "attn" and not (first and q == 0):
                            add(g - 1, (q - 1) % RING, at_[q * PER:(q + 1) * PER])
                rolled(dve, TRIPS, trip)
                ch.k += adds
                ch.leave(TRIPS, RING * per)
                ch.n -= adds
                add(GROUPS - 1, RING - 1, tiles_of(CHUNKS, PER))
                dve.nop(nofuse=True).then_inc(stage_done, 1)

            def bn_finish(n, g, b):
                ch.link(dve.bn_aggr(mv[:, 0:2], stats[:, 0:NBLK * 6]))
                dve.tensor_scalar(mv[:, 1:2], mv[:, 1:2], EPS, None, ALU.add).then_inc(var_ready, 1)
                dve.wait_ge(std_ready, n["norms"] + 1)
                ch.link(dve.reciprocal(mv[:, 1:2], mv[:, 1:2]))
                ch.link(dve.tensor_tensor(scale[:, 0:1], mv[:, 1:2], feat(g), ALU.mult))
                ch.link(dve.tensor_tensor(mv[:, 0:1], mv[:, 0:1], scale[:, 0:1], ALU.mult))
                dve.tensor_tensor(shift[:, 0:1], feat(b), mv[:, 0:1], ALU.subtract).then_inc(stage_done, 1)

            def linear(n, terms, func, bias, dst, g, b):
                if g is None:
                    return
                with dve.Fori(0, NBLK) as j:
                    dve.wait_ge(mm_free, n["blocks"] * NBLK + j + 1)
                    ch.trip(j, 1)
                    ch.mark(dve.bn_stats(stats[:, ds(j * 6, 6)],
                                         T(dst)[:, ds(j * BLK, BLK)]))
                ch.leave(NBLK, 1)
                ch.wait()
                bn_finish(n, g, b)

            def norm_apply(n, src, dst, func, then):
                with dve.Fori(0, NBLK) as j:
                    dve.wait_ge(act_blk, n["applied"] * NBLK + j + 1)
                    ch.trip(j, 1)
                    ch.mark(dve.bn_stats(stats[:, ds(j * 6, 6)], T(dst)[:, ds(j * BLK, BLK)]))
                ch.leave(NBLK, 1)
                ch.wait()
                bn_finish(n, *then)

            def norm_linear(n, src, mid, w, bias, g, b):
                base = n["blocks"] * NBLK
                with dve.Fori(0, SWEEPS) as i:
                    ch.trip(i, SLOTS_PS)
                    for s in range(SLOTS_PS):
                        d = T(src)[:, ds(s * BLK + i * (SLOTS_PS * BLK), BLK)]
                        dve.wait_ge(mm_full, base + SLOTS_PS * i + s + 1)
                        dve.tensor_scalar(d, ps[:, s, 0:BLK], feat(bias), None, ALU.add).then_inc(mm_free, 1)
                        dve.wait_ge(mm_free, base + SLOTS_PS * i + s + 1)
                        ch.mark(dve.bn_stats(stats[:, ds(s * 6 + i * (SLOTS_PS * 6), 6)], d))
                ch.leave(SWEEPS, SLOTS_PS)
                ch.wait()
                bn_finish(n, g, b)

            def norm_out(n, src, dst, func, tab):
                with dve.Fori(0, NBLK) as j:
                    dve.wait_ge(act_blk, n["applied"] * NBLK + j + 1)
                    x = T(XT)[:, ds(j * BLK, BLK)]
                    dve.tensor_tensor(x, x, T(dst)[:, ds(j * BLK, BLK)], ALU.add).then_inc(added, 1)

            def q_tiles(n, src, dst):
                dve.memset(T(src, NODES_PAD)[:, N:], 0.0).then_inc(pads_zero, 1)

            def conv(n, l):
                base = n["blocks"] * NBLK
                with dve.Fori(0, SWEEPS) as i:
                    ch.trip(i, 3 * SLOTS_PS)
                    for s in range(SLOTS_PS):
                        dve.wait_ge(mm_full, base + SLOTS_PS * i + s + 1)
                        at_ = NA * NODES_PAD + s * 2 * D + i * (SLOTS_PS * 2 * D)
                        d = big[0:NT, ds(at_, 2 * D)]
                        ch.link(dve.tensor_tensor(d, d, ps[0:NT, s, 0:2 * D], ALU.add))
                        d2 = d.rearrange("p (t w) -> p t w", w=D)
                        dve.tensor_tensor(d2, d2, row(("v_b2", l)).unsqueeze(1).to_broadcast([NT, 2, D]), ALU.add)\
                           .then_inc(mm_free, 1)
                        dve.wait_ge(mm_free, base + SLOTS_PS * i + s + 1)
                        for k in range(2):
                            ch.mark(dve.bn_stats(stats[0:NT, ds((s * 2 + k) * 6 + i * (SLOTS_PS * 12), 6)],
                                                 big[0:NT, ds(at_ + k * D, D)]))
                ch.leave(SWEEPS, 3 * SLOTS_PS)
                ch.wait()
                dve.nop(nofuse=True).then_inc(stage_done, 1)

            def linear_nat(n, terms, w, bias, dst):
                base = n["blocks"] * NBLK
                with dve.Fori(0, SWEEPS) as i:
                    for s in range(SLOTS_PS):
                        dve.wait_ge(mm_full, base + SLOTS_PS * i + s + 1)
                        d = big[0:NT, ds(dst * NODES_PAD + s * 2 * w + i * (SLOTS_PS * 2 * w), 2 * w)]
                        p_ = ps[0:NT, s, 0:2 * w]
                        if bias is None:
                            ins = dve.tensor_copy(d, p_)
                        else:
                            ins = dve.tensor_tensor(d.rearrange("p (t w) -> p t w", w=w),
                                                    p_.rearrange("p (t w) -> p t w", w=w),
                                                    row(bias, w).unsqueeze(1).to_broadcast([NT, 2, w]), ALU.add)
                        ins.then_inc(mm_free, 1)
                dve.wait_ge(mm_free, base + NBLK)
                dve.nop(nofuse=True).then_inc(stage_done, 1)

            def layer_norm(n, b, w, g, h, relu, to, tab, have):
                if not have:
                    with dve.Fori(0, 5) as i:
                        ch.trip(i, NTILES // 5)
                        for k in range(NTILES // 5):
                            ch.mark(dve.bn_stats(stats[0:NT, ds(k * 6 + i * (NTILES // 5 * 6), 6)],
                                                 big[0:NT, ds(b * NODES_PAD + k * w + i * (NTILES // 5 * w), w)]))
                    ch.leave(5, NTILES // 5)
                    ch.wait()
                me, mo, se, so = (st3[:, :, k] for k in (1, 4, 2, 5))
                tot, dif, sq = (mv3[0:NT, :, k] for k in range(3))
                ch.mark(dve.tensor_tensor(tot, me, mo, ALU.add))
                ch.mark(dve.tensor_tensor(dif, me, mo, ALU.subtract))
                ch.link(dve.tensor_tensor(sq, se, so, ALU.add))
                ch.mark(dve.tensor_scalar(sq, sq, 1.0 / w, None, ALU.mult))
                ch.link(dve.scalar_tensor_tensor(dif, dif, 0.25, dif, ALU.mult, ALU.mult))
                ch.link(dve.tensor_tensor(sq, sq, dif, ALU.add))
                dve.tensor_scalar(sq, sq, EPS, None, ALU.add).then_inc(var_ready, 1)
                dve.wait_ge(std_ready, n["norms"] + 1)
                ch.link(dve.reciprocal(scale[0:NT, :], sq))
                dve.scalar_tensor_tensor(shift[0:NT, :], tot, -0.5, scale[0:NT, :], ALU.mult, ALU.mult)\
                   .then_inc(stat_ready, 1)
                k = NTILES // 5
                for i in range(5):
                    dve.wait_ge(ln_part, 5 * n["layer_norm"] + i + 1)
                    if g is None:
                        continue
                    x = nat(b, w)[:, i * k:(i + 1) * k, :]
                    ch.link(dve.tensor_tensor(x, x, row(g, w).unsqueeze(1).to_broadcast([NT, k, w]), ALU.mult))
                    last = dve.tensor_tensor(x, x, row(h, w).unsqueeze(1).to_broadcast([NT, k, w]), ALU.add)
                    if relu:
                        ch.link(last)
                        last = dve.tensor_scalar(x, x, 0.0, None, ALU.max)
                    last.then_inc(ln_fifth, 1)
                if to is None and tab is None:
                    if g is not None:
                        dve.wait_ge(ln_fifth, 5 * n["scaled"] + 5)
                    dve.nop(nofuse=True).then_inc(stage_done, 1)

            def add_(n, a, b):
                dve.tensor_tensor(nat(a), nat(a), nat(b), ALU.add).then_inc(stage_done, 1)

            def copy(n, a, b):
                dve.tensor_copy(nat(a), nat(b)).then_inc(stage_done, 1)

            def attend(n):
                ch.link(dve.tensor_scalar(T(HT), T(HT), ATTN_EPS, None, ALU.add))
                ch.link(dve.reciprocal(T(HT), T(HT)))
                ch.link(dve.tensor_tensor(T(AC), T(AC), T(HT), ALU.mult))
                ch.link(dve.tensor_tensor(T(AC), T(AC), T(XT), ALU.add))
                with dve.Fori(0, NBLK) as j:
                    ch.trip(j, 1)
                    ch.mark(dve.bn_stats(stats[:, ds(j * 6, 6)],
                                         T(AC)[:, ds(j * BLK, BLK)]))
                ch.leave(NBLK, 1)
                ch.wait()
                bn_finish(n, "bn_g", "bn_b")

            walk(dve, setup=setup, rank=rank, scatter_d=scatter_d, load_meta=load_meta,
                 edges=edges, linear=linear, norm_apply=norm_apply, norm_linear=norm_linear, norm_out=norm_out,
                 linear_nat=linear_nat, layer_norm=layer_norm, add=add_, copy=copy, attend=attend, conv=conv,
                 q_tiles=q_tiles)


def kernel(**inputs):
    import concourse.bacc as bacc
    from concourse.bass_utils import run_bass_kernel_spmd

    g = {k: np.asarray(v) for k, v in inputs.items()}

    def columns(w):
        return np.concatenate(list(w), axis=1)

    def padded(a, fill):
        full = np.full(E_PAD, fill, a.dtype)
        full[:E] = a
        return np.ascontiguousarray(full.reshape(COLS, P).T)

    def rows_padded(a):
        full = np.zeros((E_PAD, a.shape[1]), a.dtype)
        full[:E] = a
        return full

    l0, l1, l2, l3 = ({k[len(p):]: v for k, v in g.items() if k.startswith(p)}
                      for p in ("L0_gnn_", "L1_gnn_", "L2_gnn_", "L3_gnn_"))
    src, dst = g["src"], g["dst"]
    if src.dtype != np.int32:
        src, dst = src.astype(np.int32), dst.astype(np.int32)
    attr16 = np.zeros((A16 + 1, E_PAD), np.float32)
    attr16[:A16, :E] = g["edge_attr_16"].T
    attr16[A16] = 1.0
    arrays = {
        "x": np.ascontiguousarray(g["x"]),
        "x_t": np.ascontiguousarray(g["x"].T),
        "dst_key": padded(dst, TILES * P), "src_key": padded(src, TILES * P),
        "src_val": padded(src, 0), "dst_val": padded(dst, 0),
        "attr128_t": np.ascontiguousarray(rows_padded(g["edge_attr_128"]).T),
        "attr16_t": attr16,
        "attr64": rows_padded(g["edge_attr_64"]),
        "weights": np.concatenate([
            columns(l0["W1"]), columns(l0["W2"]), columns(l2["W1"]), columns(l2["W2"]), l0["fp_W1"],
            l0["fp_W2"][:D], l0["fp_W2"][D:], l1["W_S_w"].T, l1["W_T_w"].T, l3["WE"], l3["WK"], l3["WV"],
            l3["WQ"]], axis=1),
        "rows": np.concatenate([np.ravel(a) for a in (
            l0["ln_g"], l0["ln_b"], l0["fp_b1"], l0["fp_ln1_g"], l0["fp_ln1_b"], l0["fp_b2"], l0["fp_ln2_g"],
            l0["fp_ln2_b"], l2["b2"], l2["gamma"], l2["beta"], l0["eps"])]),
        "feats": np.ascontiguousarray(np.concatenate([
            l0["b1"], l0["bn1_g"], l0["bn1_b"], l0["b2"], l0["bn2_g"], l0["bn2_b"], l0["obn_g"], l0["obn_b"],
            l2["b1"], l1["W_S_b"][None], l3["bn_gamma"][None], l3["bn_beta"][None]]).T),
        "attr_w": np.concatenate([l1["T_w"].T, l1["T_b"][None], l1["W_T_b"][None]]),
        "ea_w": np.concatenate([l2["We"], l2["be"][None]]),
    }
    nc = bacc.Bacc("TRN2", target_bir_lowering=False, num_devices=1)
    A = {k: nc.dram_tensor(f"in_{k}", v.shape, mybir.dt.from_np(v.dtype), kind="ExternalInput").ap()
         for k, v in arrays.items()}
    A["out"] = nc.dram_tensor("out", (N, D), F32, kind="ExternalOutput").ap()
    program(nc, A)
    r = run_bass_kernel_spmd(nc, [{f"in_{k}": np.ascontiguousarray(v) for k, v in arrays.items()}], core_ids=[0])
    return r.results[0]["out"]
```

```python
from contextlib import ExitStack

import numpy as np
import concourse.bass as bass
from concourse import mybir

F32, I32 = mybir.dt.float32, mybir.dt.int32
ALU, ACT = mybir.AluOpType, mybir.ActivationFunctionType
ds = bass.ds

N, E, D = 6250, 106250, 128
P = 128
LAYERS = 4
HEADS = 8
DH = D // HEADS
A16, A64 = 16, 64
EPS = 1e-5
ATTN_EPS = 1e-6

TILES = -(-N // P)
BUCKETS = TILES + 1
NODES_PAD = BUCKETS * P
PER = 4
RING = 4
COLS = -(-E // (P * PER * RING)) * PER * RING
E_PAD = COLS * P
CHUNKS = (E + TILES * (P - 1)) // P + -(-(E_PAD - E) // P)
CHUNKS = -(-CHUNKS // (PER * RING)) * PER * RING
SLOTS = CHUNKS * P
LEAD = 3
LOOK = PER * RING
TCOLS = -(-CHUNKS // P)
GROUPS = CHUNKS // PER
TRIPS = GROUPS // RING
PIECES = 5
LOADS = COLS // PER // RING
TAIL = CHUNKS - COLS + PER

NT = 125
NTILES = N // NT
BLK = 2 * NT
NBLK = N // BLK
SLOTS_PS = 5
SWEEPS = NBLK // SLOTS_PS

REC_D = D + D + 2
REC_S = A64 + 2 + 2
STEP = 10
PARTS = (8, 8, 8)
XT, HT, AC, NA, RE = range(5)


def weight_columns():
    at, where = 0, {}
    for name, width in (("w1", LAYERS * D), ("w2", LAYERS * D), ("v1", LAYERS * D), ("v2", LAYERS * D),
                        ("f1", 2 * D), ("f2", 2 * D), ("ws", D), ("wt", D), ("we", D), ("kv", 2 * D), ("q", D)):
        where[name] = at
        at += width
    return where, at


def row_columns():
    at, where = 0, {}
    for name, width in (("ln_g", D), ("ln_b", D), ("f_b1", 2 * D), ("f_g1", 2 * D), ("f_h1", 2 * D),
                        ("f_b2", D), ("f_g2", D), ("f_h2", D), ("v_b2", LAYERS * D), ("gamma", LAYERS * D),
                        ("beta", LAYERS * D), ("eps", LAYERS)):
        where[name] = at
        at += width
    return where, at


def feature_columns():
    names = [f"{n}{l}" for n in ("b1", "bn1_g", "bn1_b", "b2", "bn2_g", "bn2_b", "obn_g", "obn_b", "v_b1")
             for l in range(LAYERS)] + ["s_b", "bn_g", "bn_b"]
    return {n: i for i, n in enumerate(names)}, len(names)


W_AT, W_N = weight_columns()
R_AT, R_N = row_columns()
C_AT, C_N = feature_columns()


def network(do):
    do("setup")
    do("rank", "d")
    do("scatter_d")
    do("load_meta", "d")
    for l in range(LAYERS):
        act = ACT.Identity if l == LAYERS - 1 else ACT.Relu
        do("edges", "sum", "x" if l == 0 else "xg", l)
        do("linear", [(("w1", l), AC)], ACT.Identity, f"b1{l}", HT, f"bn1_g{l}", f"bn1_b{l}")
        do("norm_linear", HT, AC, ("w2", l), f"b2{l}", f"bn2_g{l}", f"bn2_b{l}")
        do("norm_apply", HT, AC, act, (f"obn_g{l}", f"obn_b{l}"))
        do("norm_out", AC, HT, act, "xg" if l < LAYERS - 1 else None)
    do("layer_norm", NA, D, ("ln_g", 0), ("ln_b", 0), False, AC, None, False)
    do("linear_nat", [(AC, "f1", 0)], 2 * D, "f_b1", XT, None)
    do("layer_norm", XT, 2 * D, ("f_g1", 0), ("f_h1", 0), True, None, None, False)
    do("to_t", XT, 2 * D, 0, AC)
    do("to_t", XT, 2 * D, D, RE)
    do("linear_nat", [(AC, "f2", 0), (RE, "f2", D)], D, "f_b2", NA, None)
    do("load_x", RE)
    do("layer_norm", NA, D, ("f_g2", 0), ("f_h2", 0), True, None, None, False)
    do("add", NA, RE)
    do("layer_norm", NA, D, None, None, False, XT, "xg", False)
    do("load_meta", "s")
    do("edges", "attr", "xg", 0)
    do("linear", [(("ws", 0), XT), (("wt", 0), AC), ("attr", HT)], ACT.Relu, "s_b", AC, None, None)
    do("to_nat", AC, RE)
    do("add", RE, NA)
    do("layer_norm", RE, D, None, None, False, XT, "xg", False)
    do("copy", NA, RE)
    for l in range(LAYERS):
        do("edges", "msg", "xg", l)
        do("conv", l)
        do("layer_norm", NA, D, ("gamma", l), ("beta", l), False, XT if l < LAYERS - 1 else None,
           "xg" if l < LAYERS - 1 else None, True)
    do("add", NA, RE)
    do("layer_norm", NA, D, None, None, False, XT, None, False)
    do("q_tiles", XT, RE)
    do("linear_nat", [(XT, "kv", 0)], 2 * D, None, AC, "kv")
    do("edges", "attn", "kv", 0)
    do("attend")
    do("norm_out", AC, HT, ACT.Identity, None)
    do("layer_norm", NA, D, None, None, False, None, "out", False)


def rolled(eng, count, body):
    body(0, True)
    if count > 1:
        with eng.Fori(1, count) as i:
            body(i, False)


class Chain:

    def __init__(self, eng, sem):
        self.eng, self.sem, self.n, self.base, self.k = eng, sem, 0, None, 0

    def mark(self, ins):
        ins.then_inc(self.sem, 1)
        if self.base is None:
            self.n += 1
        else:
            self.k += 1

    def wait(self):
        self.eng.wait_ge(self.sem, self.n if self.base is None else self.base + self.k)

    def link(self, ins):
        self.mark(ins)
        self.wait()

    def trip(self, i, per):
        self.base, self.k = self.n + i * per, 0

    def leave(self, trips, per):
        assert self.k == per, (self.k, per)
        self.n, self.base = self.n + trips * per, None


def program(nc, A):
    ctx = ExitStack()
    with ctx:
        def sb(name, shape, dt=F32):
            return ctx.enter_context(nc.sbuf_tensor(name, shape, dt))

        def sem(name):
            return ctx.enter_context(nc.semaphore(name))

        rec_d = nc.dram_tensor("rec_d", [SLOTS, REC_D], F32).ap()
        rec_s = nc.dram_tensor("rec_s", [SLOTS, REC_S], F32).ap()
        tile_row = {w: nc.dram_tensor(f"tile_row_{w}", [TCOLS, P], I32).ap() for w in "ds"}
        table = {"x": A["x"], "out": A["out"],
                 "xg": nc.dram_tensor("x_table", [N, D], F32).ap(),
                 "kv": nc.dram_tensor("kv_table", [N, 2 * D], F32).ap()}

        big = sb("big", [P, 5 * NODES_PAD])
        weights = sb("weights", [P, W_N])
        rows = sb("rows", [P, R_N])
        feats = sb("feats", [P, C_N])
        attr_w = sb("attr_w", [A64 + 2, D])
        ea_w = sb("ea_w", [A16 + 1, D])
        idx = {w: sb(f"idx_{w}", [P, CHUNKS + LOOK], I32) for w in "ds"}
        node = {w: sb(f"node_{w}", [P, CHUNKS + LOOK]) for w in "ds"}
        tile_at = sb("tile_at", [1, TCOLS * P], I32)
        packed = {w: sb(f"packed_{w}", [1, LEAD + TCOLS * P // PER], I32) for w in "ds"}
        last_chunk = {w: sb(f"last_chunk_{w}", [1, BUCKETS], I32) for w in "ds"}
        gath = sb("gath", [P, RING, PER, D])
        onehot = sb("onehot", [P, RING, PER, P])
        idx_ring = sb("idx_ring", [P, RING, PER], I32)
        q_ring = sb("q_ring", [P, RING, PER], I32)
        heads = sb("heads", [P, RING, PER * HEADS])
        iota = sb("iota", [P, P])
        part = sb("part", [P, 1])
        one = sb("one", [P, 1])
        ident = sb("ident", [P, P])
        stats = sb("stats", [P, NTILES * 6])
        st3 = stats[0:NT, :].rearrange("p (t s) -> p t s", s=6)
        mv = sb("mv", [P, NTILES * 3])
        mv3 = mv[:, :].rearrange("p (t s) -> p t s", s=3)
        scale = sb("scale", [P, NTILES])
        shift = sb("shift", [P, NTILES])
        eps1 = sb("eps1", [P, LAYERS])
        small_i = sb("small_i", [P, 2, BUCKETS], I32)
        ps = ctx.enter_context(nc.psum_tensor("ps", [P, 8, 512], F32))

        before = onehot[:, 0, 0, :]
        ones = onehot[:, 0, 1, :]
        small = onehot[:, 1, :, :].rearrange("p k e -> p (k e)")[:, 0:8 * BUCKETS]\
            .rearrange("p (a b) -> p a b", b=BUCKETS)
        small_pack, small_tile = (onehot[0:1, 2, k:k + 2, :].rearrange("p k e -> p (k e)")[:, 0:TCOLS * P // PER]
                                  for k in (0, 2))
        small_i_tiles = small_i[:, 0, 0:TCOLS]

        def T(b, n=N, rows_=P):
            return big[0:rows_, b * NODES_PAD:b * NODES_PAD + n]

        def nat(b, w=D):
            return big[0:NT, b * NODES_PAD:b * NODES_PAD + NTILES * w].rearrange("p (t w) -> p t w", w=w)

        def weight(name, off=0, width=D):
            return weights[:, W_AT[name] + off:W_AT[name] + off + width]

        def row(name, width=D):
            name, l = name if isinstance(name, tuple) else (name, 0)
            at = R_AT[name] + l * D
            return rows[0:NT, at:at + width]

        def feat(name):
            return feats[:, C_AT[name]:C_AT[name] + 1]

        at = [0]

        def part_of_big(shape, start=None):
            if start is not None:
                at[0] = start
            n = int(np.prod(shape[1:]))
            v = big[0:shape[0], at[0]:at[0] + n]
            at[0] += n
            assert at[0] <= 5 * NODES_PAD
            if len(shape) == 4:
                v = v.rearrange("p (a b c) -> p a b c", a=shape[1], b=shape[2])
            elif len(shape) == 3:
                v = v.rearrange("p (a b) -> p a b", a=shape[1])
            return v

        meta_d = part_of_big([P, COLS, 2], HT * NODES_PAD).bitcast(I32)
        pos_d = part_of_big([P, COLS]).bitcast(I32)
        key = {w: part_of_big([P, COLS]).bitcast(I32) for w in "ds"}
        val = {w: part_of_big([P, COLS]).bitcast(I32) for w in "ds"}
        tile_i = part_of_big([P, COLS]).bitcast(I32)
        tile_f = part_of_big([P, COLS])
        equal = [part_of_big([P, COLS]) for _ in range(2)]
        count = [part_of_big([P, COLS]) for _ in range(2)]
        pos_f = part_of_big([P, COLS])
        ones_c = part_of_big([P, COLS])
        rec = part_of_big([P, RING, PER, REC_D])
        attr_t = part_of_big([P, RING, PER * P])
        a16_t = gath[0:A16 + 1, :, :, :].rearrange("p r k e -> p r (k e)")
        blank = part_of_big([P, REC_D], RE * NODES_PAD)
        blank_s = part_of_big([P, REC_S])
        meta_in = {"d": part_of_big([P, CHUNKS, 2], NA * NODES_PAD).bitcast(I32),
                   "s": part_of_big([P, CHUNKS, 2], RE * NODES_PAD + RING * PER * (A64 + 2)).bitcast(I32)}
        attr_r = part_of_big([P, RING, PER, A64 + 2], RE * NODES_PAD)
        ea_r = part_of_big([P, RING, PER, D], HT * NODES_PAD)
        msg_r = part_of_big([P, RING, PER, D])
        kv_r = part_of_big([P, RING, PER, 2 * D], NA * NODES_PAD)
        eh_r = part_of_big([P, RING, PER, D])
        spare = sb("spare", [P, COLS * 3 + RING * PER * REC_S])
        meta_s = spare[:, 0:2 * COLS].rearrange("p (c m) -> p c m", m=2).bitcast(I32)
        pos_s = spare[:, 2 * COLS:3 * COLS].bitcast(I32)
        rec2 = spare[:, 3 * COLS:].rearrange("p (r k w) -> p r k w", r=RING, k=PER)
        sc_r = spare[:, 0:RING * PER * D].rearrange("p (r h d) -> p r h d", r=RING, d=DH)
        oht_r = spare[:, RING * PER * D:RING * PER * D + 2 * PER * P].rearrange("p (r k e) -> p r k e", r=2, k=PER)
        pos = {"d": pos_d, "s": pos_s}

        stage_done = sem("stage_done")
        keys_in = sem("keys_in")
        loaded = sem("loaded")
        consts = sem("consts")
        pool_step = sem("pool_step")
        dve_chain = sem("dve_chain")
        score_chain = sem("score_chain")
        totals_ready = sem("totals_ready")
        sums_ready = sem("sums_ready")
        tiles_ready = sem("tiles_ready")
        ranked = sem("ranked")
        moved = sem("moved")
        blank_s_done = sem("blank_s_done")
        blanked = sem("blanked")
        att_in = [sem(f"att_in{q}") for q in range(RING)]
        att2_in = [sem(f"att2_in{q}") for q in range(RING)]
        rec_mm, rec_ready = sem("rec_mm"), sem("rec_ready")
        rec_out = [sem(f"rec_out{q}") for q in range(RING)]
        rec2_out = [sem(f"rec2_out{q}") for q in range(RING)]
        meta_loaded = [sem(f"meta_loaded{k}") for k in range(PIECES)]
        meta_kept = sem("meta_kept")
        idx_ready = sem("idx_ready")
        onehot_ready = sem("onehot_ready")
        distances = sem("distances")
        msg_sum, msg_ready = sem("msg_sum"), sem("msg_ready")
        attn_ready, score_ready, exp_done = sem("attn_ready"), sem("score_ready"), sem("exp_done")
        seg_done = sem("seg_done")
        gathered = {k: [sem(f"gathered_{k}{q}") for q in range(RING)] for k in ("sum", "attr", "msg", "attn")}
        turned, turned_in, q_rows = sem("turned"), sem("turned_in"), sem("q_rows")
        pads_zero = sem("pads_zero")
        hidden_full, hidden_free = sem("hidden_full"), sem("hidden_free")
        added = sem("added")
        ln_fifth = sem("ln_fifth")
        edge_in = {k: [sem(f"edge_in_{k}{q}") for q in range(RING)] for k in ("attr", "msg", "attn")}
        mm_full, mm_free = sem("mm_full"), sem("mm_free")
        act_blk = sem("act_blk")
        var_ready, std_ready = sem("var_ready"), sem("std_ready")
        stat_ready = sem("stat_ready")
        ln_part = sem("ln_part")
        io_done = sem("io_done")
        fifth_stored = sem("fifth_stored")

        block = ctx.enter_context(nc.Block())

        def walk(eng, **mine):
            seen = {}
            stage = [0]

            def do(kind, *args):
                names = [kind, (kind, args[0])] if kind == "edges" else [kind]
                if kind in ("linear", "to_nat", "to_t", "linear_nat", "norm_linear", "norm_out", "conv", "q_tiles") \
                        or (kind == "layer_norm" and args[5] is not None):
                    names.append("blocks")
                if kind == "layer_norm" and args[2] is not None:
                    names.append("scaled")
                if kind in ("norm_linear", "norm_out", "norm_apply"):
                    names.append("applied")
                if kind == "load_x" or kind == "linear_nat" and args[4]:
                    names.append("io")
                if kind == "norm_out" and args[3] or kind == "layer_norm" and args[6]:
                    names.append("io_fifths")
                if kind in ("layer_norm", "attend", "norm_linear", "norm_apply") \
                        or (kind == "linear" and args[4] is not None):
                    names.append("norms")
                n = {x: seen.get(x, 0) for x in names}
                if kind in mine:
                    if stage[0]:
                        eng.wait_ge(stage_done, stage[0])
                    mine[kind](n, *args)
                stage[0] += 1
                for x in names:
                    seen[x] = seen.get(x, 0) + 1

            network(do)
            return stage[0]

        HIDDEN_PS = 8 - SLOTS_PS

        def hid(j):
            return ps[:, SLOTS_PS + j % HIDDEN_PS, 0:BLK]

        def piece(k):
            return slice(CHUNKS // PIECES * k, CHUNKS // PIECES * (k + 1))

        def tiles_of(engine, w, g, count_):
            v = nc.values_load_multi_w_load_instructions(packed[w][0:1, ds(g + LEAD, count_)], engines=[engine],
                                                         skip_runtime_bounds_check_because="packed tiles are below "
                                                         "64 ** PER * P by the way that they are made")[1]
            return [[((x >> (6 * k)) & (63 * P)).with_bounds(min_val=0, max_val=NODES_PAD - P)
                     for k in range(PER)] for x in v]

        def onehots_before(n):
            return n["edges"] * (GROUPS + 1)

        src_of = {"sum": "d", "attr": "s", "msg": "d", "attn": "d"}

        @block.sync
        def _(sp):
            rd = rec_d.rearrange("(c p) w -> p c w", p=P)
            rs = rec_s.rearrange("(c p) w -> p c w", p=P)

            def setup(n):
                for w, name in (("d", "dst"), ("s", "src")):
                    sp.dma_start(key[w], A[f"{name}_key"]).then_inc(keys_in, 16)
                for w, name in (("d", "src"), ("s", "dst")):
                    sp.dma_start(val[w], A[f"{name}_val"]).then_inc(keys_in, 16)
                for dst, src in ((T(XT), A["x_t"]), (weights[:, :], A["weights"]), (feats[:, :], A["feats"]),
                                 (rows[:, :], A["rows"].partition_broadcast(P)),
                                 (attr_w[:, :], A["attr_w"]), (ea_w[:, :], A["ea_w"])):
                    sp.dma_start(dst, src).then_inc(loaded, 16)

            def prepare(w):
                k = "ds".index(w)
                sp.wait_ge(tiles_ready, k + 1)
                with nc.allow_non_contiguous_dma(reason="a few hundred values"):
                    sp.dma_start(tile_row[w].rearrange("k p -> p k"), small_i_tiles).then_inc(moved, 16)
                sp.wait_ge(moved, 32 * k + 16)
                sp.dma_start(tile_at[:, :], tile_row[w].rearrange("k p -> (k p)").unsqueeze(0)).then_inc(moved, 16)
                sp.wait_ge(moved, 32 * k + 32)
                r, b = (rec_d, blank) if w == "d" else (rec_s, blank_s)
                tail = (rd if w == "d" else rs)[:, CHUNKS - TAIL:CHUNKS, :]
                sp.dma_start(tail, b.unsqueeze(1).to_broadcast([P, TAIL, b.shape[1]])).then_inc(blanked, 16)
                with sp.Fori(0, BUCKETS) as i:
                    c = sp.value_load(last_chunk[w][0:1, ds(i, 1)], min_val=0, max_val=SLOTS - P)
                    sp.wait_ge(blanked, 16 * (BUCKETS + 1) * k + 16 * i + 16)
                    sp.dma_start(r[ds(c, P), :], b).then_inc(blanked, 16)
                sp.wait_ge(blanked, 16 * (BUCKETS + 1) * (k + 1))

            def rank(n, w):
                prepare(w)
                sp.wait_ge(loaded, 16 * 6)
                sp.wait_ge(ranked, 1)
                sp.nop(nofuse=True).then_inc(stage_done, 1)

            def scatter_d(n):
                def trip(i, first):
                    for q in range(RING):
                        if not first:
                            sp.wait_ge(rec_ready, RING * i + q - RING + 1)
                        cols = ds((i * RING + q) * PER * P, PER * P)
                        sp.dma_start(attr_t[:, q, :], A["attr128_t"][:, cols]).then_inc(att_in[q], 16)
                        sp.dma_start(a16_t[:, q, :], A["attr16_t"][:, cols]).then_inc(att_in[q], 16)
                rolled(sp, LOADS, trip)
                for q in range(RING):
                    sp.wait_ge(rec_out[q], 16 * PER * LOADS)
                sp.wait_ge(ranked, 2)
                sp.nop(nofuse=True).then_inc(stage_done, 1)

            def load_attr64():
                a64 = A["attr64"].rearrange("(c p) w -> p c w", p=P)

                def trip(i, first):
                    for q in range(RING):
                        if not first:
                            sp.wait_ge(rec2_out[q], 16 * PER * i)
                        sp.dma_start(rec2[:, q, :, 0:A64], a64[:, ds((i * RING + q) * PER, PER), :])\
                          .then_inc(att2_in[q], 16)
                rolled(sp, LOADS, trip)

            def load_meta(n, w):
                if w == "d":
                    src = rd[:, :, 2 * D:REC_D]
                else:
                    for q in range(RING):
                        sp.wait_ge(rec2_out[q], 16 * PER * LOADS)
                    src = rs[:, :, A64 + 2:REC_S]
                for k in range(PIECES):
                    c = piece(k)
                    sp.dma_start(meta_in[w][:, c, :], src[:, c, :].bitcast(I32)).then_inc(meta_loaded[k], 16)

            def edges(n, way, tab, l):
                if way == "sum":
                    if l == 0:
                        prepare("s")
                        sp.nop(nofuse=True).then_inc(blank_s_done, 1)
                        load_attr64()
                    return
                ring, src = {"attr": (attr_r, rs[:, :, 0:A64 + 2]), "msg": (ea_r, rd[:, :, D:2 * D]),
                             "attn": (eh_r, rd[:, :, 0:D])}[way]
                base, done = n["edges"] * (GROUPS + RING), n["edges", way]
                with sp.Fori(0, TRIPS) as i:
                    for q in range(RING):
                        sp.wait_ge(idx_ready, base + RING * i + q + 1)
                        sp.dma_start(ring[:, q, :, :], src[:, ds((i * RING + q) * PER, PER), :])\
                          .then_inc(edge_in[way][q], 16)

            total = walk(sp, setup=setup, rank=rank, scatter_d=scatter_d, load_meta=load_meta, edges=edges)
            sp.wait_ge(stage_done, total)

        @block.gpsimd
        def _(pool):
            def setup(n):
                pool.iota(iota[:, :], [[1, P]], base=0, channel_multiplier=0,
                          allow_small_or_imprecise_dtypes=True).then_inc(consts, 1)
                pool.iota(part[:, :], [[0, 1]], base=0, channel_multiplier=1,
                          allow_small_or_imprecise_dtypes=True).then_inc(consts, 1)
                pool.memset(ident[:, :], 0.0).then_inc(pool_step, 1)
                pool.memset(before, 1.0).then_inc(pool_step, 1)
                pool.memset(ones, 1.0).then_inc(consts, 1)
                pool.wait_ge(pool_step, 2)
                pool.affine_select(out=ident[:, :], in_=ident[:, :], compare_op=ALU.not_equal, fill=1.0, base=0,
                                   pattern=[[-1, P]], channel_multiplier=1).then_inc(consts, 1)
                pool.affine_select(out=before, in_=before, compare_op=ALU.is_gt, fill=0.0, base=0,
                                   pattern=[[1, P]], channel_multiplier=-1).then_inc(consts, 1)

            def scatter_d(n):
                def trip(i, first):
                    for q in range(RING):
                        pool.wait_ge(rec_ready, RING * i + q + 1)
                        pool.nop(nofuse=True)
                        for k in range(PER):
                            pool.indirect_dma_start(
                                rec_d, bass.IndirectOffsetOnAxis(ap=idx_ring[:, q, k:k + 1], axis=0),
                                rec[:, q, k, :], None).then_inc(rec_out[q], 16)
                rolled(pool, LOADS, trip)

            def scatter_s(start, trips):
                def trip(i, first):
                    for q in range(RING):
                        g = RING * i + q
                        if q % 2 == 0:
                            two = slice(q, q + 2)
                            if not first:
                                pool.wait_ge(rec2_out[q], 16 * PER * i)
                                pool.wait_ge(rec2_out[q + 1], 16 * PER * i)
                                pool.nop(nofuse=True)
                            pool.tensor_copy(rec2[:, two, :, A64 + 2:REC_S].bitcast(I32),
                                             meta_s[:, ds(g * PER, 2 * PER), :].rearrange("p (r k) m -> p r k m", r=2))
                            pool.tensor_copy(q_ring[:, two, :], pos_s[:, ds(g * PER, 2 * PER)]
                                             .rearrange("p (r k) -> p r k", r=2)).then_inc(pool_step, 1)
                            pool.wait_ge(pool_step, 2 + (RING // 2) * i + q // 2 + 1)
                        pool.wait_ge(att2_in[q], 16 * (i + 1))
                        pool.nop(nofuse=True)
                        for k in range(PER):
                            pool.indirect_dma_start(
                                rec_s, bass.IndirectOffsetOnAxis(ap=q_ring[:, q, k:k + 1], axis=0),
                                rec2[:, q, k, :], None).then_inc(rec2_out[q], 16)
                if start == 0:
                    pool.wait_ge(blank_s_done, 1)
                    trip(0, True)
                with pool.Fori(max(start, 1), start + trips) as i:
                    trip(i, False)

            def edges(n, way, tab, l):
                base = n["edges"] * (GROUPS + RING)
                ring = kv_r if way == "attn" else gath
                with pool.Fori(0, TRIPS) as i:
                    for q in range(RING):
                        pool.wait_ge(idx_ready, base + RING * i + q + 1)
                        pool.nop(nofuse=True)
                        for k in range(PER):
                            pool.indirect_dma_start(
                                ring[:, q, k, :], None, table[tab],
                                bass.IndirectOffsetOnAxis(ap=idx_ring[:, q, k:k + 1], axis=0))\
                                .then_inc(gathered[way][q], 16)
                if way == "sum":
                    start = sum(PARTS[:l])
                    scatter_s(start, PARTS[l] if l < LAYERS - 1 else LOADS - start)

            walk(pool, setup=setup, scatter_d=scatter_d, edges=edges)

        @block.tensor
        def _(pe):
            def rank(n, w):
                pe.wait_ge(totals_ready, "ds".index(w) + 1)
                pe.matmul(ps[:, 6, 0:BUCKETS], ones, small[:, 0, :], start=True, stop=True)
                pe.matmul(ps[:, 7, 0:BUCKETS], before, small[:, 0, :], start=True, stop=True)\
                  .then_inc(sums_ready, 1)

            def scatter_d(n):
                def trip(i, first):
                    for q in range(RING):
                        pe.wait_ge(att_in[q], 32 * i + 32)
                        if not first or q >= 2:
                            pe.wait_ge(rec_ready, RING * i + q - 1)
                        for k in range(PER):
                            c = slice(k * P, (k + 1) * P)
                            pe.matmul(ps[:, q % 2, c], attr_t[:, q, c], weight("we"), start=True, stop=True)
                            last = pe.matmul(ps[:, 2 + q % 2, c], a16_t[:, q, c], ea_w[:, :], start=True, stop=True)
                        last.then_inc(rec_mm, 1)
                trip(0, True)
                with pe.Fori(1, 4) as i:
                    trip(i, False)
                rank(n, "s")
                with pe.Fori(4, LOADS) as i:
                    trip(i, False)

            def edges_attn():
                def turn(g, q, base):
                    pe.wait_ge(onehot_ready, base + g + 1)
                    for k in range(PER):
                        last = pe.transpose(ps[:, 4 + q % 2, k * P:(k + 1) * P], onehot[:, q, k, :], ident[:, :])
                    last.then_inc(turned, 1)

                def q_of(g, q, at_):
                    pe.wait_ge(turned_in, g + 1)
                    for k in range(PER):
                        last = pe.matmul(ps[:, 6 + q % 2, k * P:(k + 1) * P], oht_r[:, q % 2, k, :],
                                         big[:, ds(at_[k] + RE * NODES_PAD, P)], start=True, stop=True)
                    last.then_inc(q_rows, 1)

                def sums(g, q):
                    pe.wait_ge(attn_ready, g + 1)
                    for k in range(PER):
                        at2 = 2 * (q % 2) + k // 2
                        c = (k % 2) * 2 * P
                        sc = sc_r[:, q, k * HEADS:(k + 1) * HEADS, :].rearrange("p h d -> p (h d)")
                        pe.matmul(ps[:, at2, c:c + P], sc, onehot[:, q, k, :], start=True, stop=True)
                        last = pe.matmul(ps[:, at2, c + P:c + 2 * P], gath[:, q, k, :], onehot[:, q, k, :],
                                         start=True, stop=True)
                    last.then_inc(seg_done, 1)
                return turn, q_of, sums

            def edges(n, way, tab, l):
                base, done = onehots_before(n), n["edges", way]
                if way == "attn":
                    turn, q_of, sums = edges_attn()
                    turn(0, 0, base)
                    q_of(0, 0, tiles_of(mybir.EngineType.PE, "d", 0, 1)[0])
                    turn(1, 1, base)

                    def trip(i, first):
                        at_ = tiles_of(mybir.EngineType.PE, "d", i * RING + 1, RING)
                        for q in range(RING):
                            q_of(i * RING + q + 1, (q + 1) % RING, at_[q])
                            if not (first and q == 0):
                                sums(i * RING + q - 1, (q - 1) % RING)
                            turn(i * RING + q + 2, (q + 2) % RING, base)
                    rolled(pe, TRIPS, trip)
                    sums(GROUPS - 1, RING - 1)
                    return
                with pe.Fori(0, TRIPS) as i:
                    for q in range(RING):
                        pe.wait_ge(onehot_ready, base + RING * i + q + 1)
                        if way in ("sum", "attr"):
                            pe.wait_ge(gathered[way][q], 16 * PER * (done * TRIPS + i + 1))
                        if way == "attr":
                            pe.wait_ge(edge_in[way][q], 16 * (done * TRIPS + i + 1))
                        if way == "msg":
                            pe.wait_ge(msg_ready, done * GROUPS + RING * i + q + 1)
                        src = msg_r if way == "msg" else gath
                        for k in range(PER):
                            c = slice(k * P, (k + 1) * P)
                            last = pe.matmul(ps[:, q, c], src[:, q, k, :], onehot[:, q, k, :], start=True, stop=True)
                            if way == "attr":
                                last = pe.matmul(ps[0:A64 + 2, RING + q, c], attr_r[:, q, k, :], onehot[:, q, k, :],
                                                 start=True, stop=True)
                        last.then_inc(seg_done, 1)

            def blocks(n, one, fixed=False, ready=None):
                base = n["blocks"] * NBLK

                def sweep(i, first):
                    for s in range(SLOTS_PS):
                        if not first:
                            pe.wait_ge(mm_free, base + SLOTS_PS * i + s - SLOTS_PS + 1)
                        if ready is not None:
                            ready(i * SLOTS_PS + s)
                        one(i * SLOTS_PS + s, s).then_inc(mm_full, 1)
                if fixed:
                    for i in range(SWEEPS):
                        sweep(i, i == 0)
                else:
                    rolled(pe, SWEEPS, sweep)

            def linear(n, terms, func, bias, dst, g, b):
                def one(j, s):
                    for t, (w, src) in enumerate(terms):
                        k = P if w != "attr" else A64 + 2
                        lhs = attr_w[:, :] if w == "attr" else weight(w[0], w[1] * D)
                        last = pe.matmul(ps[:, s, 0:BLK], lhs, T(src, rows_=k)[:, ds(j * BLK, BLK)],
                                         start=t == 0, stop=t == len(terms) - 1)
                    return last
                blocks(n, one)

            def to_nat(n, src, dst):
                def one(j, s):
                    for k in range(2):
                        last = pe.transpose(ps[0:NT, s, k * D:(k + 1) * D], T(src)[:, j * BLK + k * NT:j * BLK + (k + 1) * NT],
                                            ident[:, :])
                    return last
                blocks(n, one, fixed=True)

            def to_t(n, src, w, off, dst):
                def one(j, s):
                    for k in range(2):
                        at_ = src * NODES_PAD + off + (2 * j + k) * w
                        last = pe.transpose(ps[:, s, k * NT:(k + 1) * NT],
                                            big[0:NT, at_:at_ + D],
                                            ident[0:NT, 0:NT])
                    return last
                blocks(n, one, fixed=True)

            def linear_nat(n, terms, w, bias, dst, tab):
                def one(j, s):
                    for k in range(2):
                        for t, (src, name, off) in enumerate(terms):
                            last = pe.matmul(ps[0:NT, s, k * w:(k + 1) * w], T(src)[:, j * BLK + k * NT:j * BLK + (k + 1) * NT],
                                             weight(name, off, w), start=t == 0, stop=t == len(terms) - 1)
                    return last
                blocks(n, one, fixed=True)

            def norm_linear(n, src, mid, w, bias, g, b):
                def one(j, s):
                    return pe.matmul(ps[:, s, 0:BLK], weight(w[0], w[1] * D), T(mid)[:, ds(j * BLK, BLK)],
                                     start=True, stop=True)
                blocks(n, one, ready=lambda j: pe.wait_ge(act_blk, n["applied"] * NBLK + j + 1))

            def norm_out(n, src, dst, func, tab):
                def one(j, s):
                    for k in range(2):
                        last = pe.transpose(ps[0:NT, s, k * D:(k + 1) * D],
                                            T(XT)[:, j * BLK + k * NT:j * BLK + (k + 1) * NT], ident[:, :])
                    return last
                blocks(n, one, fixed=True, ready=lambda j: pe.wait_ge(added, n["norm_out"] * NBLK + j + 1))

            def layer_norm(n, b, w, g, h, relu, to, tab, have):
                if to is None:
                    return

                def ready(j):
                    if j % SLOTS_PS == 0:
                        if g is None:
                            pe.wait_ge(ln_part, 5 * n["layer_norm"] + j // SLOTS_PS + 1)
                        else:
                            pe.wait_ge(ln_fifth, 5 * n["scaled"] + j // SLOTS_PS + 1)

                def one(j, s):
                    for k in range(2):
                        at_ = b * NODES_PAD + (2 * j + k) * w
                        last = pe.transpose(ps[:, s, k * NT:(k + 1) * NT], big[0:NT, at_:at_ + D], ident[0:NT, 0:NT])
                    return last
                blocks(n, one, fixed=True, ready=ready)

            def conv(n, l):
                def hidden(j):
                    if j >= HIDDEN_PS:
                        pe.wait_ge(hidden_free, n["conv"] * NBLK + j - HIDDEN_PS + 1)
                    pe.matmul(hid(j), weight("v1", l * D), T(AC)[:, j * BLK:(j + 1) * BLK], start=True, stop=True)\
                      .then_inc(hidden_full, 1)

                def one(j, s):
                    if j + 1 < NBLK:
                        hidden(j + 1)
                    pe.wait_ge(hidden_free, n["conv"] * NBLK + j + 1)
                    for k in range(2):
                        last = pe.matmul(ps[0:NT, s, k * D:(k + 1) * D],
                                         T(HT)[:, j * BLK + k * NT:j * BLK + (k + 1) * NT], weight("v2", l * D),
                                         start=True, stop=True)
                    return last
                hidden(0)
                blocks(n, one, fixed=True)

            def q_tiles(n, src, dst):
                pe.wait_ge(pads_zero, 1)

                def one(j, s):
                    for k in range(2):
                        c = (2 * j + k) * P
                        last = pe.matmul(ps[:, s, k * P:(k + 1) * P], T(src, NODES_PAD)[:, c:c + P], weight("q"),
                                         start=True, stop=True)
                    return last
                blocks(n, one, fixed=True)

            walk(pe, rank=rank, scatter_d=scatter_d, edges=edges, linear=linear, to_nat=to_nat, to_t=to_t,
                 linear_nat=linear_nat, norm_linear=norm_linear, norm_out=norm_out, layer_norm=layer_norm,
                 conv=conv, q_tiles=q_tiles)

        @block.scalar
        def _(act):
            def scatter_d(n):
                def trip(i, first):
                    for q in range(RING):
                        g = RING * i + q
                        act.wait_ge(rec_mm, g + 1)
                        if not first:
                            act.wait_ge(rec_out[q], 16 * PER * i)
                        act.activation(rec[:, q, :, 0:D], ps[:, q % 2, :].rearrange("p (k f) -> p k f", f=D), ACT.Copy)
                        act.activation(rec[:, q, :, D:2 * D], ps[:, 2 + q % 2, :].rearrange("p (k f) -> p k f", f=D),
                                       ACT.Silu)
                        act.copy(rec[:, q, :, 2 * D:REC_D].bitcast(I32), meta_d[:, ds(g * PER, PER), :])
                        act.copy(idx_ring[:, q, :], pos_d[:, ds(g * PER, PER)]).then_inc(rec_ready, 1)
                rolled(act, LOADS, trip)

            def edges(n, way, tab, l):
                done = n["edges", way]
                if way == "msg":
                    with act.Fori(0, TRIPS) as i:
                        for q in range(RING):
                            act.wait_ge(msg_sum, done * GROUPS + RING * i + q + 1)
                            act.activation(msg_r[:, q, :, :], msg_r[:, q, :, :], ACT.Relu).then_inc(msg_ready, 1)
                if way == "attn":
                    def turn(g, q):
                        act.wait_ge(turned, g + 1)
                        act.activation(oht_r[:, q % 2, :, :], ps[:, 4 + q % 2, :].rearrange("p (k e) -> p k e", e=P),
                                       ACT.Copy).then_inc(turned_in, 1)

                    def one_hots(g, q, wait):
                        if wait:
                            act.wait_ge(seg_done, n["edges"] * GROUPS + g - RING + 1)
                        for k in range(PER):
                            last = act.activation(onehot[:, q, k, :], iota[:, :], ACT.Abs, scale=-1.0,
                                                  bias=node["d"][:, ds(g * PER + k, 1)])
                        last.then_inc(distances, 1)
                        act.wait_ge(distances, g + 1)
                        act.activation(onehot[:, q, :, :], onehot[:, q, :, :], ACT.Relu, bias=one[:, 0:1], scale=-1.0)\
                           .then_inc(onehot_ready, 1)
                    one_hots(0, 0, False)
                    one_hots(1, 1, False)
                    turn(0, 0)
                    turn(1, 1)

                    def free(g, q):
                        act.wait_ge(attn_ready, g + 1)
                        act.copy(idx_ring[:, q, :], idx["d"][:, ds((g + RING) * PER, PER)]).then_inc(idx_ready, 1)

                    def trip(i, first):
                        for q in range(RING):
                            g = i * RING + q
                            one_hots(g + 2, (q + 2) % RING, not (first and q < 2))
                            act.wait_ge(score_ready, g + 1)
                            act.activation(sc_r[:, q, :, :], heads[:, q, :].unsqueeze(2)
                                           .to_broadcast([P, PER * HEADS, DH]), ACT.Exp, scale=1.0 / DH ** 0.5)\
                               .then_inc(exp_done, 1)
                            if not (first and q == 0):
                                free(g - 1, (q - 1) % RING)
                            turn(g + 2, q)
                    rolled(act, TRIPS, trip)
                    free(GROUPS - 1, RING - 1)

            def root(n, v):
                act.wait_ge(var_ready, n["norms"] + 1)
                act.activation(v, v, ACT.Sqrt).then_inc(std_ready, 1)

            def attend(n):
                root(n, mv[:, 1:2])

            def evacuate(n, one, end):
                base = n["blocks"] * NBLK
                with act.Fori(0, SWEEPS) as i:
                    for s in range(SLOTS_PS):
                        act.wait_ge(mm_full, base + SLOTS_PS * i + s + 1)
                        one(i * SLOTS_PS + s, s).then_inc(mm_free, 1)
                if end:
                    act.wait_ge(mm_free, base + NBLK)
                    act.nop(nofuse=True).then_inc(stage_done, 1)

            def linear(n, terms, func, bias, dst, g, b):
                base = n["blocks"] * NBLK
                evacuate(n, lambda j, s: act.activation(T(dst)[:, ds(j * BLK, BLK)], ps[:, s, 0:BLK], func,
                                                        bias=feat(bias)), g is None)
                if g is not None:
                    root(n, mv[:, 1:2])

            def to_nat(n, src, dst):
                evacuate(n, lambda j, s: act.activation(
                    big[0:NT, ds(dst * NODES_PAD + j * 2 * D, 2 * D)], ps[0:NT, s, 0:2 * D], ACT.Copy), True)

            def to_t(n, src, w, off, dst):
                evacuate(n, lambda j, s: act.activation(T(dst)[:, ds(j * BLK, BLK)], ps[:, s, 0:BLK], ACT.Copy), True)

            def apply(dst, src, func, j):
                act.activation(T(dst)[:, ds(j * BLK, BLK)], T(src)[:, ds(j * BLK, BLK)], func,
                               bias=shift[:, 0:1], scale=scale[:, 0:1]).then_inc(act_blk, 1)

            def norm_apply(n, src, dst, func, then):
                with act.Fori(0, NBLK) as j:
                    apply(dst, src, func, j)
                root(n, mv[:, 1:2])

            def norm_linear(n, src, mid, w, bias, g, b):
                with act.Fori(0, NBLK) as j:
                    apply(mid, src, ACT.Relu, j)
                root(n, mv[:, 1:2])

            FIFTH = NTILES // 5

            def store_fifth(tab, b, i):
                act.dma_start(table[tab][ds(i * (FIFTH * NT), FIFTH * NT), :].rearrange("(t p) w -> p t w", p=NT),
                              big[0:NT, ds(b * NODES_PAD + i * (FIFTH * D), FIFTH * D)]
                              .rearrange("p (t w) -> p t w", w=D)).then_inc(fifth_stored, 16)

            def end_of(n, tab):
                if tab is not None:
                    act.wait_ge(fifth_stored, 16 * 5 * (n["io_fifths"] + 1))
                act.nop(nofuse=True).then_inc(stage_done, 1)

            def norm_out(n, src, dst, func, tab):
                base = n["blocks"] * NBLK

                def out(i):
                    for s in range(SLOTS_PS):
                        act.wait_ge(mm_full, base + SLOTS_PS * i + s + 1)
                        act.activation(big[0:NT, ds(NA * NODES_PAD + s * 2 * D + i * (SLOTS_PS * 2 * D), 2 * D)],
                                       ps[0:NT, s, 0:2 * D], ACT.Copy).then_inc(mm_free, 1)
                    if tab is not None:
                        act.wait_ge(mm_free, base + SLOTS_PS * i + SLOTS_PS)
                        store_fifth(tab, NA, i)

                def sweep(i, first):
                    for s in range(SLOTS_PS):
                        apply(dst, src, func, i * SLOTS_PS + s)
                    if not first:
                        out(i - 1)
                rolled(act, SWEEPS, sweep)
                out(SWEEPS - 1)
                act.wait_ge(mm_free, base + NBLK)
                end_of(n, tab)

            def layer_norm(n, b, w, g, h, relu, to, tab, have):
                base = n["blocks"] * NBLK if to is not None else 0
                root(n, mv3[0:NT, :, 2])
                act.wait_ge(stat_ready, n["layer_norm"] + 1)

                def out(i):
                    if tab is not None:
                        if g is None:
                            act.wait_ge(ln_part, 5 * n["layer_norm"] + i + 1)
                        else:
                            act.wait_ge(ln_fifth, 5 * n["scaled"] + i + 1)
                        store_fifth(tab, b, i)
                    if to is not None:
                        for s in range(SLOTS_PS):
                            act.wait_ge(mm_full, base + SLOTS_PS * i + s + 1)
                            act.activation(T(to)[:, ds(s * BLK + i * (SLOTS_PS * BLK), BLK)], ps[:, s, 0:BLK],
                                           ACT.Copy).then_inc(mm_free, 1)

                def fifth(i, first):
                    for k in range(FIFTH):
                        t = big[0:NT, ds(b * NODES_PAD + k * w + i * (FIFTH * w), w)]
                        last = act.activation(t, t, ACT.Identity, bias=shift[0:NT, ds(i * FIFTH + k, 1)],
                                              scale=scale[0:NT, ds(i * FIFTH + k, 1)])
                    last.then_inc(ln_part, 1)
                    if not first:
                        out(i - 1)
                rolled(act, 5, fifth)
                out(4)
                if to is not None:
                    act.wait_ge(mm_free, base + NBLK)
                if to is not None or tab is not None:
                    end_of(n, tab)

            def conv(n, l):
                for j in range(NBLK):
                    act.wait_ge(hidden_full, n["conv"] * NBLK + j + 1)
                    act.activation(T(HT)[:, j * BLK:(j + 1) * BLK], hid(j), ACT.Silu,
                                   bias=feat(f"v_b1{l}")).then_inc(hidden_free, 1)

            def q_tiles(n, src, dst):
                evacuate(n, lambda j, s: act.activation(T(dst, NODES_PAD)[:, ds(j * 2 * P, 2 * P)],
                                                        ps[:, s, 0:2 * P], ACT.Copy), True)

            def linear_nat(n, terms, w, bias, dst, tab):
                if tab is None:
                    return
                for i in range(5):
                    act.wait_ge(mm_free, n["blocks"] * NBLK + SLOTS_PS * (i + 1))
                    act.dma_start(table[tab][i * FIFTH * NT:(i + 1) * FIFTH * NT, :].rearrange("(t p) w -> p t w", p=NT),
                                  nat(dst, w)[:, i * FIFTH:(i + 1) * FIFTH, :]).then_inc(io_done, 16)
                act.wait_ge(io_done, 16 * (n["io"] + 5))
                act.nop(nofuse=True).then_inc(stage_done, 1)

            def load_x(n, b):
                act.dma_start(nat(b), A["x"].rearrange("(t p) w -> p t w", p=NT)).then_inc(io_done, 16)
                act.wait_ge(io_done, 16 * (n["io"] + 1))
                act.nop(nofuse=True).then_inc(stage_done, 1)

            walk(act, scatter_d=scatter_d, edges=edges, linear=linear, to_nat=to_nat, to_t=to_t,
                 norm_apply=norm_apply, norm_linear=norm_linear, norm_out=norm_out, layer_norm=layer_norm,
                 attend=attend, conv=conv, q_tiles=q_tiles, linear_nat=linear_nat, load_x=load_x)

        @block.vector
        def _(dve):
            ch, sch = Chain(dve, dve_chain), Chain(dve, score_chain)

            def setup(n):
                dve.wait_ge(keys_in, 16 * 4)
                dve.wait_ge(consts, 5)
                ch.mark(dve.memset(blank, 0.0))
                ch.link(dve.memset(blank_s, 0.0))
                dve.memset(blank[:, REC_D - 1:REC_D].bitcast(I32), P)
                dve.memset(blank_s[:, REC_S - 1:REC_S].bitcast(I32), P)
                dve.memset(ones_c, 1.0)
                dve.memset(one[:, :], 1.0)
                dve.memset(rec2[:, :, :, A64:A64 + 2], 1.0)
                for w in "ds":
                    dve.memset(idx[w][:, CHUNKS:], 0)
                    dve.memset(packed[w][:, 0:LEAD], 0)
                    last = dve.memset(node[w][:, CHUNKS:], -1.0)
                last.then_inc(stage_done, 1)

            def rank(n, w):
                k = "ds".index(w)
                meta = meta_d if w == "d" else meta_s
                ch.link(dve.tensor_single_scalar(tile_i, key[w], 7, ALU.arith_shift_right))
                ch.link(dve.tensor_copy(tile_f, tile_i))
                dve.tensor_single_scalar(meta[:, :, meta.shape[2] - 1], key[w], P - 1, ALU.bitwise_and)
                dve.tensor_copy(meta[:, :, 0], val[w])
                with dve.Fori(0, BUCKETS // STEP) as i:
                    ch.trip(i, STEP)
                    for m in range(STEP):
                        b = i * STEP + m
                        ch.link(dve.tensor_scalar(equal[m % 2], tile_f, iota[:, ds(b, 1)], 0.0, ALU.is_equal, ALU.add,
                                                  accum_out=small[:, 0, ds(b, 1)]))
                ch.leave(BUCKETS // STEP, STEP)
                dve.memset(pos_f, 0.0).then_inc(totals_ready, 1)
                dve.wait_ge(sums_ready, k + 1)
                ch.link(dve.tensor_scalar(small[:, 1, :], ps[:, 6, 0:BUCKETS], float(P - 1), None, ALU.add))
                ch.link(dve.tensor_copy(small_i[:, 0, :], small[:, 1, :]))
                ch.link(dve.tensor_single_scalar(small_i[:, 1, :], small_i[:, 0, :], 7, ALU.arith_shift_right))
                ch.link(dve.tensor_copy(small[:, 2, :], small_i[:, 1, :]))
                ch.link(dve.tensor_tensor_scan(small[:, 3, :], ones[:, 0:BUCKETS], small[:, 2, :], 0.0,
                                               ALU.mult, ALU.add))
                ch.link(dve.tensor_tensor(small[:, 4, :], small[:, 3, :], small[:, 2, :], ALU.subtract))
                ch.link(dve.scalar_tensor_tensor(small[:, 5, :], small[:, 4, :], float(P), ps[:, 7, 0:BUCKETS],
                                                 ALU.mult, ALU.add))
                ch.link(dve.tensor_scalar(small[:, 5, :], small[:, 5, :], -1.0, None, ALU.add))
                ch.link(dve.tensor_scalar(small[:, 6, :], small[:, 3, :], -1.0, 0.0, ALU.add, ALU.max))
                dve.tensor_scalar(last_chunk[w][:, :], small[0:1, 6, :], float(P), None, ALU.mult)
                for c in range(TCOLS):
                    ch.link(dve.tensor_scalar(small[:, 7, c:c + 1], part[:, :], float(c * P), None, ALU.add))
                    ch.link(dve.tensor_scalar(small[:, 1, :], small[:, 4, :], small[:, 7, c:c + 1], 0.0, ALU.is_le,
                                              ALU.add, accum_out=small[:, 2, c:c + 1]))
                ch.link(dve.tensor_scalar(small[:, 7, 0:TCOLS], small[:, 2, 0:TCOLS], -1.0, float(P), ALU.add, ALU.mult))
                dve.tensor_copy(small_i_tiles, small[:, 7, 0:TCOLS]).then_inc(tiles_ready, 1)
                with dve.Fori(0, BUCKETS // STEP) as i:
                    ch.trip(i, 3 * STEP)
                    for m in range(STEP):
                        b, e, c = i * STEP + m, equal[m % 2], count[m % 2]
                        ch.link(dve.tensor_scalar(e, tile_f, iota[:, ds(b, 1)], None, ALU.is_equal))
                        ch.link(dve.tensor_tensor_scan(c, ones_c, e, small[:, 5, ds(b, 1)], ALU.mult, ALU.add))
                        dve.nop(nofuse=True)
                        ch.link(dve.copy_predicated(pos_f, e.bitcast(I32), c))
                ch.leave(BUCKETS // STEP, 3 * STEP)
                dve.tensor_copy(pos[w], pos_f).then_inc(ranked, 1)

            def scatter_d(n):
                dve.tensor_scalar(eps1[:, :], rows[:, R_AT["eps"]:R_AT["eps"] + LAYERS], 1.0, None, ALU.add)
                rank(n, "s")

            def keep(w, k):
                dve.wait_ge(meta_loaded[k], 16 * ("ds".index(w) + 1))
                dve.tensor_copy(idx[w][:, piece(k)], meta_in[w][:, piece(k), 0])
                return dve.tensor_copy(node[w][:, piece(k)], meta_in[w][:, piece(k), 1])

            def load_meta(n, w):
                four = tile_at[:, :].rearrange("p (g k) -> p g k", k=PER)
                acc = small_pack
                ch.link(dve.tensor_copy(acc, four[:, :, PER - 1]))
                for k in reversed(range(PER - 1)):
                    ch.link(dve.tensor_copy(small_tile, four[:, :, k]))
                    ch.link(dve.scalar_tensor_tensor(acc, acc, 64.0, small_tile, ALU.mult, ALU.add))
                dve.tensor_copy(packed[w][:, LEAD:], acc)
                keep(w, 0).then_inc(stage_done, 1)

            def edges(n, way, tab, l):
                w, done = src_of[way], n["edges", way]
                for q in range(RING):
                    dve.tensor_copy(idx_ring[:, q, :], idx[w][:, q * PER:(q + 1) * PER]).then_inc(idx_ready, 1)
                if way == "sum":
                    dve.tensor_scalar(T(AC), T(XT), eps1[:, l:l + 1], None, ALU.mult)
                elif way == "msg":
                    dve.tensor_copy(T(AC), T(XT))
                    dve.tensor_tensor(nat(NA), nat(NA), row(("v_b2", l)).unsqueeze(1).to_broadcast([NT, NTILES, D]),
                                      ALU.add)
                else:
                    dve.memset(T(AC), 0.0)
                    dve.memset(T(HT, NODES_PAD, A64 + 2 if way == "attr" else P), 0.0)
                ch.link(dve.memset(T(AC, NODES_PAD)[:, N:], 0.0))
                adds = 2 * PER if way == "attr" else PER
                lag = {"msg": 2, "attn": 3}.get(way, 1)
                two = big[:, :].rearrange("p (b n) -> p b n", b=5)

                def free(g, q):
                    dve.tensor_copy(idx_ring[:, q, :], idx[w][:, ds((g + RING) * PER, PER)]).then_inc(idx_ready, 1)

                def add(g, q, at_, between=()):
                    dve.wait_ge(seg_done, n["edges"] * GROUPS + g + 1)
                    if way in ("sum", "attr"):
                        free(g, q)
                    for k in range(PER):
                        c = slice(k * P, (k + 1) * P)
                        ch.wait()
                        if way == "attn":
                            a = two[:, HT:AC + 1, ds(at_[k], P)]
                            p_ = ps[:, 2 * (q % 2) + k // 2, (k % 2) * 2 * P:(k % 2 + 1) * 2 * P]
                            ch.mark(dve.tensor_tensor(a, a, p_.rearrange("p (b n) -> p b n", b=2), ALU.add))
                        else:
                            a = big[:, ds(at_[k] + AC * NODES_PAD, P)]
                            ch.mark(dve.tensor_tensor(a, a, ps[:, q, c], ALU.add))
                        if way == "attr":
                            r = A64 + 2
                            z = big[0:r, ds(at_[k] + HT * NODES_PAD, P)]
                            ch.mark(dve.tensor_tensor(z, z, ps[0:r, RING + q, c], ALU.add))
                        for step in between[k:k + 1]:
                            step()
                    for step in between[PER:]:
                        step()

                def one_hots(g, q):
                    dve.tensor_tensor(onehot[:, q, :, :], iota[:, :].unsqueeze(1).to_broadcast([P, PER, P]),
                                      node[w][:, ds(g * PER, PER)].unsqueeze(2).to_broadcast([P, PER, P]),
                                      ALU.is_equal).then_inc(onehot_ready, 1)

                def message(i, q):
                    dve.wait_ge(gathered[way][q], 16 * PER * (done * TRIPS + i + 1))
                    dve.wait_ge(edge_in[way][q], 16 * (done * TRIPS + i + 1))
                    dve.tensor_tensor(msg_r[:, q, :, :], gath[:, q, :, :], ea_r[:, q, :, :], ALU.add)\
                       .then_inc(msg_sum, 1)

                def times_q(i, q):
                    dve.wait_ge(gathered[way][q], 16 * PER * (i + 1))
                    dve.wait_ge(q_rows, i * RING + q + 1)
                    sch.mark(dve.tensor_tensor(gath[:, q, :, :], kv_r[:, q, :, 0:D],
                                               ps[:, 6 + q % 2, :].rearrange("p (k f) -> p k f", f=D), ALU.mult))

                def times_eh(i, q):
                    dve.wait_ge(edge_in[way][q], 16 * (i + 1))
                    sch.wait()
                    sch.mark(dve.tensor_tensor(gath[:, q, :, :], gath[:, q, :, :], eh_r[:, q, :, :], ALU.mult))

                def head_sums(q):
                    sch.wait()
                    sch.mark(dve.tensor_reduce(heads[:, q, :], gath[:, q, :, :].rearrange("p k (h d) -> p (k h) d", d=DH),
                                               mybir.AxisListType.X, ALU.add))

                def clamp(q):
                    sch.wait()
                    dve.tensor_scalar(heads[:, q, :], heads[:, q, :], -5.0 * DH ** 0.5, 5.0 * DH ** 0.5,
                                      ALU.max, ALU.min).then_inc(score_ready, 1)

                def times_scores(g, q):
                    ch.wait()
                    dve.wait_ge(exp_done, g + 1)
                    sc = sc_r[:, q, :, :].rearrange("p (k h) d -> p k (h d)", k=PER)
                    dve.tensor_tensor(gath[:, q, :, :], kv_r[:, q, :, D:2 * D], sc, ALU.mult).then_inc(attn_ready, 1)

                def free_read(g, q):
                    dve.wait_ge(msg_sum, done * GROUPS + g + 1)
                    free(g, q)

                if way != "attn":
                    one_hots(0, 0)

                def trip(i, first):
                    ch.trip(i, RING * adds)
                    if way == "attn":
                        sch.trip(i, 3 * RING)
                    if not first:
                        ch.k -= lag * adds
                    at_ = tiles_of(mybir.EngineType.DVE, w, i * RING - lag, RING)
                    for q in range(RING):
                        g, before_q = i * RING + q, (q - 1) % RING
                        if way == "attn":
                            steps = [lambda: times_q(i, q), lambda: times_eh(i, q), lambda: head_sums(q),
                                     lambda: clamp(q)]
                            if not (first and q == 0):
                                steps.append(lambda: times_scores(g - 1, before_q))
                        elif way == "msg":
                            steps = [lambda: one_hots(g + 1, (q + 1) % RING), lambda: message(i, q), lambda: None,
                                     lambda: free_read(g, q)]
                        else:
                            steps = [lambda: one_hots(g + 1, (q + 1) % RING)]
                        if first and q < lag:
                            for step in steps:
                                step()
                        else:
                            add(g - lag, (q - lag) % RING, at_[q], steps)
                if way == "attr" or way == "sum" and l == 0:
                    trip(0, True)
                    ends = [TRIPS // PIECES * (k + 1) - 1 for k in range(PIECES - 1)] + [TRIPS]
                    for k in range(PIECES):
                        if k > 0:
                            keep(w, k).then_inc(meta_kept, 1)
                            dve.wait_ge(meta_kept, (PIECES - 1) * "ds".index(w) + k)
                        with dve.Fori(ends[k - 1] if k > 0 else 1, ends[k]) as i:
                            trip(i, False)
                else:
                    rolled(dve, TRIPS, trip)
                ch.k += lag * adds
                ch.leave(TRIPS, RING * adds)
                ch.n -= lag * adds
                at_ = tiles_of(mybir.EngineType.DVE, w, GROUPS - lag, lag)
                last = lambda: None
                if way == "attn":
                    sch.leave(TRIPS, 3 * RING)
                    last = lambda: times_scores(GROUPS - 1, RING - 1)
                for k in range(lag):
                    add(GROUPS - lag + k, (GROUPS - lag + k) % RING, at_[k],
                        [lambda: None] * PER + [last] if k == 0 else ())
                ch.wait()
                dve.nop(nofuse=True).then_inc(stage_done, 1)

            def bn_finish(n, g, b):
                ch.link(dve.bn_aggr(mv[:, 0:2], stats[:, 0:NBLK * 6]))
                dve.tensor_scalar(mv[:, 1:2], mv[:, 1:2], EPS, None, ALU.add).then_inc(var_ready, 1)
                dve.wait_ge(std_ready, n["norms"] + 1)
                ch.link(dve.reciprocal(mv[:, 1:2], mv[:, 1:2]))
                ch.link(dve.tensor_tensor(scale[:, 0:1], mv[:, 1:2], feat(g), ALU.mult))
                ch.link(dve.tensor_tensor(mv[:, 0:1], mv[:, 0:1], scale[:, 0:1], ALU.mult))
                dve.tensor_tensor(shift[:, 0:1], feat(b), mv[:, 0:1], ALU.subtract).then_inc(stage_done, 1)

            def linear(n, terms, func, bias, dst, g, b):
                if g is None:
                    return
                with dve.Fori(0, NBLK) as j:
                    dve.wait_ge(mm_free, n["blocks"] * NBLK + j + 1)
                    ch.trip(j, 1)
                    ch.mark(dve.bn_stats(stats[:, ds(j * 6, 6)],
                                         T(dst)[:, ds(j * BLK, BLK)]))
                ch.leave(NBLK, 1)
                ch.wait()
                bn_finish(n, g, b)

            def norm_apply(n, src, dst, func, then):
                with dve.Fori(0, NBLK) as j:
                    dve.wait_ge(act_blk, n["applied"] * NBLK + j + 1)
                    ch.trip(j, 1)
                    ch.mark(dve.bn_stats(stats[:, ds(j * 6, 6)], T(dst)[:, ds(j * BLK, BLK)]))
                ch.leave(NBLK, 1)
                ch.wait()
                bn_finish(n, *then)

            def norm_linear(n, src, mid, w, bias, g, b):
                base = n["blocks"] * NBLK
                with dve.Fori(0, SWEEPS) as i:
                    ch.trip(i, SLOTS_PS)
                    for s in range(SLOTS_PS):
                        d = T(src)[:, ds(s * BLK + i * (SLOTS_PS * BLK), BLK)]
                        dve.wait_ge(mm_full, base + SLOTS_PS * i + s + 1)
                        dve.tensor_scalar(d, ps[:, s, 0:BLK], feat(bias), None, ALU.add).then_inc(mm_free, 1)
                        dve.wait_ge(mm_free, base + SLOTS_PS * i + s + 1)
                        ch.mark(dve.bn_stats(stats[:, ds(s * 6 + i * (SLOTS_PS * 6), 6)], d))
                ch.leave(SWEEPS, SLOTS_PS)
                ch.wait()
                bn_finish(n, g, b)

            def norm_out(n, src, dst, func, tab):
                with dve.Fori(0, NBLK) as j:
                    dve.wait_ge(act_blk, n["applied"] * NBLK + j + 1)
                    x = T(XT)[:, ds(j * BLK, BLK)]
                    dve.tensor_tensor(x, x, T(dst)[:, ds(j * BLK, BLK)], ALU.add).then_inc(added, 1)

            def q_tiles(n, src, dst):
                dve.memset(T(src, NODES_PAD)[:, N:], 0.0).then_inc(pads_zero, 1)

            def conv(n, l):
                base = n["blocks"] * NBLK
                with dve.Fori(0, SWEEPS) as i:
                    ch.trip(i, 2 * SLOTS_PS)
                    for s in range(SLOTS_PS):
                        dve.wait_ge(mm_full, base + SLOTS_PS * i + s + 1)
                        at_ = NA * NODES_PAD + s * 2 * D + i * (SLOTS_PS * 2 * D)
                        d = big[0:NT, ds(at_, 2 * D)]
                        dve.tensor_tensor(d, d, ps[0:NT, s, 0:2 * D], ALU.add).then_inc(mm_free, 1)
                        dve.wait_ge(mm_free, base + SLOTS_PS * i + s + 1)
                        for k in range(2):
                            ch.mark(dve.bn_stats(stats[0:NT, ds((s * 2 + k) * 6 + i * (SLOTS_PS * 12), 6)],
                                                 big[0:NT, ds(at_ + k * D, D)]))
                ch.leave(SWEEPS, 2 * SLOTS_PS)
                ch.wait()
                dve.nop(nofuse=True).then_inc(stage_done, 1)

            def linear_nat(n, terms, w, bias, dst, tab):
                base = n["blocks"] * NBLK
                with dve.Fori(0, SWEEPS) as i:
                    for s in range(SLOTS_PS):
                        dve.wait_ge(mm_full, base + SLOTS_PS * i + s + 1)
                        d = big[0:NT, ds(dst * NODES_PAD + s * 2 * w + i * (SLOTS_PS * 2 * w), 2 * w)]
                        p_ = ps[0:NT, s, 0:2 * w]
                        if bias is None:
                            ins = dve.tensor_copy(d, p_)
                        else:
                            ins = dve.tensor_tensor(d.rearrange("p (t w) -> p t w", w=w),
                                                    p_.rearrange("p (t w) -> p t w", w=w),
                                                    row(bias, w).unsqueeze(1).to_broadcast([NT, 2, w]), ALU.add)
                        ins.then_inc(mm_free, 1)
                if tab is None:
                    dve.wait_ge(mm_free, base + NBLK)
                    dve.nop(nofuse=True).then_inc(stage_done, 1)

            def layer_norm(n, b, w, g, h, relu, to, tab, have):
                if not have:
                    with dve.Fori(0, 5) as i:
                        ch.trip(i, NTILES // 5)
                        for k in range(NTILES // 5):
                            ch.mark(dve.bn_stats(stats[0:NT, ds(k * 6 + i * (NTILES // 5 * 6), 6)],
                                                 big[0:NT, ds(b * NODES_PAD + k * w + i * (NTILES // 5 * w), w)]))
                    ch.leave(5, NTILES // 5)
                    ch.wait()
                me, mo, se, so = (st3[:, :, k] for k in (1, 4, 2, 5))
                tot, dif, sq = (mv3[0:NT, :, k] for k in range(3))
                ch.mark(dve.tensor_tensor(tot, me, mo, ALU.add))
                ch.mark(dve.tensor_tensor(dif, me, mo, ALU.subtract))
                ch.link(dve.tensor_tensor(sq, se, so, ALU.add))
                ch.mark(dve.tensor_scalar(sq, sq, 1.0 / w, None, ALU.mult))
                ch.link(dve.scalar_tensor_tensor(dif, dif, 0.25, dif, ALU.mult, ALU.mult))
                ch.link(dve.tensor_tensor(sq, sq, dif, ALU.add))
                dve.tensor_scalar(sq, sq, EPS, None, ALU.add).then_inc(var_ready, 1)
                dve.wait_ge(std_ready, n["norms"] + 1)
                ch.link(dve.reciprocal(scale[0:NT, :], sq))
                dve.scalar_tensor_tensor(shift[0:NT, :], tot, -0.5, scale[0:NT, :], ALU.mult, ALU.mult)\
                   .then_inc(stat_ready, 1)
                k = NTILES // 5
                for i in range(5):
                    dve.wait_ge(ln_part, 5 * n["layer_norm"] + i + 1)
                    if g is None:
                        continue
                    x = nat(b, w)[:, i * k:(i + 1) * k, :]
                    ch.link(dve.tensor_tensor(x, x, row(g, w).unsqueeze(1).to_broadcast([NT, k, w]), ALU.mult))
                    last = dve.tensor_tensor(x, x, row(h, w).unsqueeze(1).to_broadcast([NT, k, w]), ALU.add)
                    if relu:
                        ch.link(last)
                        last = dve.tensor_scalar(x, x, 0.0, None, ALU.max)
                    last.then_inc(ln_fifth, 1)
                if to is None and tab is None:
                    if g is not None:
                        dve.wait_ge(ln_fifth, 5 * n["scaled"] + 5)
                    dve.nop(nofuse=True).then_inc(stage_done, 1)

            def add_(n, a, b):
                dve.tensor_tensor(nat(a), nat(a), nat(b), ALU.add).then_inc(stage_done, 1)

            def copy(n, a, b):
                dve.tensor_copy(nat(a), nat(b)).then_inc(stage_done, 1)

            def attend(n):
                ch.link(dve.tensor_scalar(T(HT), T(HT), ATTN_EPS, None, ALU.add))
                ch.link(dve.reciprocal(T(HT), T(HT)))
                ch.link(dve.tensor_tensor(T(AC), T(AC), T(HT), ALU.mult))
                ch.link(dve.tensor_tensor(T(AC), T(AC), T(XT), ALU.add))
                with dve.Fori(0, NBLK) as j:
                    ch.trip(j, 1)
                    ch.mark(dve.bn_stats(stats[:, ds(j * 6, 6)],
                                         T(AC)[:, ds(j * BLK, BLK)]))
                ch.leave(NBLK, 1)
                ch.wait()
                bn_finish(n, "bn_g", "bn_b")

            walk(dve, setup=setup, rank=rank, scatter_d=scatter_d, load_meta=load_meta,
                 edges=edges, linear=linear, norm_apply=norm_apply, norm_linear=norm_linear, norm_out=norm_out,
                 linear_nat=linear_nat, layer_norm=layer_norm, add=add_, copy=copy, attend=attend, conv=conv,
                 q_tiles=q_tiles)


def kernel(**inputs):
    import concourse.bacc as bacc
    from concourse.bass_utils import run_bass_kernel_spmd

    g = {k: np.asarray(v) for k, v in inputs.items()}

    def columns(w):
        return np.concatenate(list(w), axis=1)

    def padded(a, fill):
        full = np.full(E_PAD, fill, a.dtype)
        full[:E] = a
        return np.ascontiguousarray(full.reshape(COLS, P).T)

    def rows_padded(a):
        full = np.zeros((E_PAD, a.shape[1]), a.dtype)
        full[:E] = a
        return full

    l0, l1, l2, l3 = ({k[len(p):]: v for k, v in g.items() if k.startswith(p)}
                      for p in ("L0_gnn_", "L1_gnn_", "L2_gnn_", "L3_gnn_"))
    src, dst = g["src"], g["dst"]
    if src.dtype != np.int32:
        src, dst = src.astype(np.int32), dst.astype(np.int32)
    attr16 = np.zeros((A16 + 1, E_PAD), np.float32)
    attr16[:A16, :E] = g["edge_attr_16"].T
    attr16[A16] = 1.0
    arrays = {
        "x": np.ascontiguousarray(g["x"]),
        "x_t": np.ascontiguousarray(g["x"].T),
        "dst_key": padded(dst, TILES * P), "src_key": padded(src, TILES * P),
        "src_val": padded(src, 0), "dst_val": padded(dst, 0),
        "attr128_t": np.ascontiguousarray(rows_padded(g["edge_attr_128"]).T),
        "attr16_t": attr16,
        "attr64": rows_padded(g["edge_attr_64"]),
        "weights": np.concatenate([
            columns(l0["W1"]), columns(l0["W2"]), columns(l2["W1"]), columns(l2["W2"]), l0["fp_W1"],
            l0["fp_W2"][:D], l0["fp_W2"][D:], l1["W_S_w"].T, l1["W_T_w"].T, l3["WE"], l3["WK"], l3["WV"],
            l3["WQ"]], axis=1),
        "rows": np.concatenate([np.ravel(a) for a in (
            l0["ln_g"], l0["ln_b"], l0["fp_b1"], l0["fp_ln1_g"], l0["fp_ln1_b"], l0["fp_b2"], l0["fp_ln2_g"],
            l0["fp_ln2_b"], l2["b2"], l2["gamma"], l2["beta"], l0["eps"])]),
        "feats": np.ascontiguousarray(np.concatenate([
            l0["b1"], l0["bn1_g"], l0["bn1_b"], l0["b2"], l0["bn2_g"], l0["bn2_b"], l0["obn_g"], l0["obn_b"],
            l2["b1"], l1["W_S_b"][None], l3["bn_gamma"][None], l3["bn_beta"][None]]).T),
        "attr_w": np.concatenate([l1["T_w"].T, l1["T_b"][None], l1["W_T_b"][None]]),
        "ea_w": np.concatenate([l2["We"], l2["be"][None]]),
    }
    nc = bacc.Bacc("TRN2", target_bir_lowering=False, num_devices=1)
    A = {k: nc.dram_tensor(f"in_{k}", v.shape, mybir.dt.from_np(v.dtype), kind="ExternalInput").ap()
         for k, v in arrays.items()}
    A["out"] = nc.dram_tensor("out", (N, D), F32, kind="ExternalOutput").ap()
    program(nc, A)
    r = run_bass_kernel_spmd(nc, [{f"in_{k}": np.ascontiguousarray(v) for k, v in arrays.items()}], core_ids=[0])
    return r.results[0]["out"]
```
